# Optimizing a Trainium2 kernel written in Bass

```python
import numpy as np
import jax
import jax.numpy as jnp

def _softmax(x, axis=-1):
    return jax.nn.softmax(x, axis=axis)

def _gelu(x):
    return jax.nn.gelu(x, approximate=True)

def _silu(x):
    return jax.nn.silu(x)

def _sigmoid(x):
    return jax.nn.sigmoid(x)

def _layernorm(x, axis=-1, eps=1e-05):
    m = jnp.mean(x, axis=axis, keepdims=True)
    v = jnp.var(x, axis=axis, keepdims=True)
    return (x - m) / jnp.sqrt(v + eps)

def _scatter_add(tgt, idx, src, axis=0):
    return tgt.at[idx].add(src)

def _segment_sum(src, seg, n):
    return jax.ops.segment_sum(src, seg, n)
kernel_name = 'mk_xattn_ffn_d4_seqx_r8_fae534'

def setup_inputs(seed: int=0):
    np.random.seed(seed)
    _w = jnp.asarray

    def _rec_inputs():
        import jax
        import jax.numpy as jnp
        _rk = jax.random.key(seed)
        x = -0.0003929 + 0.9999 * jax.random.normal(jax.random.fold_in(_rk, 1), (128, 64, 128), jnp.float32)
        _lenS = 64 - jax.random.randint(jax.random.fold_in(_rk, 7), (128,), 0, max(1, 64 // 4) + 1, jnp.int32)
        _lenS2 = 64 - jax.random.randint(jax.random.fold_in(_rk, 8), (128,), 0, max(1, 64 // 4) + 1, jnp.int32)
        _ctx_1024P = jax.random.normal(jax.random.fold_in(_rk, 11), (128, 16, 128), jnp.float32)
        _ctx_1024c = jax.random.dirichlet(jax.random.fold_in(_rk, 511), 0.3 * jnp.ones((16,), jnp.float32), (128, 64))
        _ctx_1024t = jnp.einsum('bsk,bkd->bsd', _ctx_1024c, _ctx_1024P)
        _ctx_1024t = _ctx_1024t * jax.lax.rsqrt(jnp.mean(jnp.square(_ctx_1024t)) + 1e-12) * 0.953939
        ctx_1024 = 2.81802e-05 + 1.00001 * (_ctx_1024t + 0.3 * jax.random.normal(jax.random.fold_in(_rk, 611), (128, 64, 128), jnp.float32))
        _validS = jnp.arange(64)[None, :] < _lenS[:, None]
        _validS2 = jnp.arange(64)[None, :] < _lenS2[:, None]
        _causal = jnp.tril(jnp.ones((64, 64), dtype=bool))
        mask_BxS2_bf1 = jnp.ones((128, 64), dtype=bool)
        return (x, ctx_1024, mask_BxS2_bf1)
    x, ctx_1024, mask_BxS2_bf1 = _rec_inputs()

    def _L0_xattn_setup():
        import jax, jax.numpy as jnp
        import numpy as np
        B, N, D_MODEL, H, W = (4, 512, 128, 16, 32)
        D_K = D_MODEL // H

        def _look_around(x, pad_value):
            pad_width = [(0, 0), (1, 0), (0, 0)] + [(0, 0)] * (x.ndim - 3)
            padded = jnp.pad(x, pad_width, constant_values=pad_value)
            return jnp.concatenate([padded[:, :-1], padded[:, 1:]], axis=2)

        def _local_attention(q, k, v, mask):
            b, h, n, d = q.shape
            nw = n // W
            scale = d ** (-0.5)
            bq = (q * scale).reshape(b * h, nw, W, d)
            bk = _look_around(k.reshape(b * h, nw, W, d), 0.0)
            bv = _look_around(v.reshape(b * h, nw, W, d), 0.0)
            pos = jnp.arange(n).reshape(1, nw, W)
            bq_t = pos
            bq_k = _look_around(pos, -1)
            causal = bq_t[..., :, None] >= bq_k[..., None, :]
            valid = (bq_k != -1)[..., None, :]
            kmask = _look_around(mask.reshape(b, nw, W), False)
            kmask = jnp.repeat(kmask, h, axis=0)[:, :, None, :]
            full_mask = causal & valid & kmask
            sim = jnp.einsum('bnid,bnjd->bnij', bq, bk)
            sim = jnp.where(full_mask, sim, jnp.finfo(sim.dtype).min)
            attn = jax.nn.softmax(sim, axis=-1)
            out = jnp.einsum('bnij,bnjd->bnid', attn, bv)
            return out.reshape(b, h, n, d)
        key = jax.random.key(seed)
        ks = jax.random.split(key, 12)
        mk = lambda k, shape: jax.random.normal(k, shape, dtype=jnp.float32)
        inp = {'query': mk(ks[0], (B, N, D_MODEL)), 'key': mk(ks[1], (B, N, D_MODEL)), 'value': mk(ks[2], (B, N, D_MODEL)), 'mask': jnp.ones((B, N), dtype=bool)}
        scale = 0.02
        for i, nm in enumerate(['q', 'k', 'v', 'o']):
            inp[f'W_{nm}'] = mk(ks[3 + 2 * i], (D_MODEL, D_MODEL)) * scale
            inp[f'b_{nm}'] = jnp.zeros((D_MODEL,), dtype=jnp.float32)
        return inp
    _L0_xattn_all = _L0_xattn_setup()
    _L0_xattn_in = {k: v for k, v in _L0_xattn_all.items() if k in ('W_q', 'b_q', 'W_k', 'b_k', 'W_v', 'b_v', 'W_o', 'b_o')}
    del _L0_xattn_all

    def _L0_ffn_setup():
        import jax, jax.numpy as jnp
        import numpy as np
        H = 128
        I = 256
        E = 8
        B, S = (2, 512)
        EPS = 1e-05
        INIT = 0.02

        def _layernorm(x, w, b):
            mu = jnp.mean(x, axis=-1, keepdims=True)
            var = jnp.mean(jnp.square(x - mu), axis=-1, keepdims=True)
            return (x - mu) * jax.lax.rsqrt(var + EPS) * w + b
        key = jax.random.key(seed)
        ks = jax.random.split(key, 9)
        return {'hidden_states': jax.random.normal(ks[0], (B, S, H), jnp.float32), 'ln_w': jnp.ones((H,), jnp.float32), 'ln_b': jnp.zeros((H,), jnp.float32), 'router_w': jax.random.normal(ks[1], (H, E), jnp.float32) * INIT, 'gate_w': jax.random.normal(ks[2], (E, H, I), jnp.float32) * INIT, 'up_w': jax.random.normal(ks[3], (E, H, I), jnp.float32) * INIT, 'down_w': jax.random.normal(ks[4], (E, I, H), jnp.float32) * INIT, 'sh_gate': jax.random.normal(ks[5], (H, I), jnp.float32) * INIT, 'sh_up': jax.random.normal(ks[6], (H, I), jnp.float32) * INIT, 'sh_down': jax.random.normal(ks[7], (I, H), jnp.float32) * INIT}
    _L0_ffn_all = _L0_ffn_setup()
    _L0_ffn_in = {k: v for k, v in _L0_ffn_all.items() if k in ('ln_w', 'ln_b', 'router_w', 'gate_w', 'up_w', 'down_w', 'sh_gate', 'sh_up', 'sh_down')}
    del _L0_ffn_all

    def _L1_xattn_setup():
        import jax, jax.numpy as jnp
        import numpy as np
        DIM = 128
        NUM_HEADS = 16
        HEAD_DIM = DIM // NUM_HEADS
        key = jax.random.key(seed)
        ks = jax.random.split(key, 8)
        B, N, N2 = (2, 256, 256)
        s = 1.0 / np.sqrt(DIM)
        return {'x': jax.random.normal(ks[0], (B, N, DIM), jnp.float32), 'y': jax.random.normal(ks[1], (B, N2, DIM), jnp.float32), 'Wq': jax.random.normal(ks[2], (DIM, DIM), jnp.float32) * s, 'bq': jnp.zeros((DIM,), jnp.float32), 'Wkv': jax.random.normal(ks[3], (DIM, 2 * DIM), jnp.float32) * s, 'bkv': jnp.zeros((2 * DIM,), jnp.float32), 'Wo': jax.random.normal(ks[4], (DIM, DIM), jnp.float32) * s, 'bo': jnp.zeros((DIM,), jnp.float32)}
    _L1_xattn_all = _L1_xattn_setup()
    _L1_xattn_in = {k: v for k, v in _L1_xattn_all.items() if k in ('Wq', 'bq', 'Wkv', 'bkv', 'Wo', 'bo')}
    del _L1_xattn_all

    def _L1_ffn_setup():
        import jax, jax.numpy as jnp
        import numpy as np
        QMIN, QMAX = (-128.0, 127.0)

        def _affine_quantize(x):
            amin, amax = (jnp.min(x), jnp.max(x))
            scale = jnp.maximum((amax - amin) / 255.0, 1e-08)
            zp = jnp.clip(jnp.round(-amin / scale) + QMIN, QMIN, QMAX)
            q = jnp.clip(jnp.round(x / scale) + zp, QMIN, QMAX)
            return (q, scale, zp)

        def _sym_quantize(w):
            scale = jnp.maximum(jnp.max(jnp.abs(w)) / 127.0, 1e-08)
            q = jnp.clip(jnp.round(w / scale), -127.0, 127.0)
            return (q, scale)

        def _qlinear(x, W, b):
            xq, sx, zx = _affine_quantize(x)
            wq, sw = _sym_quantize(W)
            acc = jnp.einsum('bsh,oh->bso', xq - zx, wq)
            return acc * (sx * sw) + b
        key = jax.random.key(seed)
        k1, k2, k3, k4, k5 = jax.random.split(key, 5)
        d, h = (128, 512)
        x = jax.random.normal(k1, (4, 512, d), dtype=jnp.float32)
        W1 = jax.random.normal(k2, (h, d), dtype=jnp.float32) * (1.0 / np.sqrt(d))
        b1 = jax.random.normal(k3, (h,), dtype=jnp.float32) * 0.02
        W2 = jax.random.normal(k4, (d, h), dtype=jnp.float32) * (1.0 / np.sqrt(h))
        b2 = jax.random.normal(k5, (d,), dtype=jnp.float32) * 0.02
        return {'x': x, 'W1': W1, 'b1': b1, 'W2': W2, 'b2': b2}
    _L1_ffn_all = _L1_ffn_setup()
    _L1_ffn_in = {k: v for k, v in _L1_ffn_all.items() if k in ('W1', 'b1', 'W2', 'b2')}
    del _L1_ffn_all

    def _L2_xattn_setup():
        import jax, jax.numpy as jnp
        import numpy as np
        R = 3.9
        STRENGTH = 0.1
        N_ITER = 10
        I0 = 1.0
        OMEGA = 1.0
        KWAVE = 2.0
        ALPHA_BASE = 1.0
        LC = 0.5
        DE = 2.0
        CHIRP_N = 1
        AMIN = 0.1
        AMAX = 3.0
        FD = 1.5
        T = 0.0
        ATT_ALPHA = 1.5
        EPS = 1e-10
        FCI = 0.7
        STAB = 0.8
        DEMAND = 0.6
        BASE = 0.5
        SENS = 1.0
        DECAY = 0.1
        B, S, D4 = (4, 256, 128)

        def hamilton(a, b):
            aw, ax, ay, az = jnp.split(a, 4, axis=-1)
            bw, bx, by, bz = jnp.split(b, 4, axis=-1)
            w = aw * bw - ax * bx - ay * by - az * bz
            x = aw * bx + ax * bw + ay * bz - az * by
            y = aw * by - ax * bz + ay * bw + az * bx
            z = aw * bz + ax * by - ay * bx + az * bw
            return jnp.concatenate([w, x, y, z], axis=-1)
        key = jax.random.key(seed)
        ks = jax.random.split(key, 8)
        sc = 0.02
        return {'query': jax.random.normal(ks[0], (B, S, D4), jnp.float32), 'memory': jax.random.normal(ks[1], (B, S, D4), jnp.float32), 'Wq': jax.random.normal(ks[2], (D4, D4), jnp.float32) * sc, 'bq': jnp.zeros((D4,), jnp.float32), 'Wk': jax.random.normal(ks[3], (D4, D4), jnp.float32) * sc, 'bk': jnp.zeros((D4,), jnp.float32), 'Wv': jax.random.normal(ks[4], (D4, D4), jnp.float32) * sc, 'bv': jnp.zeros((D4,), jnp.float32)}
    _L2_xattn_all = _L2_xattn_setup()
    _L2_xattn_in = {k: v for k, v in _L2_xattn_all.items() if k in ('Wq', 'bq', 'Wk', 'bk', 'Wv', 'bv')}
    del _L2_xattn_all

    def _L2_ffn_setup():
        import jax, jax.numpy as jnp
        import numpy as np
        INT8_MAX = 127.0

        def _absmax_scale(x, axes):
            amax = jnp.max(jnp.abs(x), axis=axes, keepdims=True)
            return jnp.maximum(amax, 1e-12) / INT8_MAX
        key = jax.random.key(seed)
        k1, k2 = jax.random.split(key)
        lhs = jax.random.normal(k1, (4, 1024, 128), dtype=jnp.float32)
        rhs = jax.random.normal(k2, (128, 128), dtype=jnp.float32)
        return {'lhs': lhs, 'rhs': rhs}
    _L2_ffn_all = _L2_ffn_setup()
    _L2_ffn_in = {k: v for k, v in _L2_ffn_all.items() if k in ('rhs',)}
    del _L2_ffn_all

    def _L3_xattn_setup():
        import jax, jax.numpy as jnp
        import numpy as np
        B, SQ, SK, D, H = (4, 256, 256, 128, 16)
        HD = D // H
        key = jax.random.key(seed)
        ks = jax.random.split(key, 8)
        s = 1.0 / np.sqrt(D)
        return {'query': jax.random.normal(ks[0], (B, SQ, D), jnp.float32), 'key_value': jax.random.normal(ks[1], (B, SK, D), jnp.float32), 'Wq': jax.random.normal(ks[2], (D, D), jnp.float32) * s, 'bq': jnp.zeros((D,), jnp.float32), 'Wkv': jax.random.normal(ks[3], (D, 2 * D), jnp.float32) * s, 'bkv': jnp.zeros((2 * D,), jnp.float32), 'Wo': jax.random.normal(ks[4], (D, D), jnp.float32) * s, 'bo': jnp.zeros((D,), jnp.float32)}
    _L3_xattn_all = _L3_xattn_setup()
    _L3_xattn_in = {k: v for k, v in _L3_xattn_all.items() if k in ('Wq', 'bq', 'Wkv', 'bkv', 'Wo', 'bo')}
    del _L3_xattn_all

    def _L3_ffn_setup():
        import jax, jax.numpy as jnp
        import numpy as np
        DIM = 128
        HIDDEN = 384
        SCALE = 1.0 / 127.0

        def _dequant(w_int, dtype):
            return w_int.astype(dtype) * jnp.asarray(SCALE, dtype)
        key = jax.random.key(seed)
        k_x, k_g, k_u, k_d = jax.random.split(key, 4)
        x = jax.random.normal(k_x, (4, 256, DIM), dtype=jnp.float32)
        w_gate = jax.random.randint(k_g, (HIDDEN, DIM), -127, 128, dtype=jnp.int32)
        w_up = jax.random.randint(k_u, (HIDDEN, DIM), -127, 128, dtype=jnp.int32)
        w_down = jax.random.randint(k_d, (DIM, HIDDEN), -127, 128, dtype=jnp.int32)
        return {'x': x, 'w_gate': w_gate, 'w_up': w_up, 'w_down': w_down}
    _L3_ffn_all = _L3_ffn_setup()
    _L3_ffn_in = {k: v for k, v in _L3_ffn_all.items() if k in ('w_gate', 'w_up', 'w_down')}
    del _L3_ffn_all
    return {'x': x, 'ctx_1024': ctx_1024, 'mask_BxS2_bf1': mask_BxS2_bf1, 'L0_xattn_W_q': _L0_xattn_in['W_q'], 'L0_xattn_b_q': _L0_xattn_in['b_q'], 'L0_xattn_W_k': _L0_xattn_in['W_k'], 'L0_xattn_b_k': _L0_xattn_in['b_k'], 'L0_xattn_W_v': _L0_xattn_in['W_v'], 'L0_xattn_b_v': _L0_xattn_in['b_v'], 'L0_xattn_W_o': _L0_xattn_in['W_o'], 'L0_xattn_b_o': _L0_xattn_in['b_o'], 'L0_ffn_ln_w': _L0_ffn_in['ln_w'], 'L0_ffn_ln_b': _L0_ffn_in['ln_b'], 'L0_ffn_router_w': _L0_ffn_in['router_w'], 'L0_ffn_gate_w': _L0_ffn_in['gate_w'], 'L0_ffn_up_w': _L0_ffn_in['up_w'], 'L0_ffn_down_w': _L0_ffn_in['down_w'], 'L0_ffn_sh_gate': _L0_ffn_in['sh_gate'], 'L0_ffn_sh_up': _L0_ffn_in['sh_up'], 'L0_ffn_sh_down': _L0_ffn_in['sh_down'], 'L1_xattn_Wq': _L1_xattn_in['Wq'], 'L1_xattn_bq': _L1_xattn_in['bq'], 'L1_xattn_Wkv': _L1_xattn_in['Wkv'], 'L1_xattn_bkv': _L1_xattn_in['bkv'], 'L1_xattn_Wo': _L1_xattn_in['Wo'], 'L1_xattn_bo': _L1_xattn_in['bo'], 'L1_ffn_W1': _L1_ffn_in['W1'], 'L1_ffn_b1': _L1_ffn_in['b1'], 'L1_ffn_W2': _L1_ffn_in['W2'], 'L1_ffn_b2': _L1_ffn_in['b2'], 'L2_xattn_Wq': _L2_xattn_in['Wq'], 'L2_xattn_bq': _L2_xattn_in['bq'], 'L2_xattn_Wk': _L2_xattn_in['Wk'], 'L2_xattn_bk': _L2_xattn_in['bk'], 'L2_xattn_Wv': _L2_xattn_in['Wv'], 'L2_xattn_bv': _L2_xattn_in['bv'], 'L2_ffn_rhs': _L2_ffn_in['rhs'], 'L3_xattn_Wq': _L3_xattn_in['Wq'], 'L3_xattn_bq': _L3_xattn_in['bq'], 'L3_xattn_Wkv': _L3_xattn_in['Wkv'], 'L3_xattn_bkv': _L3_xattn_in['bkv'], 'L3_xattn_Wo': _L3_xattn_in['Wo'], 'L3_xattn_bo': _L3_xattn_in['bo'], 'L3_ffn_w_gate': _L3_ffn_in['w_gate'], 'L3_ffn_w_up': _L3_ffn_in['w_up'], 'L3_ffn_w_down': _L3_ffn_in['w_down']}

def reference(x, ctx_1024, mask_BxS2_bf1, L0_xattn_W_q, L0_xattn_b_q, L0_xattn_W_k, L0_xattn_b_k, L0_xattn_W_v, L0_xattn_b_v, L0_xattn_W_o, L0_xattn_b_o, L0_ffn_ln_w, L0_ffn_ln_b, L0_ffn_router_w, L0_ffn_gate_w, L0_ffn_up_w, L0_ffn_down_w, L0_ffn_sh_gate, L0_ffn_sh_up, L0_ffn_sh_down, L1_xattn_Wq, L1_xattn_bq, L1_xattn_Wkv, L1_xattn_bkv, L1_xattn_Wo, L1_xattn_bo, L1_ffn_W1, L1_ffn_b1, L1_ffn_W2, L1_ffn_b2, L2_xattn_Wq, L2_xattn_bq, L2_xattn_Wk, L2_xattn_bk, L2_xattn_Wv, L2_xattn_bv, L2_ffn_rhs, L3_xattn_Wq, L3_xattn_bq, L3_xattn_Wkv, L3_xattn_bkv, L3_xattn_Wo, L3_xattn_bo, L3_ffn_w_gate, L3_ffn_w_up, L3_ffn_w_down):
    import jax
    import jax.numpy as jnp

    def _L0_xattn_ref(query, key, value, mask, W_q, b_q, W_k, b_k, W_v, b_v, W_o, b_o):
        import jax, jax.numpy as jnp
        import numpy as np
        B, N, D_MODEL, H, W = (4, 512, 128, 16, 32)
        D_K = D_MODEL // H

        def _look_around(x, pad_value):
            pad_width = [(0, 0), (1, 0), (0, 0)] + [(0, 0)] * (x.ndim - 3)
            padded = jnp.pad(x, pad_width, constant_values=pad_value)
            return jnp.concatenate([padded[:, :-1], padded[:, 1:]], axis=2)

        def _local_attention(q, k, v, mask):
            b, h, n, d = q.shape
            nw = n // W
            scale = d ** (-0.5)
            bq = (q * scale).reshape(b * h, nw, W, d)
            bk = _look_around(k.reshape(b * h, nw, W, d), 0.0)
            bv = _look_around(v.reshape(b * h, nw, W, d), 0.0)
            pos = jnp.arange(n).reshape(1, nw, W)
            bq_t = pos
            bq_k = _look_around(pos, -1)
            causal = bq_t[..., :, None] >= bq_k[..., None, :]
            valid = (bq_k != -1)[..., None, :]
            kmask = _look_around(mask.reshape(b, nw, W), False)
            kmask = jnp.repeat(kmask, h, axis=0)[:, :, None, :]
            full_mask = causal & valid & kmask
            sim = jnp.einsum('bnid,bnjd->bnij', bq, bk)
            sim = jnp.where(full_mask, sim, jnp.finfo(sim.dtype).min)
            attn = jax.nn.softmax(sim, axis=-1)
            out = jnp.einsum('bnij,bnjd->bnid', attn, bv)
            return out.reshape(b, h, n, d)
        b, n, _ = query.shape

        def proj(x, Wm, bias):
            return (x @ Wm.T + bias).reshape(b, n, H, D_K).transpose(0, 2, 1, 3)
        q = proj(query, W_q, b_q)
        k = proj(key, W_k, b_k)
        v = proj(value, W_v, b_v)
        x = _local_attention(q, k, v, mask)
        x = x.transpose(0, 2, 1, 3).reshape(b, n, H * D_K)
        return x @ W_o.T + b_o

    def _L0_ffn_ref(hidden_states, ln_w, ln_b, router_w, gate_w, up_w, down_w, sh_gate, sh_up, sh_down):
        import jax, jax.numpy as jnp
        import numpy as np
        H = 128
        I = 256
        E = 8
        B, S = (2, 512)
        EPS = 1e-05
        INIT = 0.02

        def _layernorm(x, w, b):
            mu = jnp.mean(x, axis=-1, keepdims=True)
            var = jnp.mean(jnp.square(x - mu), axis=-1, keepdims=True)
            return (x - mu) * jax.lax.rsqrt(var + EPS) * w + b
        b, s, h = hidden_states.shape
        normed = _layernorm(hidden_states, ln_w, ln_b)
        xf = normed.reshape(-1, h)
        logits = xf @ router_w
        top_idx = jnp.argmax(logits, axis=-1)
        top_score = jax.nn.sigmoid(jnp.max(logits, axis=-1))

        def body(acc, ew):
            g, u, d, e = ew
            w = jnp.where(top_idx == e, top_score, 0.0)[:, None]
            xe = xf * w
            hmid = jax.nn.silu(xe @ g) * (xe @ u)
            return (acc + hmid @ d, None)
        routed, _ = jax.lax.scan(body, jnp.zeros_like(xf), (gate_w, up_w, down_w, jnp.arange(E)))
        shared = jax.nn.silu(xf @ sh_gate) * (xf @ sh_up) @ sh_down
        moe_out = (routed + shared).reshape(b, s, h)
        return hidden_states + moe_out

    def _L1_xattn_ref(x, y, Wq, bq, Wkv, bkv, Wo, bo):
        import jax, jax.numpy as jnp
        import numpy as np
        DIM = 128
        NUM_HEADS = 16
        HEAD_DIM = DIM // NUM_HEADS
        B, N, C = x.shape
        B2, N2, _ = y.shape
        H, hd = (NUM_HEADS, HEAD_DIM)
        scaling = hd ** (-0.5)
        q = (x @ Wq + bq).reshape(B, N, H, hd).transpose(0, 2, 1, 3)
        kv = (y @ Wkv + bkv).reshape(B2, N2, 2, H, hd).transpose(0, 3, 2, 1, 4)
        k, v = (kv[:, :, 0], kv[:, :, 1])
        attn = jnp.einsum('bhnd,bhmd->bhnm', q * scaling, k)
        attn = jax.nn.softmax(attn, axis=-1)
        out = jnp.einsum('bhnm,bhmd->bhnd', attn, v)
        out = out.transpose(0, 2, 1, 3).reshape(B, N, C)
        return out @ Wo + bo

    def _L1_ffn_ref(x, W1, b1, W2, b2):
        import jax, jax.numpy as jnp
        import numpy as np
        QMIN, QMAX = (-128.0, 127.0)

        def _affine_quantize(x):
            amin, amax = (jnp.min(x), jnp.max(x))
            scale = jnp.maximum((amax - amin) / 255.0, 1e-08)
            zp = jnp.clip(jnp.round(-amin / scale) + QMIN, QMIN, QMAX)
            q = jnp.clip(jnp.round(x / scale) + zp, QMIN, QMAX)
            return (q, scale, zp)

        def _sym_quantize(w):
            scale = jnp.maximum(jnp.max(jnp.abs(w)) / 127.0, 1e-08)
            q = jnp.clip(jnp.round(w / scale), -127.0, 127.0)
            return (q, scale)

        def _qlinear(x, W, b):
            xq, sx, zx = _affine_quantize(x)
            wq, sw = _sym_quantize(W)
            acc = jnp.einsum('bsh,oh->bso', xq - zx, wq)
            return acc * (sx * sw) + b
        h = _qlinear(x, W1, b1)
        h = jax.nn.gelu(h, approximate=False)
        out = _qlinear(h, W2, b2)
        return out

    def _L2_xattn_ref(query, memory, Wq, bq, Wk, bk, Wv, bv):
        import jax, jax.numpy as jnp
        import numpy as np
        R = 3.9
        STRENGTH = 0.1
        N_ITER = 10
        I0 = 1.0
        OMEGA = 1.0
        KWAVE = 2.0
        ALPHA_BASE = 1.0
        LC = 0.5
        DE = 2.0
        CHIRP_N = 1
        AMIN = 0.1
        AMAX = 3.0
        FD = 1.5
        T = 0.0
        ATT_ALPHA = 1.5
        EPS = 1e-10
        FCI = 0.7
        STAB = 0.8
        DEMAND = 0.6
        BASE = 0.5
        SENS = 1.0
        DECAY = 0.1
        B, S, D4 = (4, 256, 128)

        def hamilton(a, b):
            aw, ax, ay, az = jnp.split(a, 4, axis=-1)
            bw, bx, by, bz = jnp.split(b, 4, axis=-1)
            w = aw * bw - ax * bx - ay * by - az * bz
            x = aw * bx + ax * bw + ay * bz - az * by
            y = aw * by - ax * bz + ay * bw + az * bx
            z = aw * bz + ax * by - ay * bx + az * bw
            return jnp.concatenate([w, x, y, z], axis=-1)
        s = jax.nn.sigmoid(jnp.linalg.norm(query, axis=-1))
        for _ in range(N_ITER):
            s = R * s * (1.0 - s)
        q = query * (1.0 + STRENGTH * (s[..., None] - 0.5))
        seq = q.shape[1]
        alpha = float(np.clip(ALPHA_BASE * (1.0 + LC * (FD - DE) / DE), AMIN, AMAX))
        beta = 2 * CHIRP_N + 1 - 2 * FD
        lam = jnp.arange(seq, dtype=q.dtype) / seq
        wave = I0 * jnp.sin(OMEGA * T + alpha * lam) * jnp.cos(OMEGA * T - KWAVE * lam + beta * lam ** 2)
        q = q * (1.0 + 0.1 * wave[None, :, None])
        dop = (1 - DECAY) * BASE + DECAY * jax.nn.sigmoid(jnp.float32(FCI * SENS))
        ser = (1 - DECAY) * BASE + DECAY * jax.nn.sigmoid(jnp.float32(STAB * SENS))
        nor = (1 - DECAY) * BASE + DECAY * jax.nn.sigmoid(jnp.float32(DEMAND * SENS))
        mem = memory * (0.4 * dop + 0.3 * ser + 0.3 * nor)
        Q = q @ Wq.T + bq
        K = mem @ Wk.T + bk
        V = mem @ Wv.T + bv
        Qf = jnp.fft.fft(Q, axis=-2)
        Kf = jnp.fft.fft(K, axis=-2)
        Vf = jnp.fft.fft(V, axis=-2)
        kidx = jnp.arange(seq, dtype=jnp.float32)
        filt = jnp.exp(1j * ATT_ALPHA * jnp.arctan(jnp.log(kidx + EPS)))[None, :, None]
        QK = hamilton(Qf * filt, Kf * filt)
        QKV = hamilton(QK, Vf * filt)
        attended = jnp.fft.ifft(QKV, axis=-2).real.astype(query.dtype)
        return attended

    def _L2_ffn_ref(lhs, rhs):
        import jax, jax.numpy as jnp
        import numpy as np
        INT8_MAX = 127.0

        def _absmax_scale(x, axes):
            amax = jnp.max(jnp.abs(x), axis=axes, keepdims=True)
            return jnp.maximum(amax, 1e-12) / INT8_MAX
        lhs_scale = _absmax_scale(lhs, (2,))
        rhs_scale = _absmax_scale(rhs, (0,))
        q_lhs = jnp.clip(jnp.round(lhs / lhs_scale), -INT8_MAX, INT8_MAX).astype(jnp.int8)
        q_rhs = jnp.clip(jnp.round(rhs / rhs_scale), -INT8_MAX, INT8_MAX).astype(jnp.int8)
        acc = jax.lax.dot_general(q_lhs, q_rhs, (((2,), (0,)), ((), ())), preferred_element_type=jnp.int32)
        return acc.astype(jnp.float32) * lhs_scale * rhs_scale

    def _L3_xattn_ref(query, key_value, Wq, bq, Wkv, bkv, Wo, bo):
        import jax, jax.numpy as jnp
        import numpy as np
        B, SQ, SK, D, H = (4, 256, 256, 128, 16)
        HD = D // H
        b, sq, _ = query.shape
        sk = key_value.shape[1]
        Q = (query @ Wq + bq).reshape(b, sq, H, HD).transpose(0, 2, 1, 3)
        KV = (key_value @ Wkv + bkv).reshape(b, sk, 2, H, HD)
        K = KV[:, :, 0].transpose(0, 2, 1, 3)
        V = KV[:, :, 1].transpose(0, 2, 1, 3)
        scale = 1.0 / np.sqrt(HD).astype(np.float32)
        scores = jnp.einsum('bhqd,bhkd->bhqk', Q, K) * scale
        attn = jax.nn.softmax(scores, axis=-1)
        out = jnp.einsum('bhqk,bhkd->bhqd', attn, V)
        out = out.transpose(0, 2, 1, 3).reshape(b, sq, D)
        return out @ Wo + bo

    def _L3_ffn_ref(x, w_gate, w_up, w_down):
        import jax, jax.numpy as jnp
        import numpy as np
        DIM = 128
        HIDDEN = 384
        SCALE = 1.0 / 127.0

        def _dequant(w_int, dtype):
            return w_int.astype(dtype) * jnp.asarray(SCALE, dtype)
        wg = _dequant(w_gate, x.dtype)
        wu = _dequant(w_up, x.dtype)
        wd = _dequant(w_down, x.dtype)
        gate = jnp.einsum('bsd,hd->bsh', x, wg)
        up = jnp.einsum('bsd,hd->bsh', x, wu)
        h = jax.nn.silu(gate) * up
        return jnp.einsum('bsh,dh->bsd', h, wd)
    x = x + _L0_xattn_ref(_layernorm(x, axis=-1), ctx_1024, ctx_1024, mask_BxS2_bf1, L0_xattn_W_q, L0_xattn_b_q, L0_xattn_W_k, L0_xattn_b_k, L0_xattn_W_v, L0_xattn_b_v, L0_xattn_W_o, L0_xattn_b_o)
    x = x + _L0_ffn_ref(_layernorm(x, axis=-1), L0_ffn_ln_w, L0_ffn_ln_b, L0_ffn_router_w, L0_ffn_gate_w, L0_ffn_up_w, L0_ffn_down_w, L0_ffn_sh_gate, L0_ffn_sh_up, L0_ffn_sh_down)
    x = x + _L1_xattn_ref(_layernorm(x, axis=-1), ctx_1024, L1_xattn_Wq, L1_xattn_bq, L1_xattn_Wkv, L1_xattn_bkv, L1_xattn_Wo, L1_xattn_bo)
    x = x + _L1_ffn_ref(_layernorm(x, axis=-1), L1_ffn_W1, L1_ffn_b1, L1_ffn_W2, L1_ffn_b2)
    x = x + _L2_xattn_ref(_layernorm(x, axis=-1), ctx_1024, L2_xattn_Wq, L2_xattn_bq, L2_xattn_Wk, L2_xattn_bk, L2_xattn_Wv, L2_xattn_bv)
    x = x + _L2_ffn_ref(_layernorm(x, axis=-1), L2_ffn_rhs)
    x = x + _L3_xattn_ref(_layernorm(x, axis=-1), ctx_1024, L3_xattn_Wq, L3_xattn_bq, L3_xattn_Wkv, L3_xattn_bkv, L3_xattn_Wo, L3_xattn_bo)
    x = x + _L3_ffn_ref(_layernorm(x, axis=-1), L3_ffn_w_gate, L3_ffn_w_up, L3_ffn_w_down)
    return x

_drawn_inputs = setup_inputs


def setup_inputs(seed=0):
    import zlib

    import numpy as np

    out = dict(_drawn_inputs(seed))
    spreads = {'L0_xattn_b_q': (0.0, 0.8),
     'L0_xattn_b_k': (0.0, 2.0),
     'L0_xattn_b_v': (0.0, 0.1),
     'L0_xattn_b_o': (0.0, 0.1),
     'L0_ffn_ln_w': (1.0, 0.6),
     'L0_ffn_ln_b': (0.0, 0.8),
     'L1_xattn_bq': (0.0, 2.0),
     'L1_xattn_bkv': (0.0, 0.682),
     'L1_xattn_bo': (0.0, 0.609),
     'L2_xattn_bq': (0.0, 0.1),
     'L2_xattn_bk': (0.0, 0.1),
     'L2_xattn_bv': (0.0, 0.1),
     'L3_xattn_bq': (0.0, 2.0),
     'L3_xattn_bkv': (0.0, 0.8),
     'L3_xattn_bo': (0.0, 0.8)}
    factors = {'L0_xattn_W_q': 8.0,
     'L0_xattn_W_k': 8.0,
     'L0_ffn_router_w': 8.0,
     'L0_ffn_gate_w': 8.0,
     'L0_ffn_up_w': 8.0,
     'L0_ffn_down_w': 8.0,
     'L0_ffn_sh_gate': 8.0,
     'L0_ffn_sh_up': 8.0,
     'L0_ffn_sh_down': 8.0,
     'L1_ffn_b1': 31.44,
     'L3_xattn_Wq': 4.549,
     'L1_xattn_Wq': 4.484,
     'L1_ffn_b2': 27.515}
    for name, (base, spread) in spreads.items():
        noise = np.random.default_rng([zlib.crc32(name.encode()), seed]).standard_normal(out[name].shape)
        drawn = base * np.exp(spread * noise) if base else spread * noise
        out[name] = jnp.asarray(drawn.astype(out[name].dtype))
    for name, factor in factors.items():
        out[name] = (out[name] * factor).astype(out[name].dtype)
    return out
```

```python
import math
from contextlib import ExitStack
import numpy as np
import concourse.bass as bass
from concourse import mybir

F32 = mybir.dt.float32
BF16 = mybir.dt.bfloat16
U8 = mybir.dt.uint8
ALU = mybir.AluOpType
ACT = mybir.ActivationFunctionType
AX = mybir.AxisListType

P = 128
TOKENS = 128 * 64
TILES = TOKENS // P
SEQ = 64
LANES = 2
ROUNDS = TILES // LANES
HEADS, HD = 16, 8
EPS = 1e-5
MASKED = 1e30
MAGIC = 1.5 * 2 ** 23
EXPERTS, FFN0, FFN1, FFN3 = 8, 256, 512, 384
GROUP = 4
FREQ = SEQ // 2 + 1
LOGISTIC, LOGISTIC_STEPS = 3.9, 10
STOP = 8


class Steps:

    def __init__(self, sem, base, names):
        self.sem, self.base, self.names = sem, base, names

    def at(self, i, name):
        return i * len(self.names) + (self.base + self.names.index(name) + 1)

    def end(self, rounds):
        return self.base + rounds * len(self.names)


def build_program(nc, dram, out):
    with ExitStack() as ctx:
        sb = lambda name, shape, dt=F32: ctx.enter_context(nc.sbuf_tensor(name, shape, dt))
        pb = lambda name, shape: ctx.enter_context(nc.psum_tensor(name, shape, F32))
        sem = lambda name: ctx.enter_context(nc.semaphore(name))

        x = sb("x", [P, TILES, P])
        stats = sb("stats", [P, TILES, 6])
        mean = sb("mean", [P, TILES])
        agg = sb("agg", [P, 4, TILES])
        rstd = sb("rstd", [P, TILES])
        vpe = sb("vpe", [P, TILES])
        minus_half = sb("minus_half", [P, TILES])
        half = sb("half", [P, TILES])
        ident = sb("ident", [P, P])

        head_mask = sb("head_mask", [P, 4])
        causal = sb("causal", [P, P])
        half_pad = sb("half_pad", [P, 1])

        area = sb("area", [P, TOKENS * FFN1 // P])
        where = [0]

        def part(width):
            where[0] += width
            return area[:, where[0] - width:where[0]]
        def attention_weights():
            return dict(wq=part(P), wk=part(P), wv=part(P), wo=part(2 * P).rearrange("p (j n) -> p j n", j=2),
                        bq=part(1), bk=part(1), bv=part(P))
        att = {0: attention_weights(), 1: attention_weights()}
        gate_up = part(EXPERTS * 2 * FFN0).rearrange("p (e n) -> p e n", e=EXPERTS)
        down0 = part(2 * EXPERTS * P).rearrange("p (c n) -> p c n", c=2)
        shared_gu = part(2 * FFN0)
        shared_dn = part(2 * P).rearrange("p (c n) -> p c n", c=2)
        router = part(EXPERTS)
        ln_w = part(P)
        ln_b = part(P)
        rank = part(EXPERTS)
        rstd2 = part(TILES)
        key_mask = part(TOKENS // 4).bitcast(U8)
        am = [part(P) for _ in range(LANES)]
        w_raw = part(2 * FFN1).rearrange("p (k n) -> p k n", k=2)
        w_rnd = part(FFN1)
        moe = []
        for l in range(LANES):
            moe.append(dict(nrm=part(P), nT=part(P), mx=part(1), eq=part(EXPERTS), pick=part(1), one=part(EXPERTS),
                            th=part(1), w=part(EXPERTS), silu=part(2 * FFN0), h=part(2 * FFN0),
                            hT=part(2 * FFN0), acc=part(P), red=part(P)))
        hidden = area[:].rearrange("p (g n) -> p g n", n=GROUP * FFN1)
        where[0] = 0
        att[3] = attention_weights()
        f_wq = part(P)
        f_wk = part(4 * P).rearrange("p (r n) -> p r n", r=4)
        f_wv = part(4 * P).rearrange("p (r n) -> p r n", r=4)
        f_bq = part(1)
        f_bk = part(4)
        f_bv = part(4)
        f_unit = part(8 * P).rearrange("p (s n) -> p s n", s=8)
        dft = part(P)
        idft = part(P)
        wave = part(1)
        dc_q = part(P)
        dc_kv = part(16).rearrange("p (v r b) -> p v r b", v=2, r=4)
        chaos = part(3 * TILES).rearrange("p (k t) -> p k t", k=3)
        norm = part(TILES)
        eneg = part(TILES)
        fac = part(TILES)
        fl = []
        for l in range(LANES):
            fl.append(dict(qh=part(P), p1=part(4 * P), p2=part(4 * 2 * (FREQ - 2)), p3=part(4 * 2 * (FREQ - 2)), qk=part(P), g=part(P), gT=part(P)))
        r_raw = part(P)
        r_t = part(P)
        r_scale = part(2)
        r_diag = part(P)
        r_bc = part(P)
        r_q = part(P // 2).bitcast(BF16)
        q8 = []
        for l in range(LANES):
            q8.append(dict(amax=part(GROUP), ls=part(GROUP), inv=part(GROUP), y=part(GROUP * P), yT=part(GROUP * P // 2).bitcast(BF16)))
        g_raw = part(3 * FFN3).bitcast(mybir.dt.int32)
        g_w = part(3 * FFN3)
        ff = []
        for l in range(LANES):
            ff.append(dict(xn=part(2 * P), xnT=part(2 * P), silu=part(2 * FFN3), hT=part(2 * FFN3)))

        w_q = sb("w_q", [P, 2, FFN1], BF16)
        b1 = sb("b1", [P, 4])
        b2 = sb("b2", [P, P])
        ones = sb("ones", [P, P])
        magic = sb("magic", [P, 1])
        scratch = sb("scratch", [P, 1])
        tmx = sb("tmx", [P, 2, TILES])
        gcol = sb("gcol", [P, 4])
        grow = sb("grow", [4, 1])
        gdiag = sb("gdiag", [4, 4])
        gall = sb("gall", [P, 4])
        qs = sb("qs", [P, 16])
        hmm = sb("hmm", [P, 2, TILES // GROUP])

        def lane(name, shape, dt=F32):
            return [sb(f"{name}{l}", shape, dt) for l in range(LANES)]
        xn = lane("xn", [P, P])
        cx = lane("cx", [P, P])
        xcT = lane("xcT", [P, 2, P])
        qx = lane("qx", [P, 2, 4, SEQ])
        kT = lane("kT", [P, P])
        vbd = lane("vbd", [P, HEADS, 2, 9])
        mx = lane("mx", [P, 16])
        prob = lane("prob", [P, 16, SEQ])
        probT = lane("probT", [P, 8, P])
        rc = lane("rc", [P, 8, 2])
        fx = lane("fx", [P, 16])
        o = lane("o", [P, 2, 8, 8])
        oT = lane("oT", [65, 2, 2, SEQ])
        xqT = [qx[l][:].rearrange("p b j q -> p (b j q)")[:, 0:256].bitcast(BF16) for l in range(LANES)]
        hq = [prob[l][:].rearrange("p g k -> p (g k)").bitcast(BF16) for l in range(LANES)]

        ps_s = [pb(f"ps_s{l}", [P, 1024]) for l in range(LANES)]
        ps_a = [pb(f"ps_a{l}", [P, 512]) for l in range(LANES)]
        ps_b = [pb(f"ps_b{l}", [P, 512]) for l in range(LANES)]

        loaded = {n: sem(f"loaded_{n}") for n in ("x", "const", "att0", "att1", "att3", "ffn0", "ffn1", "late")}
        ctx_in = [sem(f"ctx_in{l}") for l in range(LANES)]
        dve_sem = [sem(f"dve_done{l}") for l in range(LANES)]
        act_sem = [sem(f"act_done{l}") for l in range(LANES)]
        pe_sem = [sem(f"pe_done{l}") for l in range(LANES)]
        pool_sem = [sem(f"pool_done{l}") for l in range(LANES)]
        filled = sem("filled")
        x_stats = sem("x_stats")
        rstd_ready = sem("rstd_ready")
        vpe_ready = sem("vpe_ready")
        stored = sem("stored")

        x_tiles = dram["x"].rearrange("(t p) d -> p t d", p=P)
        ctx_tiles = dram["ctx_1024"].rearrange("(t p) d -> t p d", p=P)
        out_tiles = out.rearrange("(t p) d -> p t d", p=P)

        layers = {}
        base = dict(dve=0, act=0, pe=0, pool=0, ctx=0)

        def declare(key, rounds, dve=(), act=(), pe=(), pool=(), context=False):
            lay = dict(dve=[Steps(s, base["dve"], dve) for s in dve_sem], act=[Steps(s, base["act"], act) for s in act_sem],
                       pe=[Steps(s, base["pe"], pe) for s in pe_sem], pool=[Steps(s, base["pool"], pool) for s in pool_sem],
                       ctx=base["ctx"], rounds=rounds)
            for n, names in (("dve", dve), ("act", act), ("pe", pe), ("pool", pool)):
                base[n] += rounds * len(names)
            base["ctx"] += 16 * rounds if context else 0
            layers[key] = lay

        def attention_layer(L):
            declare(f"att{L}", ROUNDS, context=True,
                    dve=["xn", "qx", "v"] + (["am", "masked"] if L == 0 else []) + ["mx", "sub"]
                        + (["fx", "fs"] if L == 0 else []) + ["rc", "o", "fin", "st"],
                    act=["xcT", "kT", "exp", "probT", "oT"],
                    pe=["xcT", "proj", "s0", "s1", "s2", "s", "probT", "pv", "oT", "y"],
                    pool=["zero"] if L == 0 else [])
        QROUNDS = ROUNDS // GROUP
        attention_layer(0)
        declare("ffn0", ROUNDS, dve=["xn", "nrm", "nw", "nb", "mx", "eq", "pick", "one", "th", "w", "xw", "sh", "h", "acc", "sel", "red", "acc2", "fin", "st"],
                act=["nT", "tanh", "ssilu", "xwT", "silu", "hT"], pe=["nT", "lg", "sh", "xwT", "gu", "hT", "dn"])
        attention_layer(1)
        declare("ffn1a", QROUNDS, dve=["xs", "xn", "xr", "xc", "xT", "hmx", "hmn"], act=["g0", "g1", "g2", "g3"],
                pe=["xT", "m0", "m1", "m2", "m3"])
        declare("ffn1b", QROUNDS, dve=["hc", "hb", "yb", "fin", "st"], act=["hr"], pe=["y"])
        declare("freq", ROUNDS, context=True, dve=["xs", "q", "kb", "p3", "vb", "r3", "fin", "st"],
                act=["xf", "cf", "qk", "g", "gT"], pe=["dft", "pq", "pk", "pv", "qk", "g", "gT", "y"])
        declare("ffn2", QROUNDS, dve=["xs", "xn", "amax", "ls", "ls2", "inv", "y", "yr", "yc", "yT", "a", "b", "fin", "st"], pe=["yT", "mm"])
        attention_layer(3)
        declare("ffn3", ROUNDS // 2, dve=["xn", "h0", "h1", "fin"], act=["xnT", "s0", "s1"], pe=["xnT", "gu0", "gu1", "y"])
        ORDER = ["att0", "ffn0", "att1", "ffn1b", "freq", "ffn2", "att3", "ffn3"]

        dve_chain = sem("dve_chain")
        pool_chain = sem("pool_chain")
        act_chain = sem("act_chain")
        to_pe = sem("column_ready")
        from_pe = sem("column_turned")
        norm_ready = sem("norm_ready")
        hidden_scaled = sem("hidden_scaled")
        eneg_ready = sem("eneg_ready")


        block = ctx.enter_context(nc.Block())

        LATE = [("f_wq", f_wq), ("f_wk", f_wk), ("f_wv", f_wv), ("f_bq", f_bq), ("f_bk", f_bk), ("f_bv", f_bv),
                ("c_unit", f_unit), ("c_dft", dft), ("c_idft", idft), ("c_wave", wave), ("r_raw", r_raw), ("g_raw", g_raw)]

        @block.sync
        def _(sp):
            sp.dma_start(ident[:], dram["c_ident"]).then_inc(loaded["const"], 16)
            sp.dma_start(head_mask[:], dram["c_head_mask"]).then_inc(loaded["const"], 16)
            sp.dma_start(causal[:], dram["c_causal"]).then_inc(loaded["const"], 16)
            sp.dma_start(half_pad[:], dram["c_half_pad"]).then_inc(loaded["const"], 16)
            for c in range(4):
                q = TILES // 4
                sp.dma_start(x[:, c * q:(c + 1) * q, :], x_tiles[:, c * q:(c + 1) * q, :]).then_inc(loaded["x"], 16)
            def weights(L):
                w = att[L]
                for n in ("wq", "wk", "wv", "bq", "bk"):
                    sp.dma_start(w[n], dram[f"a{L}_{n}"]).then_inc(loaded[f"att{L}"], 16)
                sp.dma_start(w["wo"][0:64], dram[f"a{L}_wo"]).then_inc(loaded[f"att{L}"], 16)
                sp.dma_start(w["wo"][64:65, 0, :], dram[f"a{L}_bo"]).then_inc(loaded[f"att{L}"], 16)
                sp.dma_start(w["bv"], dram[f"a{L}_bv"].to_broadcast([P, P])).then_inc(loaded[f"att{L}"], 16)
                if L == 0:
                    sp.dma_start(key_mask, dram["mask_BxS2_bf1"].to_broadcast([P, TOKENS])).then_inc(loaded["const"], 16)
                    for n, where_ in (("gate_up", gate_up), ("down0", down0), ("shared_gu", shared_gu), ("shared_dn", shared_dn), ("router", router)):
                        sp.dma_start(where_, dram[n]).then_inc(loaded["ffn0"], 16)
                    for n, where_ in (("ln_w", ln_w), ("ln_b", ln_b), ("c_rank", rank)):
                        sp.dma_start(where_, dram[n].to_broadcast([P, where_.shape[1]])).then_inc(loaded["ffn0"], 16)
            weights(0)
            weights(1)
            for n, where_ in (("w12", w_raw), ("b1", b1[:])):
                sp.dma_start(where_, dram[n]).then_inc(loaded["ffn1"], 16)
            sp.dma_start(b2[:], dram["b2"].to_broadcast([P, P])).then_inc(loaded["ffn1"], 16)

            def ctx_loads(key):
                lay = layers[key]
                for l in range(LANES):
                    if lay["pe"][l].base:
                        sp.wait_ge(pe_sem[l], lay["pe"][l].base)
                    sp.dma_start(cx[l][:], ctx_tiles[l]).then_inc(ctx_in[l], 16)
                with nc.sync.Fori(0, ROUNDS - 1) as i:
                    for l in range(LANES):
                        sp.wait_ge(pe_sem[l], lay["pe"][l].at(i, lay["pe"][l].names[0]))
                        sp.dma_start(cx[l][:], ctx_tiles[(i + 1) * LANES + l]).then_inc(ctx_in[l], 16)

            ctx_loads("att0")
            if STOP >= 3:
                ctx_loads("att1")
            if STOP >= 5:
                for l in range(LANES):
                    sp.wait_ge(dve_sem[l], layers["ffn1b"]["dve"][l].end(QROUNDS))
                for n, where_ in LATE:
                    sp.dma_start(where_, dram[n]).then_inc(loaded["late"], 16)
                weights(3)
                ctx_loads("freq")
            if STOP >= 7:
                ctx_loads("att3")
            last = layers[ORDER[STOP - 1]]
            for l in range(LANES):
                sp.wait_ge(dve_sem[l], last["dve"][l].end(last["rounds"]))
            sp.dma_start(out_tiles, x[:]).then_inc(stored, 16)
            sp.wait_ge(stored, 16)
            for n, count in (("att1", 8), ("ffn0", 8), ("ffn1", 3)):
                sp.wait_ge(loaded[n], 16 * count)

        @block.gpsimd
        def _(pool):
            fills = []
            for l in range(LANES):
                fills += [(vbd[l][:], 0.0), (oT[l][64:65], 1.0), (vbd[l][0:64, :, 0, 8:9], 1.0), (vbd[l][64:128, :, 1, 8:9], 1.0)]
            fills += [(minus_half[:], -0.5), (ones[:], 1.0), (magic[:], MAGIC), (half[:], 0.5)]
            for n, (where, value) in enumerate(fills):
                if n:
                    pool.wait_ge(filled, n)
                nc.gpsimd.memset(where, value).then_inc(filled, 1)

            def deviations(n):
                pool.wait_ge(vpe_ready, n + 1)
                nc.gpsimd.tensor_tensor(rstd[:], vpe[:], minus_half[:], ALU.pow).then_inc(rstd_ready, 1)

            pool.wait_ge(filled, len(fills))
            deviations(0)
            lay = layers["att0"]
            with nc.gpsimd.Fori(0, ROUNDS) as i:
                for l in range(LANES):
                    pool.wait_ge(act_sem[l], lay["act"][l].at(i, "exp"))
                    nc.gpsimd.nop(nofuse=True)
                    nc.gpsimd.memset(prob[l][0:32, :, 32:64], 0.0)
                    nc.gpsimd.memset(prob[l][64:96, :, 32:64], 0.0).then_inc(pool_sem[l], 1)
            if STOP >= 2:
                deviations(1)
                chain = [0]

                def step(ins):
                    chain[0] += 1
                    ins.then_inc(pool_chain, 1)
                    pool.wait_ge(pool_chain, chain[0])
                pool.wait_ge(rstd_ready, 2)
                step(nc.gpsimd.tensor_tensor(rstd2, rstd[:], rstd[:], ALU.mult))
                step(nc.gpsimd.tensor_scalar(rstd2, rstd2, -EPS, 1.0 + EPS, ALU.mult, ALU.add))
                step(nc.gpsimd.tensor_tensor(rstd2, rstd2, minus_half[:], ALU.pow))
                nc.gpsimd.tensor_tensor(rstd2, rstd2, rstd[:], ALU.mult).then_inc(rstd_ready, 1)
            if STOP >= 3:
                deviations(2)
            if STOP >= 4:
                deviations(3)
            if STOP >= 5:
                deviations(4)
                pool.wait_ge(rstd_ready, 6)
                for l in range(LANES):
                    pool.wait_ge(dve_sem[l], layers["ffn1b"]["dve"][l].end(QROUNDS))
                step(nc.gpsimd.tensor_tensor(norm, rstd[:], rstd[:], ALU.mult))
                step(nc.gpsimd.tensor_scalar(norm, norm, -EPS * P, 1.0 * P, ALU.mult, ALU.add))
                nc.gpsimd.tensor_tensor(norm, norm, half[:], ALU.pow).then_inc(norm_ready, 1)
            if STOP >= 6:
                deviations(5)
            if STOP >= 7:
                deviations(6)
            if STOP >= 8:
                deviations(7)

        @block.scalar
        def _(act):
            def attention(L):
                lay, w = layers[f"att{L}"], att[L]
                act.wait_ge(loaded[f"att{L}"], 16 * 8)
                nc.scalar.activation(scratch[:], magic[:], ACT.Exp, scale=0.0).then_inc(act_chain, 1)
                with nc.scalar.Fori(0, ROUNDS) as i:
                    pe = [lambda n, l=l: act.wait_ge(pe_sem[l], lay["pe"][l].at(i, n)) for l in range(LANES)]
                    for l in range(LANES):
                        pe[l]("xcT")
                        nc.scalar.copy(xcT[l][:], ps_a[l][:, 0:256]).then_inc(act_sem[l], 1)
                    for l in range(LANES):
                        pe[l]("proj")
                        nc.scalar.activation(kT[l][:], ps_a[l][:, 0:128], ACT.Identity, bias=w["bk"]).then_inc(act_sem[l], 1)
                    for l in range(LANES):
                        act.wait_ge(dve_sem[l], lay["dve"][l].at(i, "sub"))
                        nc.scalar.activation(prob[l][:], prob[l][:], ACT.Exp).then_inc(act_sem[l], 1)
                    for l in range(LANES):
                        pe[l]("probT")
                        nc.scalar.copy(probT[l][:], ps_s[l][:]).then_inc(act_sem[l], 1)
                    for l in range(LANES):
                        pe[l]("oT")
                        nc.scalar.copy(oT[l][0:64].rearrange("p j b q -> p b j q"), ps_b[l][0:64, 0:256].rearrange("p (b j q) -> p b j q", b=2, j=2)).then_inc(act_sem[l], 1)
            act.wait_ge(filled, 4 * LANES + 4)
            attention(0)
            if STOP >= 2:
                lay = layers["ffn0"]
                act.wait_ge(act_chain, 1)
                nc.scalar.activation(scratch[:], magic[:], ACT.Silu, scale=0.0).then_inc(act_chain, 1)
                with nc.scalar.Fori(0, ROUNDS) as i:
                    pe = [lambda n, l=l: act.wait_ge(pe_sem[l], lay["pe"][l].at(i, n)) for l in range(LANES)]
                    dve = [lambda n, l=l: act.wait_ge(dve_sem[l], lay["dve"][l].at(i, n)) for l in range(LANES)]
                    for l in range(LANES):
                        pe[l]("nT")
                        nc.scalar.copy(moe[l]["nT"], ps_a[l][:, 0:128]).then_inc(act_sem[l], 1)
                    for l in range(LANES):
                        dve[l]("mx")
                        nc.scalar.activation(moe[l]["th"], moe[l]["mx"], ACT.Tanh, scale=0.5).then_inc(act_sem[l], 1)
                        pe[l]("sh")
                        nc.scalar.activation(moe[l]["silu"][:, 0:FFN0], ps_b[l][:, 0:FFN0], ACT.Silu).then_inc(act_sem[l], 1)
                    for l in range(LANES):
                        pe[l]("xwT")
                        nc.scalar.copy(probT[l][:], ps_s[l][:]).then_inc(act_sem[l], 1)
                    for l in range(LANES):
                        pe[l]("gu")
                        nc.scalar.activation(moe[l]["silu"][:, FFN0:2 * FFN0], ps_a[l][:, 0:FFN0], ACT.Silu).then_inc(act_sem[l], 1)
                    for l in range(LANES):
                        pe[l]("hT")
                        nc.scalar.copy(moe[l]["hT"], ps_b[l][:]).then_inc(act_sem[l], 1)
            if STOP >= 3:
                act.wait_ge(act_chain, 2)
                attention(1)
            if STOP >= 4:
                act.wait_ge(loaded["ffn1"], 16 * 3)
                lay = layers["ffn1a"]
                act.wait_ge(act_chain, 3)
                nc.scalar.activation(scratch[:], magic[:], ACT.Gelu, scale=0.0).then_inc(act_chain, 1)
                with nc.scalar.Fori(0, QROUNDS) as i:
                    for l in range(LANES):
                        for c, bank in enumerate((ps_s[l][:, 0:512], ps_s[l][:, 512:1024], ps_b[l][:], ps_a[l][:])):
                            act.wait_ge(pe_sem[l], lay["pe"][l].at(i, f"m{c}"))
                            nc.scalar.activation(hidden[:, i * LANES + l, c * 512:c * 512 + 512], bank, ACT.Gelu,
                                                 bias=b1[:, c:c + 1], scale=qs[:, 8:9]).then_inc(act_sem[l], 1)
                lay = layers["ffn1b"]
                act.wait_ge(hidden_scaled, 1)
                with nc.scalar.Fori(0, QROUNDS) as i:
                    for l in range(LANES):
                        nc.scalar.activation(hidden[:, i * LANES + l, :], hidden[:, i * LANES + l, :], ACT.Identity,
                                             bias=magic[:], scale=qs[:, 1:2]).then_inc(act_sem[l], 1)
            if STOP >= 5:
                act.wait_ge(norm_ready, 1)
                nc.scalar.activation(eneg, norm, ACT.Exp, scale=-1.0).then_inc(eneg_ready, 1)
                act.wait_ge(loaded["late"], 16 * len(LATE))
                lay = layers["freq"]
                with nc.scalar.Fori(0, ROUNDS) as i:
                    pe = [lambda n, l=l: act.wait_ge(pe_sem[l], lay["pe"][l].at(i, n)) for l in range(LANES)]
                    for l in range(LANES):
                        pe[l]("dft")
                        nc.scalar.copy(xcT[l][:, 0, :], ps_a[l][:, 0:128]).then_inc(act_sem[l], 1)
                        nc.scalar.mul(xcT[l][:, 1, :], ps_a[l][:, 128:256], MEMORY_SCALE).then_inc(act_sem[l], 1)
                    for l in range(LANES):
                        pe[l]("qk")
                        nc.scalar.copy(fl[l]["qk"], ps_b[l][:, 0:128]).then_inc(act_sem[l], 1)
                    for l in range(LANES):
                        pe[l]("g")
                        nc.scalar.copy(fl[l]["g"], ps_a[l][:, 0:128]).then_inc(act_sem[l], 1)
                    for l in range(LANES):
                        pe[l]("gT")
                        nc.scalar.copy(fl[l]["gT"], ps_b[l][:, 0:128]).then_inc(act_sem[l], 1)
            if STOP >= 7:
                act.wait_ge(act_chain, 4)
                attention(3)
            if STOP >= 8:
                lay = layers["ffn3"]
                act.wait_ge(act_chain, 5)
                nc.scalar.activation(scratch[:], magic[:], ACT.Silu, scale=0.0).then_inc(act_chain, 1)
                with nc.scalar.Fori(0, ROUNDS // 2) as i:
                    pe = [lambda n, l=l: act.wait_ge(pe_sem[l], lay["pe"][l].at(i, n)) for l in range(LANES)]
                    for l in range(LANES):
                        pe[l]("xnT")
                        nc.scalar.copy(ff[l]["xnT"], ps_b[l][:, 0:256]).then_inc(act_sem[l], 1)
                    for l in range(LANES):
                        pe[l]("gu0")
                        nc.scalar.activation(ff[l]["silu"][:, 0:512].rearrange("p (c t) -> p c t", c=2),
                                             ps_s[l][:].rearrange("p (c k t) -> p c k t", c=2, k=2)[:, :, 0, :], ACT.Silu).then_inc(act_sem[l], 1)
                        pe[l]("gu1")
                        nc.scalar.activation(ff[l]["silu"][:, 512:768], ps_a[l][:, 0:256], ACT.Silu).then_inc(act_sem[l], 1)

        @block.tensor
        def _(te):
            te.wait_ge(loaded["const"], 16 * 5)
            te.wait_ge(filled, 4 * LANES + 4)

            def attention(L):
                lay, w = layers[f"att{L}"], att[L]
                te.wait_ge(loaded[f"att{L}"], 16 * 8)
                with nc.tensor.Fori(0, ROUNDS) as i:
                    dve = [lambda n, l=l: te.wait_ge(dve_sem[l], lay["dve"][l].at(i, n)) for l in range(LANES)]
                    act = [lambda n, l=l: te.wait_ge(act_sem[l], lay["act"][l].at(i, n)) for l in range(LANES)]
                    for l in range(LANES):
                        dve[l]("xn")
                        nc.tensor.transpose(ps_a[l][:, 0:128], xn[l][:], ident[:])
                        te.wait_ge(ctx_in[l], i * 16 + (lay["ctx"] + 16))
                        nc.tensor.transpose(ps_a[l][:, 128:256], cx[l][:], ident[:]).then_inc(pe_sem[l], 1)
                    for l in range(LANES):
                        act[l]("xcT")
                        nc.tensor.matmul(ps_b[l][:, 0:128], w["wq"], xcT[l][:, 0, :], start=True, stop=True)
                        nc.tensor.matmul(ps_a[l][:, 0:128], w["wk"], xcT[l][:, 1, :], start=True, stop=True)
                        nc.tensor.matmul(ps_b[l][:, 256:384], xcT[l][:, 1, :], w["wv"], start=True, stop=True).then_inc(pe_sem[l], 1)
                    for l in range(LANES):
                        act[l]("kT")
                        dve[l]("qx")
                        for s, first in enumerate((0, 4, 2, 6)):
                            if s >= 2:
                                te.wait_ge(pe_sem[l], lay["pe"][l].at(i, f"s{s - 2}"))
                            for c in (first, first + 1):
                                for b in range(2):
                                    jj = 2 * (c - first)
                                    mm = nc.tensor.matmul(
                                        ps_s[l][:, c * 128 + b * 64:c * 128 + b * 64 + 64],
                                        qx[l][32 * s:32 * s + 32, b, jj:jj + 2, :],
                                        kT[l][32 * s:32 * s + 32, b * 64:b * 64 + 64], start=True, stop=True)
                            mm.then_inc(pe_sem[l], 1)
                    for l in range(LANES):
                        if L == 0:
                            te.wait_ge(pool_sem[l], lay["pool"][l].at(i, "zero"))
                        else:
                            act[l]("exp")
                        for c in range(8):
                            mm = nc.tensor.transpose(ps_s[l][:, c * 128:c * 128 + 128],
                                                     prob[l][:, 2 * c:2 * c + 2, :], ident[:])
                        mm.then_inc(pe_sem[l], 1)
                    for l in range(LANES):
                        act[l]("probT")
                        dve[l]("v")
                        for c in range(8):
                            mm = nc.tensor.matmul(ps_a[l][:, c * 36:c * 36 + 36], probT[l][:, c, :],
                                                  vbd[l][:, 2 * c:2 * c + 2, :, :], start=True, stop=True)
                        mm.then_inc(pe_sem[l], 1)
                    for l in range(LANES):
                        dve[l]("o")
                        nc.tensor.nop(nofuse=True)
                        for b in range(2):
                            mm = nc.tensor.transpose(ps_b[l][0:64, b * 128:b * 128 + 128], o[l][:, b, :, :], ident[:])
                        mm.then_inc(pe_sem[l], 1)
                    for l in range(LANES):
                        act[l]("oT")
                        nc.tensor.matmul(ps_a[l][:, 0:128], oT[l][0:65, 0], w["wo"][0:65, 0, :], start=True, stop=False)
                        nc.tensor.matmul(ps_a[l][:, 0:128], oT[l][0:64, 1], w["wo"][0:64, 1, :], start=False, stop=True).then_inc(pe_sem[l], 1)
            attention(0)
            if STOP >= 2:
                lay = layers["ffn0"]
                te.wait_ge(loaded["ffn0"], 16 * 8)
                with nc.tensor.Fori(0, ROUNDS) as i:
                    dve = [lambda n, l=l: te.wait_ge(dve_sem[l], lay["dve"][l].at(i, n)) for l in range(LANES)]
                    act = [lambda n, l=l: te.wait_ge(act_sem[l], lay["act"][l].at(i, n)) for l in range(LANES)]
                    for l in range(LANES):
                        dve[l]("nb")
                        nc.tensor.transpose(ps_a[l][:, 0:128], moe[l]["nrm"], ident[:]).then_inc(pe_sem[l], 1)
                    for l in range(LANES):
                        act[l]("nT")
                        nc.tensor.matmul(ps_a[l][:, 128:128 + EXPERTS], moe[l]["nT"], router, start=True, stop=True).then_inc(pe_sem[l], 1)
                        nc.tensor.matmul(ps_b[l][:], moe[l]["nT"], shared_gu, start=True, stop=True).then_inc(pe_sem[l], 1)
                    for l in range(LANES):
                        dve[l]("xw")
                        for e in range(EXPERTS):
                            mm = nc.tensor.transpose(ps_s[l][:, e * 128:e * 128 + 128], prob[l][:, 2 * e:2 * e + 2, :], ident[:])
                        mm.then_inc(pe_sem[l], 1)
                    for l in range(LANES):
                        act[l]("xwT")
                        for e in range(EXPERTS):
                            mm = nc.tensor.matmul(ps_a[l][:], probT[l][:, e, :], gate_up[:, e, :], start=(e == 0), stop=(e == EXPERTS - 1))
                        mm.then_inc(pe_sem[l], 1)
                    for l in range(LANES):
                        dve[l]("h")
                        for c in range(4):
                            mm = nc.tensor.transpose(ps_b[l][:, c * 128:c * 128 + 128], moe[l]["h"][:, c * 128:c * 128 + 128], ident[:])
                        mm.then_inc(pe_sem[l], 1)
                    for l in range(LANES):
                        act[l]("hT")
                        for c in range(2):
                            nc.tensor.matmul(ps_a[l][:, 0:128], moe[l]["hT"][:, c * 128:c * 128 + 128], shared_dn[:, c, :], start=(c == 0), stop=(c == 1))
                        for half_ in range(2):
                            for c in range(2):
                                mm = nc.tensor.matmul(ps_s[l][:, half_ * 512:half_ * 512 + 512], moe[l]["hT"][:, 256 + c * 128:256 + c * 128 + 128],
                                                      down0[:, c, half_ * 512:half_ * 512 + 512], start=(c == 0), stop=(c == 1))
                        mm.then_inc(pe_sem[l], 1)
            if STOP >= 3:
                attention(1)

            def turn(columns, n):
                te.wait_ge(to_pe, n + 1)
                nc.tensor.transpose(ps_a[0][0:columns, 0:128], gcol[:, 0:columns], ident[:]).then_inc(from_pe, 1)
                te.wait_ge(to_pe, n + 2)
                nc.tensor.matmul(ps_b[0][:, 0:columns], ones[0:columns, :], gdiag[0:columns, 0:columns], start=True, stop=True).then_inc(from_pe, 1)

            if STOP >= 4:
                turn(4, 0)
                te.wait_ge(to_pe, 3)
                lay = layers["ffn1a"]
                with nc.tensor.Fori(0, QROUNDS) as i:
                    for l in range(LANES):
                        te.wait_ge(dve_sem[l], lay["dve"][l].at(i, "xc"))
                        for k in range(GROUP):
                            mm = nc.tensor.transpose(ps_a[l][:, k * 128:k * 128 + 128], prob[l][:, 2 * k:2 * k + 2, :], ident[:])
                        mm.then_inc(pe_sem[l], 1)
                    for l in range(LANES):
                        te.wait_ge(dve_sem[l], lay["dve"][l].at(i, "xT"))
                        for c, bank in enumerate((ps_s[l][:, 0:512], ps_s[l][:, 512:1024], ps_b[l][:], ps_a[l][:])):
                            nc.tensor.matmul(bank, w_q[:, 0, c * 128:c * 128 + 128], xqT[l], start=True, stop=True).then_inc(pe_sem[l], 1)
                turn(2, 3)
                lay = layers["ffn1b"]
                with nc.tensor.Fori(0, QROUNDS) as i:
                    for l in range(LANES):
                        te.wait_ge(dve_sem[l], lay["dve"][l].at(i, "hb"))
                        for k in range(GROUP):
                            for c in range(4):
                                mm = nc.tensor.matmul(ps_a[l][:, k * 128:k * 128 + 128], hq[l][:, c * 512 + k * 128:c * 512 + k * 128 + 128],
                                                      w_q[:, 1, c * 128:c * 128 + 128], start=(c == 0), stop=(c == 3))
                        mm.then_inc(pe_sem[l], 1)
            if STOP >= 5:
                te.wait_ge(loaded["late"], 16 * len(LATE))
                lay = layers["freq"]
                re, im = slice(0, FREQ), slice(FREQ, SEQ)
                with nc.tensor.Fori(0, ROUNDS) as i:
                    dve = [lambda n, l=l: te.wait_ge(dve_sem[l], lay["dve"][l].at(i, n)) for l in range(LANES)]
                    act = [lambda n, l=l: te.wait_ge(act_sem[l], lay["act"][l].at(i, n)) for l in range(LANES)]

                    def units(bank, l):
                        dst = bank[:, 0:128].rearrange("p (b m) -> p b m", b=2)
                        p1 = fl[l]["p1"].rearrange("p (r b m) -> p r b m", r=4, b=2)
                        p2 = fl[l]["p2"].rearrange("p (r b m) -> p r b m", r=4, b=2)
                        p3 = fl[l]["p3"].rearrange("p (r b m) -> p r b m", r=4, b=2)
                        for r_ in range(4):
                            nc.tensor.matmul(dst[:, :, re], f_unit[:, r_, :], p1[:, r_, :, re], start=(r_ == 0), stop=False, skip_group_check=True)
                            nc.tensor.matmul(dst[:, :, 1:FREQ - 1], f_unit[:, 4 + r_, :], p1[:, r_, :, im], start=False, stop=False, skip_group_check=True)
                            nc.tensor.matmul(dst[:, :, im], f_unit[:, r_, :], p2[:, r_], start=False, stop=False, skip_group_check=True)
                            mm = nc.tensor.matmul(dst[:, :, im], f_unit[:, r_, :], p3[:, r_], start=False, stop=(r_ == 3), skip_group_check=True)
                        mm.then_inc(pe_sem[l], 1)

                    for l in range(LANES):
                        dve[l]("xs")
                        nc.tensor.matmul(ps_a[l][:, 0:128], xn[l][:], dft, start=True, stop=True)
                        te.wait_ge(ctx_in[l], i * 16 + (lay["ctx"] + 16))
                        nc.tensor.matmul(ps_a[l][:, 128:256], cx[l][:], dft, start=True, stop=True).then_inc(pe_sem[l], 1)
                    for l in range(LANES):
                        act[l]("cf")
                        nc.tensor.matmul(ps_a[l][:, 0:128], f_wq, xcT[l][:, 0, :], start=True, stop=True).then_inc(pe_sem[l], 1)
                        for half_, w in enumerate((f_wk, f_wv)):
                            for r_ in range(4):
                                mm = nc.tensor.matmul(ps_s[l][:, half_ * 512 + r_ * 128:half_ * 512 + r_ * 128 + 128], w[:, r_, :], xcT[l][:, 1, :], start=True, stop=True)
                            mm.then_inc(pe_sem[l], 1)
                    for l in range(LANES):
                        dve[l]("p3")
                        units(ps_b[l], l)
                    for l in range(LANES):
                        dve[l]("r3")
                        units(ps_a[l], l)
                    for l in range(LANES):
                        act[l]("g")
                        nc.tensor.transpose(ps_b[l][:, 0:128], fl[l]["g"], ident[:]).then_inc(pe_sem[l], 1)
                    for l in range(LANES):
                        act[l]("gT")
                        nc.tensor.matmul(ps_a[l][:, 0:128], idft, fl[l]["gT"], start=True, stop=True).then_inc(pe_sem[l], 1)
            if STOP >= 6:
                te.wait_ge(to_pe, 6)
                nc.tensor.transpose(ps_a[0][:, 0:128], r_t, ident[:])
                nc.tensor.matmul(ps_a[0][:, 128:256], ones[:], r_diag, start=True, stop=True).then_inc(from_pe, 1)
                te.wait_ge(to_pe, 7)
                lay = layers["ffn2"]
                with nc.tensor.Fori(0, QROUNDS) as i:
                    for l in range(LANES):
                        te.wait_ge(dve_sem[l], lay["dve"][l].at(i, "yc"))
                        for k in range(GROUP):
                            mm = nc.tensor.transpose(ps_a[l][:, k * 128:k * 128 + 128], q8[l]["y"][:, k * 128:k * 128 + 128], ident[:])
                        mm.then_inc(pe_sem[l], 1)
                    for l in range(LANES):
                        te.wait_ge(dve_sem[l], lay["dve"][l].at(i, "yT"))
                        for k in range(GROUP):
                            mm = nc.tensor.matmul(ps_b[l][:, k * 128:k * 128 + 128], q8[l]["yT"][:, k * 128:k * 128 + 128], r_q, start=True, stop=True)
                        mm.then_inc(pe_sem[l], 1)
            if STOP >= 7:
                attention(3)
            if STOP >= 8:
                te.wait_ge(to_pe, 8)
                gw = g_w[:, 0:2 * FFN3].rearrange("p (k c n) -> p k c n", k=2, c=3)
                dw = g_w[:, 2 * FFN3:3 * FFN3].rearrange("p (c n) -> p c n", c=3)
                lay = layers["ffn3"]
                with nc.tensor.Fori(0, ROUNDS // 2) as i:
                    dve = [lambda n, l=l: te.wait_ge(dve_sem[l], lay["dve"][l].at(i, n)) for l in range(LANES)]
                    act = [lambda n, l=l: te.wait_ge(act_sem[l], lay["act"][l].at(i, n)) for l in range(LANES)]
                    for l in range(LANES):
                        dve[l]("xn")
                        for k in range(2):
                            mm = nc.tensor.transpose(ps_b[l][:, k * 128:k * 128 + 128], ff[l]["xn"][:, k * 128:k * 128 + 128], ident[:])
                        mm.then_inc(pe_sem[l], 1)
                    for l in range(LANES):
                        act[l]("xnT")
                        for c, bank in enumerate((ps_s[l][:, 0:512], ps_s[l][:, 512:1024], ps_a[l][:])):
                            for k in range(2):
                                mm = nc.tensor.matmul(bank[:, k * 256:k * 256 + 256], gw[:, k, c, :], ff[l]["xnT"], start=True, stop=True)
                            if c:
                                mm.then_inc(pe_sem[l], 1)
                    for l in range(LANES):
                        dve[l]("h1")
                        for k in range(2):
                            for c in range(3):
                                mm = nc.tensor.matmul(ps_b[l][:, k * 128:k * 128 + 128], ff[l]["hT"][:, c * 256 + k * 128:c * 256 + k * 128 + 128],
                                                      dw[:, c, :], start=(c == 0), stop=(c == 2))
                        mm.then_inc(pe_sem[l], 1)

        @block.vector
        def _(dve):
            count = [0]

            def step(ins):
                count[0] += 1
                ins.then_inc(dve_chain, 1)
                dve.wait_ge(dve_chain, count[0])
            TT, TS, STT = nc.vector.tensor_tensor, nc.vector.tensor_scalar, nc.vector.scalar_tensor_tensor

            def moments():
                me, mo, ve, vo = (stats[:, :, k] for k in (1, 4, 2, 5))
                step(TT(agg[:, 0], me, mo, ALU.add))
                step(TS(mean[:], agg[:, 0], 0.5, None, ALU.mult))
                step(TT(agg[:, 1], me, mo, ALU.subtract))
                step(TT(agg[:, 2], agg[:, 1], agg[:, 1], ALU.mult))
                step(TT(agg[:, 0], ve, vo, ALU.add))
                step(TS(agg[:, 3], agg[:, 0], 1.0 / P, EPS, ALU.mult, ALU.add))
                STT(vpe[:], agg[:, 2], 0.25, agg[:, 3], ALU.mult, ALU.add).then_inc(vpe_ready, 1)

            def finished(key):
                for l in range(LANES):
                    dve.wait_ge(dve_sem[l], layers[key]["dve"][l].end(layers[key]["rounds"]))

            dve.wait_ge(loaded["x"], 16 * 4)
            with nc.vector.Fori(0, TILES) as t:
                nc.vector.bn_stats(stats[:, t, :], x[:, t, :]).then_inc(x_stats, 1)
            dve.wait_ge(x_stats, TILES)
            moments()

            def attention(L, n_rstd):
                lay, w = layers[f"att{L}"], att[L]
                dve.wait_ge(loaded["const"], 16 * 5)
                dve.wait_ge(filled, 4 * LANES + 4)
                dve.wait_ge(loaded[f"att{L}"], 16 * 8)
                dve.wait_ge(rstd_ready, n_rstd)
                bv = w["bv"].rearrange("p (h d) -> p h d", d=HD)
                with nc.vector.Fori(0, ROUNDS) as i:
                    pe = [lambda n, l=l: dve.wait_ge(pe_sem[l], lay["pe"][l].at(i, n)) for l in range(LANES)]
                    own = [lambda n, l=l: dve.wait_ge(dve_sem[l], lay["dve"][l].at(i, n)) for l in range(LANES)]
                    for l in range(LANES):
                        t = i * LANES + l
                        nc.vector.tensor_scalar(xn[l][:], x[:, t, :], mean[:, bass.ds(t, 1)], rstd[:, bass.ds(t, 1)], ALU.subtract, ALU.mult).then_inc(dve_sem[l], 1)
                    for l in range(LANES):
                        pe[l]("proj")
                        for b in range(2):
                            q = nc.vector.scalar_tensor_tensor(qx[l][:, b], ps_b[l][:, b * 64:b * 64 + 64].unsqueeze(1).to_broadcast([P, 4, SEQ]), w["bq"],
                                                               head_mask[:].unsqueeze(2).to_broadcast([P, 4, SEQ]), ALU.add, ALU.mult)
                        q.then_inc(dve_sem[l], 1)
                        for b in range(2):
                            r = slice(64 * b, 64 * b + 64)
                            v = nc.vector.tensor_tensor(vbd[l][r, :, b, 0:8], ps_b[l][r, 256:384].rearrange("p (h d) -> p h d", d=HD), bv[r], ALU.add)
                        v.then_inc(dve_sem[l], 1)
                        if L == 0:
                            t = i * LANES + l
                            nc.vector.scalar_tensor_tensor(am[l], key_mask[:, bass.ds(t * P, P)], 1.0, causal[:], ALU.subtract, ALU.min).then_inc(dve_sem[l], 1)
                    for l in range(LANES):
                        pe[l]("s")
                        s = ps_s[l][:].rearrange("p (g k) -> p g k", k=SEQ)
                        if L == 0:
                            own[l]("am")
                            nc.vector.scalar_tensor_tensor(prob[l][:].rearrange("p (c b) k -> p c (b k)", b=2), am[l].unsqueeze(1).to_broadcast([P, 8, P]), MASKED,
                                                           ps_s[l][:].rearrange("p (c k) -> p c k", k=P), ALU.mult, ALU.add).then_inc(dve_sem[l], 1)
                            s = prob[l][:]
                            own[l]("masked")
                        nc.vector.tensor_reduce(mx[l][:], s, AX.X, ALU.max).then_inc(dve_sem[l], 1)
                        own[l]("mx")
                        nc.vector.tensor_tensor(prob[l][:], s, mx[l][:].unsqueeze(2).to_broadcast([P, 16, SEQ]), ALU.subtract).then_inc(dve_sem[l], 1)
                        if L == 0:
                            nc.vector.tensor_scalar(fx[l][:], mx[l][:], -MASKED / 2, half_pad[:], ALU.is_lt, ALU.mult).then_inc(dve_sem[l], 1)
                    for l in range(LANES):
                        pe[l]("pv")
                        pv = ps_a[l][:, 0:288].rearrange("p (c j b e) -> p c j b e", c=8, j=2, b=2)
                        if L == 0:
                            own[l]("fx")
                            nc.vector.tensor_tensor(rc[l][:], pv[:, :, 0, :, 8], fx[l][:].rearrange("p (c b) -> p c b", b=2), ALU.add).then_inc(dve_sem[l], 1)
                            own[l]("fs")
                            nc.vector.reciprocal(rc[l][:], rc[l][:]).then_inc(dve_sem[l], 1)
                        else:
                            nc.vector.reciprocal(rc[l][:], pv[:, :, 0, :, 8]).then_inc(dve_sem[l], 1)
                        own[l]("rc")
                        for j in range(2):
                            r = slice(64 * j, 64 * j + 64)
                            oo = nc.vector.tensor_tensor(o[l][r].rearrange("p b c d -> p c b d"), pv[r, :, j, :, 0:8],
                                                         rc[l][r].unsqueeze(3).to_broadcast([64, 8, 2, 8]), ALU.mult)
                        oo.then_inc(dve_sem[l], 1)
                    for l in range(LANES):
                        t = i * LANES + l
                        pe[l]("y")
                        nc.vector.tensor_tensor(x[:, t, :], x[:, t, :], ps_a[l][:, 0:128], ALU.add).then_inc(dve_sem[l], 1)
                        own[l]("fin")
                        nc.vector.nop(nofuse=True)
                        nc.vector.bn_stats(stats[:, t, :], x[:, t, :]).then_inc(dve_sem[l], 1)
            attention(0, 1)

            if STOP >= 2:
                finished("att0")
                moments()
                dve.wait_ge(loaded["ffn0"], 16 * 8)
                dve.wait_ge(rstd_ready, 3)
                lay = layers["ffn0"]
                with nc.vector.Fori(0, ROUNDS) as i:
                    pe = [lambda n, l=l: dve.wait_ge(pe_sem[l], lay["pe"][l].at(i, n)) for l in range(LANES)]
                    act = [lambda n, l=l: dve.wait_ge(act_sem[l], lay["act"][l].at(i, n)) for l in range(LANES)]
                    own = [lambda n, l=l: dve.wait_ge(dve_sem[l], lay["dve"][l].at(i, n)) for l in range(LANES)]
                    for l in range(LANES):
                        t, m = i * LANES + l, moe[l]
                        TS(xn[l][:], x[:, t, :], mean[:, bass.ds(t, 1)], rstd[:, bass.ds(t, 1)], ALU.subtract, ALU.mult).then_inc(dve_sem[l], 1)
                        TS(m["nrm"], x[:, t, :], mean[:, bass.ds(t, 1)], rstd2[:, bass.ds(t, 1)], ALU.subtract, ALU.mult).then_inc(dve_sem[l], 1)
                    for l in range(LANES):
                        m = moe[l]
                        own[l]("nrm")
                        TT(m["nrm"], m["nrm"], ln_w, ALU.mult).then_inc(dve_sem[l], 1)
                        own[l]("nw")
                        TT(m["nrm"], m["nrm"], ln_b, ALU.add).then_inc(dve_sem[l], 1)
                    for l in range(LANES):
                        m = moe[l]
                        pe[l]("lg")
                        lg = ps_a[l][:, 128:128 + EXPERTS]
                        nc.vector.tensor_reduce(m["mx"], lg, AX.X, ALU.max).then_inc(dve_sem[l], 1)
                        own[l]("mx")
                        STT(m["eq"], lg, m["mx"], rank, ALU.is_equal, ALU.mult).then_inc(dve_sem[l], 1)
                        own[l]("eq")
                        nc.vector.tensor_reduce(m["pick"], m["eq"], AX.X, ALU.max).then_inc(dve_sem[l], 1)
                        own[l]("pick")
                        TS(m["one"], m["eq"], m["pick"], None, ALU.is_equal).then_inc(dve_sem[l], 1)
                        act[l]("tanh")
                        TS(m["th"], m["th"], 0.5, 0.5, ALU.mult, ALU.add).then_inc(dve_sem[l], 1)
                        own[l]("th")
                        TS(m["w"], m["one"], m["th"], None, ALU.mult).then_inc(dve_sem[l], 1)
                        own[l]("w")
                        TT(prob[l][:].rearrange("p (e j) k -> p e (j k)", j=2), m["nrm"].unsqueeze(1).to_broadcast([P, EXPERTS, P]),
                           m["w"].unsqueeze(2).to_broadcast([P, EXPERTS, P]), ALU.mult).then_inc(dve_sem[l], 1)
                    for l in range(LANES):
                        m = moe[l]
                        act[l]("ssilu")
                        TT(m["h"][:, 0:FFN0], m["silu"][:, 0:FFN0], ps_b[l][:, FFN0:2 * FFN0], ALU.mult).then_inc(dve_sem[l], 1)
                    for l in range(LANES):
                        m = moe[l]
                        act[l]("silu")
                        TT(m["h"][:, FFN0:2 * FFN0], m["silu"][:, FFN0:2 * FFN0], ps_a[l][:, FFN0:2 * FFN0], ALU.mult).then_inc(dve_sem[l], 1)
                        t = i * LANES + l
                        TT(m["acc"], x[:, t, :], xn[l][:], ALU.add).then_inc(dve_sem[l], 1)
                    for l in range(LANES):
                        t, m = i * LANES + l, moe[l]
                        pe[l]("dn")
                        TT(prob[l][:].rearrange("p (e j) k -> p e (j k)", j=2), ps_s[l][:].rearrange("p (e d) -> p e d", e=EXPERTS),
                           m["one"].unsqueeze(2).to_broadcast([P, EXPERTS, P]), ALU.mult).then_inc(dve_sem[l], 1)
                        own[l]("sel")
                        nc.vector.tensor_reduce(m["red"], prob[l][:].rearrange("p (e j) k -> p (j k) e", j=2), AX.X, ALU.add).then_inc(dve_sem[l], 1)
                        TT(m["acc"], m["acc"], ps_a[l][:, 0:128], ALU.add).then_inc(dve_sem[l], 1)
                        own[l]("acc2")
                        TT(x[:, t, :], m["acc"], m["red"], ALU.add).then_inc(dve_sem[l], 1)
                    for l in range(LANES):
                        t = i * LANES + l
                        own[l]("fin")
                        nc.vector.nop(nofuse=True)
                        nc.vector.bn_stats(stats[:, t, :], x[:, t, :]).then_inc(dve_sem[l], 1)
            if STOP >= 3:
                finished("ffn0")
                moments()
                attention(1, 4)

            def everywhere(columns, n):
                dve.wait_ge(from_pe, n + 1)
                step(nc.vector.tensor_reduce(grow[0:columns], ps_a[0][0:columns, 0:128], AX.X, ALU.max))
                TS(gdiag[0:columns, 0:columns], ident[0:columns, 0:columns], grow[0:columns], None, ALU.mult).then_inc(to_pe, 1)
                dve.wait_ge(from_pe, n + 2)
                step(nc.vector.tensor_copy(gall[:, 0:columns], ps_b[0][:, 0:columns]))

            def affine():
                step(TT(qs[:, 0:1], gall[:, 0:1], gall[:, 1:2], ALU.add))
                step(TS(qs[:, 0:1], qs[:, 0:1], 1.0 / 255.0, 1e-8, ALU.mult, ALU.max))
                step(nc.vector.reciprocal(qs[:, 1:2], qs[:, 0:1]))
                step(TS(qs[:, 2:3], gall[:, 1:2], qs[:, 1:2], MAGIC, ALU.mult, ALU.add))
                step(TS(qs[:, 2:3], qs[:, 2:3], MAGIC, 128.0, ALU.subtract, ALU.subtract))
                step(TS(qs[:, 2:3], qs[:, 2:3], -128.0, 127.0, ALU.max, ALU.min))
                step(TS(qs[:, 3:4], qs[:, 2:3], -1.0, MAGIC - 128.0, ALU.mult, ALU.add))
                step(TS(qs[:, 4:5], qs[:, 2:3], -1.0, MAGIC + 127.0, ALU.mult, ALU.add))

            if STOP >= 4:
                finished("att1")
                moments()
                dve.wait_ge(loaded["ffn1"], 16 * 3)
                step(nc.vector.tensor_reduce(tmx[:, 0], x[:], AX.X, ALU.max))
                step(nc.vector.tensor_reduce(tmx[:, 1], x[:], AX.X, ALU.min))
                dve.wait_ge(rstd_ready, 5)
                for k in range(2):
                    step(TT(tmx[:, k], tmx[:, k], mean[:], ALU.subtract))
                    step(TT(tmx[:, k], tmx[:, k], rstd[:], ALU.mult))
                step(nc.vector.tensor_reduce(gcol[:, 0:1], tmx[:, 0], AX.X, ALU.max))
                step(nc.vector.tensor_reduce(gcol[:, 1:2], tmx[:, 1], AX.X, ALU.min))
                step(TS(gcol[:, 1:2], gcol[:, 1:2], -1.0, None, ALU.mult))
                step(nc.vector.tensor_reduce(gcol[:, 2:3], w_raw[:, 0], AX.X, ALU.max, apply_absolute_value=True))
                nc.vector.tensor_reduce(gcol[:, 3:4], w_raw[:, 1], AX.X, ALU.max, apply_absolute_value=True).then_inc(to_pe, 1)
                everywhere(4, 0)
                affine()
                step(TS(qs[:, 5:7], gall[:, 2:4], 1.0 / 127.0, 1e-8, ALU.mult, ALU.max))
                step(nc.vector.reciprocal(gall[:, 2:4], qs[:, 5:7]))
                step(TT(qs[:, 8:9], qs[:, 0:1], qs[:, 5:6], ALU.mult))
                for k in range(2):
                    step(TS(w_rnd, w_raw[:, k], gall[:, 2 + k:3 + k], MAGIC, ALU.mult, ALU.add))
                    step(TS(w_rnd, w_rnd, MAGIC - 127.0, MAGIC + 127.0, ALU.max, ALU.min))
                    wq = TS(w_q[:, k], w_rnd, MAGIC, None, ALU.subtract)
                    if k == 0:
                        step(wq)
                wq.then_inc(to_pe, 1)
                lay = layers["ffn1a"]
                with nc.vector.Fori(0, QROUNDS) as i:
                    own = [lambda n, l=l: dve.wait_ge(dve_sem[l], lay["dve"][l].at(i, n)) for l in range(LANES)]
                    view = [prob[l][:].rearrange("p (k j) d -> p k (j d)", j=2)[:, 0:GROUP] for l in range(LANES)]
                    for l in range(LANES):
                        ts = bass.ds((i * LANES + l) * GROUP, GROUP)
                        TT(view[l], x[:, ts, :], mean[:, ts].unsqueeze(2).to_broadcast([P, GROUP, P]), ALU.subtract).then_inc(dve_sem[l], 1)
                    for l in range(LANES):
                        ts = bass.ds((i * LANES + l) * GROUP, GROUP)
                        own[l]("xs")
                        TT(view[l], view[l], rstd[:, ts].unsqueeze(2).to_broadcast([P, GROUP, P]), ALU.mult).then_inc(dve_sem[l], 1)
                    for l in range(LANES):
                        own[l]("xn")
                        TS(view[l], view[l], qs[:, 1:2], MAGIC, ALU.mult, ALU.add).then_inc(dve_sem[l], 1)
                    for l in range(LANES):
                        own[l]("xr")
                        TS(view[l], view[l], qs[:, 3:4], qs[:, 4:5], ALU.max, ALU.min).then_inc(dve_sem[l], 1)
                    for l in range(LANES):
                        dve.wait_ge(pe_sem[l], lay["pe"][l].at(i, "xT"))
                        TS(xqT[l], ps_a[l][:], MAGIC, None, ALU.subtract).then_inc(dve_sem[l], 1)
                    for l in range(LANES):
                        g = i * LANES + l
                        dve.wait_ge(act_sem[l], lay["act"][l].at(i, "g3"))
                        nc.vector.tensor_reduce(hmm[:, 0, bass.ds(g, 1)], hidden[:, g, :], AX.X, ALU.max).then_inc(dve_sem[l], 1)
                        nc.vector.tensor_reduce(hmm[:, 1, bass.ds(g, 1)], hidden[:, g, :], AX.X, ALU.min).then_inc(dve_sem[l], 1)
                finished("ffn1a")
                step(nc.vector.tensor_reduce(gcol[:, 0:1], hmm[:, 0], AX.X, ALU.max))
                step(nc.vector.tensor_reduce(gcol[:, 1:2], hmm[:, 1], AX.X, ALU.min))
                TS(gcol[:, 1:2], gcol[:, 1:2], -1.0, None, ALU.mult).then_inc(to_pe, 1)
                everywhere(2, 2)
                affine()
                TT(qs[:, 9:10], qs[:, 0:1], qs[:, 6:7], ALU.mult).then_inc(hidden_scaled, 1)
                dve.wait_ge(hidden_scaled, 1)
                lay = layers["ffn1b"]
                with nc.vector.Fori(0, QROUNDS) as i:
                    own = [lambda n, l=l: dve.wait_ge(dve_sem[l], lay["dve"][l].at(i, n)) for l in range(LANES)]
                    for l in range(LANES):
                        g = i * LANES + l
                        dve.wait_ge(act_sem[l], lay["act"][l].at(i, "hr"))
                        TS(hidden[:, g, :], hidden[:, g, :], qs[:, 3:4], qs[:, 4:5], ALU.max, ALU.min).then_inc(dve_sem[l], 1)
                    for l in range(LANES):
                        g = i * LANES + l
                        own[l]("hc")
                        TS(hq[l], hidden[:, g, :], MAGIC, None, ALU.subtract).then_inc(dve_sem[l], 1)
                    for l in range(LANES):
                        y = probT[l][:, 0:GROUP]
                        ts = bass.ds((i * LANES + l) * GROUP, GROUP)
                        dve.wait_ge(pe_sem[l], lay["pe"][l].at(i, "y"))
                        STT(y, ps_a[l][:].rearrange("p (k d) -> p k d", k=GROUP), qs[:, 9:10], b2[:].unsqueeze(1).to_broadcast([P, GROUP, P]), ALU.mult, ALU.add).then_inc(dve_sem[l], 1)
                        own[l]("yb")
                        TT(x[:, ts, :], x[:, ts, :], y, ALU.add).then_inc(dve_sem[l], 1)
                    for l in range(LANES):
                        own[l]("fin")
                        nc.vector.nop(nofuse=True)
                        for k in range(GROUP):
                            t = (i * LANES + l) * GROUP + k
                            st = nc.vector.bn_stats(stats[:, t, :], x[:, t, :])
                        st.then_inc(dve_sem[l], 1)

            if STOP >= 5:
                finished("ffn1b")
                moments()
                dve.wait_ge(loaded["late"], 16 * len(LATE))
                step(nc.vector.memset(dc_q, 0.0))
                for b in range(2):
                    step(TS(dc_q[:, b * SEQ:b * SEQ + 1], f_bq, float(SEQ), None, ALU.mult))
                    step(TS(dc_kv[:, 0, :, b], f_bk, float(SEQ), None, ALU.mult))
                    step(TS(dc_kv[:, 1, :, b], f_bv, float(SEQ), None, ALU.mult))
                dve.wait_ge(eneg_ready, 1)
                s_, u_, v_ = chaos[:, 0], chaos[:, 1], chaos[:, 2]
                step(TS(u_, eneg, 1.0, None, ALU.add))
                step(nc.vector.reciprocal(s_, u_))
                for _ in range(LOGISTIC_STEPS):
                    step(TS(u_, s_, -1.0, 1.0, ALU.mult, ALU.add))
                    step(STT(v_, s_, LOGISTIC, u_, ALU.mult, ALU.mult))
                    s_, v_ = v_, s_
                step(TS(u_, s_, 0.5, 0.1, ALU.subtract, ALU.mult))
                step(TS(u_, u_, 1.0, wave, ALU.add, ALU.mult))
                step(TT(fac, u_, rstd[:], ALU.mult))
                lay = layers["freq"]
                re, im, mid = slice(0, FREQ), slice(FREQ, SEQ), slice(1, FREQ - 1)
                with nc.vector.Fori(0, ROUNDS) as i:
                    pe = [lambda n, l=l: dve.wait_ge(pe_sem[l], lay["pe"][l].at(i, n)) for l in range(LANES)]
                    own = [lambda n, l=l: dve.wait_ge(dve_sem[l], lay["dve"][l].at(i, n)) for l in range(LANES)]

                    def products(l, one, four):
                        a_ = one.rearrange("p (b m) -> p b m", b=2)
                        b_ = four.rearrange("p (r b m) -> p r b m", r=4, b=2)
                        half_spectrum = [P, 4, 2, FREQ - 2]
                        TT(fl[l]["p1"].rearrange("p (r m) -> p r m", r=4), one.unsqueeze(1).to_broadcast([P, 4, P]), four.rearrange("p (r m) -> p r m", r=4), ALU.mult)
                        TT(fl[l]["p2"].rearrange("p (r b m) -> p r b m", r=4, b=2), a_[:, :, mid].unsqueeze(1).to_broadcast(half_spectrum), b_[:, :, :, im], ALU.mult)
                        TT(fl[l]["p3"].rearrange("p (r b m) -> p r b m", r=4, b=2), a_[:, :, im].unsqueeze(1).to_broadcast(half_spectrum), b_[:, :, :, mid], ALU.mult).then_inc(dve_sem[l], 1)
                    for l in range(LANES):
                        t = i * LANES + l
                        TS(xn[l][:], x[:, t, :], mean[:, bass.ds(t, 1)], fac[:, bass.ds(t, 1)], ALU.subtract, ALU.mult).then_inc(dve_sem[l], 1)
                    for l in range(LANES):
                        pe[l]("pq")
                        TT(fl[l]["qh"], ps_a[l][:, 0:128], dc_q, ALU.add).then_inc(dve_sem[l], 1)
                        pe[l]("pk")
                        dc = ps_s[l][:, 0:512].rearrange("p (r b m) -> p r b m", r=4, b=2)[:, :, :, 0]
                        TT(dc, dc, dc_kv[:, 0], ALU.add).then_inc(dve_sem[l], 1)
                        own[l]("kb")
                        products(l, fl[l]["qh"], ps_s[l][:, 0:512])
                        pe[l]("pv")
                        dc = ps_s[l][:, 512:1024].rearrange("p (r b m) -> p r b m", r=4, b=2)[:, :, :, 0]
                        TT(dc, dc, dc_kv[:, 1], ALU.add).then_inc(dve_sem[l], 1)
                    for l in range(LANES):
                        own[l]("vb")
                        dve.wait_ge(act_sem[l], lay["act"][l].at(i, "qk"))
                        products(l, fl[l]["qk"], ps_s[l][:, 512:1024])
                    for l in range(LANES):
                        t = i * LANES + l
                        pe[l]("y")
                        TT(x[:, t, :], x[:, t, :], ps_a[l][:, 0:128], ALU.add).then_inc(dve_sem[l], 1)
                    for l in range(LANES):
                        t = i * LANES + l
                        own[l]("fin")
                        nc.vector.nop(nofuse=True)
                        nc.vector.bn_stats(stats[:, t, :], x[:, t, :]).then_inc(dve_sem[l], 1)

            if STOP >= 6:
                finished("freq")
                moments()
                step(nc.vector.tensor_reduce(r_scale[:, 0:1], r_raw, AX.X, ALU.max, apply_absolute_value=True))
                step(TS(r_scale[:, 0:1], r_scale[:, 0:1], 1e-12, 1.0 / 127.0, ALU.max, ALU.mult))
                step(nc.vector.reciprocal(r_scale[:, 1:2], r_scale[:, 0:1]))
                step(TS(r_t, r_raw, r_scale[:, 1:2], MAGIC, ALU.mult, ALU.add))
                step(TS(r_t, r_t, MAGIC - 127.0, MAGIC + 127.0, ALU.max, ALU.min))
                TS(r_diag, ident[:], r_scale[:, 0:1], None, ALU.mult).then_inc(to_pe, 1)
                dve.wait_ge(from_pe, 5)
                step(TS(r_q, ps_a[0][:, 0:128], MAGIC, None, ALU.subtract))
                nc.vector.tensor_copy(r_bc, ps_a[0][:, 128:256]).then_inc(to_pe, 1)
                dve.wait_ge(to_pe, 7)
                dve.wait_ge(rstd_ready, 7)
                lay = layers["ffn2"]
                with nc.vector.Fori(0, QROUNDS) as i:
                    own = [lambda n, l=l: dve.wait_ge(dve_sem[l], lay["dve"][l].at(i, n)) for l in range(LANES)]
                    view = [q8[l]["y"].rearrange("p (k d) -> p k d", k=GROUP) for l in range(LANES)]
                    wide = [P, GROUP, P]
                    for l in range(LANES):
                        ts = bass.ds((i * LANES + l) * GROUP, GROUP)
                        TT(view[l], x[:, ts, :], mean[:, ts].unsqueeze(2).to_broadcast(wide), ALU.subtract).then_inc(dve_sem[l], 1)
                    for l in range(LANES):
                        ts = bass.ds((i * LANES + l) * GROUP, GROUP)
                        own[l]("xs")
                        TT(view[l], view[l], rstd[:, ts].unsqueeze(2).to_broadcast(wide), ALU.mult).then_inc(dve_sem[l], 1)
                    for l in range(LANES):
                        own[l]("xn")
                        nc.vector.tensor_reduce(q8[l]["amax"], view[l], AX.X, ALU.max, apply_absolute_value=True).then_inc(dve_sem[l], 1)
                    for l in range(LANES):
                        own[l]("amax")
                        TS(q8[l]["ls"], q8[l]["amax"], 1e-12, 1.0 / 127.0, ALU.max, ALU.mult).then_inc(dve_sem[l], 1)
                        own[l]("ls")
                        nc.vector.tensor_copy(q8[l]["amax"], q8[l]["ls"]).then_inc(dve_sem[l], 1)
                        nc.vector.reciprocal(q8[l]["inv"], q8[l]["ls"]).then_inc(dve_sem[l], 1)
                    for l in range(LANES):
                        own[l]("inv")
                        TT(view[l], view[l], q8[l]["inv"].unsqueeze(2).to_broadcast(wide), ALU.mult).then_inc(dve_sem[l], 1)
                    for l in range(LANES):
                        own[l]("y")
                        TS(view[l], view[l], MAGIC, None, ALU.add).then_inc(dve_sem[l], 1)
                    for l in range(LANES):
                        own[l]("yr")
                        TS(view[l], view[l], MAGIC - 127.0, MAGIC + 127.0, ALU.max, ALU.min).then_inc(dve_sem[l], 1)
                    for l in range(LANES):
                        dve.wait_ge(pe_sem[l], lay["pe"][l].at(i, "yT"))
                        TS(q8[l]["yT"], ps_a[l][:], MAGIC, None, ALU.subtract).then_inc(dve_sem[l], 1)
                    for l in range(LANES):
                        ts = bass.ds((i * LANES + l) * GROUP, GROUP)
                        dve.wait_ge(pe_sem[l], lay["pe"][l].at(i, "mm"))
                        TT(view[l], ps_b[l][:].rearrange("p (k d) -> p k d", k=GROUP), r_bc.unsqueeze(1).to_broadcast(wide), ALU.mult).then_inc(dve_sem[l], 1)
                        own[l]("a")
                        TT(view[l], view[l], q8[l]["ls"].unsqueeze(2).to_broadcast(wide), ALU.mult).then_inc(dve_sem[l], 1)
                        own[l]("b")
                        TT(x[:, ts, :], x[:, ts, :], view[l], ALU.add).then_inc(dve_sem[l], 1)
                    for l in range(LANES):
                        own[l]("fin")
                        nc.vector.nop(nofuse=True)
                        for k in range(GROUP):
                            t = (i * LANES + l) * GROUP + k
                            st = nc.vector.bn_stats(stats[:, t, :], x[:, t, :])
                        st.then_inc(dve_sem[l], 1)
            if STOP >= 7:
                finished("ffn2")
                moments()
                attention(3, 8)

            if STOP >= 8:
                finished("att3")
                moments()
                TS(g_w, g_raw, 1.0 / 127.0, None, ALU.mult).then_inc(to_pe, 1)
                dve.wait_ge(rstd_ready, 9)
                lay = layers["ffn3"]
                with nc.vector.Fori(0, ROUNDS // 2) as i:
                    for l in range(LANES):
                        for k in range(2):
                            t = (i * LANES + l) * 2 + k
                            n = TS(ff[l]["xn"][:, k * 128:k * 128 + 128], x[:, t, :], mean[:, bass.ds(t, 1)], rstd[:, bass.ds(t, 1)], ALU.subtract, ALU.mult)
                        n.then_inc(dve_sem[l], 1)
                    for l in range(LANES):
                        dve.wait_ge(act_sem[l], lay["act"][l].at(i, "s0"))
                        TT(ff[l]["hT"][:, 0:512].rearrange("p (c t) -> p c t", c=2), ff[l]["silu"][:, 0:512].rearrange("p (c t) -> p c t", c=2),
                           ps_s[l][:].rearrange("p (c k t) -> p c k t", c=2, k=2)[:, :, 1, :], ALU.mult).then_inc(dve_sem[l], 1)
                        dve.wait_ge(act_sem[l], lay["act"][l].at(i, "s1"))
                        TT(ff[l]["hT"][:, 512:768], ff[l]["silu"][:, 512:768], ps_a[l][:, 256:512], ALU.mult).then_inc(dve_sem[l], 1)
                    for l in range(LANES):
                        ts = bass.ds((i * LANES + l) * 2, 2)
                        dve.wait_ge(pe_sem[l], lay["pe"][l].at(i, "y"))
                        TT(x[:, ts, :], x[:, ts, :], ps_b[l][:, 0:256].rearrange("p (k d) -> p k d", k=2), ALU.add).then_inc(dve_sem[l], 1)


def memory_scale():
    sigmoid = lambda v: np.float32(1) / (np.float32(1) + np.exp(-np.float32(v)))
    part_ = lambda v: np.float32(0.9 * 0.5) + np.float32(0.1) * sigmoid(v)
    return float(np.float32(0.4) * part_(0.7) + np.float32(0.3) * part_(0.8) + np.float32(0.3) * part_(0.6))


MEMORY_SCALE = memory_scale()


def spectral_constants():
    f8 = np.float64
    n, k = np.arange(SEQ), np.arange(FREQ)
    angle = 2 * np.pi * np.outer(n, k) / SEQ
    forward = np.concatenate([np.cos(angle), -np.sin(angle[:, 1:FREQ - 1])], axis=1)
    filt = np.exp(1j * 1.5 * np.arctan(np.log(np.arange(SEQ, dtype=f8) + 1e-10))) ** 3
    turned = np.exp(2j * np.pi * np.outer(k, n) / SEQ)
    both = filt[:FREQ].copy()
    both[1:FREQ - 1] += np.conj(filt[SEQ - k[1:FREQ - 1]])
    g = both[:, None] * turned / SEQ
    inverse = np.concatenate([g.real, -g.imag[1:FREQ - 1]], axis=0)
    twice = lambda m: np.kron(np.eye(2), m).astype(np.float32)
    sign = [[1, 1, 1, 1], [1, -1, 1, -1], [1, -1, -1, 1], [1, 1, -1, -1]]
    units = np.zeros((8, P, P), np.float32)
    for r in range(4):
        for i in range(4):
            j = (i + r) % 4
            for c in range(32):
                units[r, i * 32 + c, (i ^ j) * 32 + c] = sign[i][j]
        units[4 + r] = -units[r]
    lam = np.arange(SEQ, dtype=np.float32) / SEQ
    alpha = np.clip(1.0 * (1.0 + 0.5 * (1.5 - 2.0) / 2.0), 0.1, 3.0)
    wave = np.sin(alpha * lam) * np.cos(-2.0 * lam + (2 * 1 + 1 - 2 * 1.5) * lam ** 2)
    return dict(c_dft=twice(forward), c_idft=twice(inverse), c_unit=np.ascontiguousarray(units.transpose(1, 0, 2)),
                c_wave=np.tile(1.0 + 0.1 * wave, 2).astype(np.float32).reshape(P, 1))



STRIPS = [0, 2, 1, 3]


def kernel(**inputs):
    import numpy as _np
    import concourse.bacc as _bacc
    from concourse import mybir as _mybir
    from concourse.bass_utils import run_bass_kernel_spmd as _run

    a = {k: _np.asarray(v) for k, v in inputs.items()}
    strip = lambda w: w.reshape(w.shape[0], 4, 32)[:, STRIPS].reshape(w.shape[0], 128)
    d = {"x": a["x"].reshape(-1, 128), "ctx_1024": a["ctx_1024"].reshape(-1, 128),
         "mask_BxS2_bf1": a["mask_BxS2_bf1"].view(_np.uint8).reshape(1, -1)}

    def attention(L, wq, wk, wv, wo, bq, bk, bv, bo):
        d.update({f"a{L}_wq": strip(wq), f"a{L}_wk": strip(wk), f"a{L}_wv": wv,
                  f"a{L}_wo": wo.reshape(8, 2, 8, 128).transpose(0, 2, 1, 3).reshape(64, 2, 128),
                  f"a{L}_bq": strip(bq[None]).reshape(128, 1), f"a{L}_bk": strip(bk[None]).reshape(128, 1),
                  f"a{L}_bv": bv.reshape(1, 128), f"a{L}_bo": bo.reshape(1, 128)})
    attention(0, a["L0_xattn_W_q"].T, a["L0_xattn_W_k"].T, a["L0_xattn_W_v"].T, a["L0_xattn_W_o"].T,
              a["L0_xattn_b_q"], a["L0_xattn_b_k"], a["L0_xattn_b_v"], a["L0_xattn_b_o"])
    for L in (1, 3):
        g = lambda n: a[f"L{L}_xattn_{n}"]
        attention(L, g("Wq"), g("Wkv")[:, :128], g("Wkv")[:, 128:], g("Wo"), g("bq"), g("bkv")[:128], g("bkv")[128:], g("bo"))

    f = lambda n: a[f"L0_ffn_{n}"]
    d["gate_up"] = _np.concatenate([f("gate_w"), f("up_w")], axis=2).transpose(1, 0, 2)
    d["down0"] = f("down_w").reshape(8, 2, 128, 128).transpose(2, 1, 0, 3).reshape(128, 2, 1024)
    d["shared_gu"] = _np.concatenate([f("sh_gate"), f("sh_up")], axis=1)
    d["shared_dn"] = f("sh_down").reshape(2, 128, 128).transpose(1, 0, 2)
    d["router"], d["ln_w"], d["ln_b"] = f("router_w"), f("ln_w").reshape(1, -1), f("ln_b").reshape(1, -1)
    d["w12"] = _np.stack([a["L1_ffn_W1"].T, a["L1_ffn_W2"].T.reshape(4, 128, 128).transpose(1, 0, 2).reshape(128, 512)], axis=1)
    d["b1"], d["b2"] = a["L1_ffn_b1"].reshape(4, 128).T, a["L1_ffn_b2"].reshape(1, -1)
    around = lambda w: _np.stack([_np.roll(w, -32 * r_, axis=-1) for r_ in range(4)], axis=1)
    h = lambda n: a[f"L2_xattn_{n}"]
    d["f_wq"], d["f_wk"], d["f_wv"] = h("Wq").T, around(h("Wk").T), around(h("Wv").T)
    d["f_bq"], d["f_bk"], d["f_bv"] = h("bq").reshape(128, 1), around(h("bk")[None])[0].T, around(h("bv")[None])[0].T
    d["r_raw"] = a["L2_ffn_rhs"].T
    m = lambda n: a[f"L3_ffn_{n}"]
    d["g_raw"] = _np.concatenate([m("w_gate").T, m("w_up").T, m("w_down").T.reshape(3, 128, 128).transpose(1, 0, 2).reshape(128, 384)], axis=1)

    r = _np.arange(128)
    d["c_ident"] = _np.eye(128, dtype=_np.float32)
    d["c_head_mask"] = ((r[:, None] % 32 // 8 == _np.arange(4)) * _np.float32(8 ** -0.5)).astype(_np.float32)
    d["c_causal"] = -(r[:, None] % 64 < r[None] % 64).astype(_np.float32)
    d["c_rank"] = (EXPERTS - _np.arange(EXPERTS, dtype=_np.float32)).reshape(1, -1)
    d.update(spectral_constants())
    d["c_half_pad"] = _np.where(r % 64 < 32, 32.0, 0.0).astype(_np.float32).reshape(128, 1)

    nc = _bacc.Bacc("TRN2", target_bir_lowering=False, num_devices=1)
    arrays, dram = {}, {}
    for n, v in d.items():
        v = _np.ascontiguousarray(v)
        arrays[f"in_{n}"] = v
        dram[n] = nc.dram_tensor(f"in_{n}", v.shape, _mybir.dt.from_np(v.dtype), kind="ExternalInput").ap()
    out = nc.dram_tensor("out", (8192, 128), F32, kind="ExternalOutput").ap()
    build_program(nc, dram, out)
    res = _run(nc, [arrays], core_ids=[0])
    return res.results[0]["out"].reshape(128, 64, 128)
```

```python
import math
from contextlib import ExitStack
import numpy as np
import concourse.bass as bass
from concourse import mybir

F32 = mybir.dt.float32
BF16 = mybir.dt.bfloat16
U8 = mybir.dt.uint8
ALU = mybir.AluOpType
ACT = mybir.ActivationFunctionType
AX = mybir.AxisListType

P = 128
TOKENS = 128 * 64
TILES = TOKENS // P
SEQ = 64
LANES = 4
ROUNDS = TILES // LANES
HEADS, HD = 16, 8
EPS = 1e-5
MASKED = 1e30
MAGIC = 1.5 * 2 ** 23
EXPERTS, FFN0, FFN1, FFN3 = 8, 256, 512, 384
GROUP = 4
WIDE = 2
FREQ = SEQ // 2 + 1
LOGISTIC, LOGISTIC_STEPS = 3.9, 10
STOP = 8


class Steps:

    def __init__(self, sem, base, names):
        self.sem, self.base, self.names = sem, base, names

    def at(self, i, name):
        return i * len(self.names) + (self.base + self.names.index(name) + 1)

    def end(self, rounds):
        return self.base + rounds * len(self.names)


def build_program(nc, dram, out):
    with ExitStack() as ctx:
        sb = lambda name, shape, dt=F32: ctx.enter_context(nc.sbuf_tensor(name, shape, dt))
        pb = lambda name, shape: ctx.enter_context(nc.psum_tensor(name, shape, F32))
        sem = lambda name: ctx.enter_context(nc.semaphore(name))

        x = sb("x", [P, TILES, P])
        stats = sb("stats", [P, TILES, 6])
        mean = sb("mean", [P, TILES])
        agg = sb("agg", [P, 4, TILES])
        rstd = sb("rstd", [P, TILES])
        vpe = sb("vpe", [P, TILES])
        minus_half = sb("minus_half", [P, TILES])
        half = sb("half", [P, TILES])
        ident = sb("ident", [P, P])

        head_mask = sb("head_mask", [P, 4])
        causal = sb("causal", [P, P])
        half_pad = sb("half_pad", [P, 1])

        area = sb("area", [P, TOKENS * FFN1 // P])
        where = [0]

        def part(width):
            where[0] += width
            return area[:, where[0] - width:where[0]]
        def attention_weights():
            return dict(wq=part(P), wk=part(P), wv=part(P), wo=part(2 * P).rearrange("p (j n) -> p j n", j=2),
                        bq=part(1), bk=part(1), bv=part(P))
        att = {0: attention_weights(), 1: attention_weights()}
        gate_up = part(EXPERTS * 2 * FFN0).rearrange("p (e n) -> p e n", e=EXPERTS)
        down0 = part(2 * EXPERTS * P).rearrange("p (c n) -> p c n", c=2)
        shared_gu = part(2 * FFN0)
        shared_dn = part(2 * P).rearrange("p (c n) -> p c n", c=2)
        router = part(EXPERTS)
        ln_w = part(P)
        ln_b = part(P)
        rank = part(EXPERTS)
        rstd2 = part(TILES)
        key_mask = part(TOKENS // 4).bitcast(U8)
        am = [part(P) for _ in range(LANES)]
        w_raw = part(2 * FFN1).rearrange("p (k n) -> p k n", k=2)
        w_rnd = part(FFN1)
        moe = []
        for l in range(LANES):
            moe.append(dict(nrm=part(P), nT=part(P), mx=part(1), eq=part(EXPERTS), pick=part(1), one=part(EXPERTS),
                            th=part(1), w=part(EXPERTS), silu=part(2 * FFN0), h=part(2 * FFN0),
                            hT=part(2 * FFN0), acc=part(P), red=part(P)))
        reach = [where[0]]
        hidden = area[:].rearrange("p (g n) -> p g n", n=GROUP * FFN1)
        where[0] = 0
        att[3] = attention_weights()
        f_wq = part(P)
        f_wk = part(4 * P).rearrange("p (r n) -> p r n", r=4)
        f_wv = part(4 * P).rearrange("p (r n) -> p r n", r=4)
        f_bq = part(1)
        f_bk = part(4)
        f_bv = part(4)
        f_unit = part(4 * P).rearrange("p (s n) -> p s n", s=4)
        dft = part(P)
        idft = part(P)
        wave = part(1)
        dc_q = part(P)
        dc_kv = part(16).rearrange("p (v r b) -> p v r b", v=2, r=4)
        chaos = part(3 * TILES).rearrange("p (k t) -> p k t", k=3)
        norm = part(TILES)
        eneg = part(TILES)
        fac = part(TILES)
        fl = []
        for l in range(LANES):
            fl.append(dict(qh=part(P), p1=part(4 * P), p2=part(4 * 2 * (FREQ - 2)), p3=part(4 * 2 * (FREQ - 2)), qk=part(P), g=part(P), gT=part(P)))
        r_raw = part(P)
        r_t = part(P)
        r_scale = part(2)
        r_diag = part(P)
        r_bc = part(P)
        r_q = part(P // 2).bitcast(BF16)
        q8 = []
        for l in range(WIDE):
            q8.append(dict(amax=part(GROUP), ls=part(GROUP), inv=part(GROUP), y=part(GROUP * P), yT=part(GROUP * P // 2).bitcast(BF16)))
        g_raw = part(3 * FFN3).bitcast(mybir.dt.int32)
        g_w = part(3 * FFN3)
        ff = []
        for l in range(WIDE):
            ff.append(dict(xn=part(2 * P), xnT=part(2 * P), silu=part(2 * FFN3), hT=part(2 * FFN3)))

        reach.append(where[0])

        w_q = sb("w_q", [P, 2, FFN1], BF16)
        b1 = sb("b1", [P, 4])
        b2 = sb("b2", [P, P])
        ones = sb("ones", [P, P])
        magic = sb("magic", [P, 1])
        scratch = sb("scratch", [P, 1])
        tmx = sb("tmx", [P, 2, TILES])
        gcol = sb("gcol", [P, 4])
        grow = sb("grow", [4, 1])
        gdiag = sb("gdiag", [4, 4])
        gall = sb("gall", [P, 4])
        qs = sb("qs", [P, 16])
        hmm = sb("hmm", [P, 2, TILES // GROUP])

        EARLY = 2
        end = [TOKENS * FFN1 // P]

        def lane(name, shape):
            width = math.prod(shape[1:])
            first = [sb(f"{name}{l}", shape)[:] for l in range(EARLY)]
            rest = []
            for l in range(EARLY, LANES):
                end[0] -= width
                flat = area[0:shape[0], end[0]:end[0] + width]
                if len(shape) > 2:
                    names = "abc"[:len(shape) - 1]
                    flat = flat.rearrange(f"p ({' '.join(names)}) -> p {' '.join(names)}", **dict(zip(names, shape[1:])))
                rest.append(flat)
            return first + rest
        xn = lane("xn", [P, P])
        cx = lane("cx", [P, P])
        xcT = lane("xcT", [P, 2, P])
        qx = lane("qx", [P, 2, 4, SEQ])
        kT = lane("kT", [P, P])
        vbd = lane("vbd", [P, HEADS, 2, 9])
        mx = lane("mx", [P, 16])
        prob = lane("prob", [P, 16, SEQ])
        probT = lane("probT", [P, 8, P])
        rc = lane("rc", [P, 8, 2])
        fx = lane("fx", [P, 16])
        o = lane("o", [P, 2, 8, 8])
        oT = lane("oT", [65, 2, 2, SEQ])
        assert max(reach) <= end[0]
        xqT = [qx[l][:].rearrange("p b j q -> p (b j q)")[:, 0:256].bitcast(BF16) for l in range(WIDE)]
        hq = [prob[l][:].rearrange("p g k -> p (g k)").bitcast(BF16) for l in range(WIDE)]

        ps_s = [pb(f"ps{l}", [P, 1024]) for l in range(LANES)]
        ps_a = [p_[:, 0:512] for p_ in ps_s]
        ps_b = [p_[:, 512:1024] for p_ in ps_s]
        wide_a = [ps_s[WIDE + l][:, 0:512] for l in range(WIDE)]
        wide_b = [ps_s[WIDE + l][:, 512:1024] for l in range(WIDE)]

        loaded = {n: sem(f"loaded_{n}") for n in ("x", "const", "att0", "att1", "att3", "ffn0", "ffn1", "late")}
        ctx_in = [sem(f"ctx_in{l}") for l in range(LANES)]
        dve_sem = [sem(f"dve_done{l}") for l in range(LANES)]
        act_sem = [sem(f"act_done{l}") for l in range(LANES)]
        pe_sem = [sem(f"pe_done{l}") for l in range(LANES)]
        pool_sem = [sem(f"pool_done{l}") for l in range(LANES)]
        filled = sem("filled")
        x_stats = sem("x_stats")
        rstd_ready = sem("rstd_ready")
        vpe_ready = sem("vpe_ready")
        stored = sem("stored")

        x_tiles = dram["x"].rearrange("(t p) d -> p t d", p=P)
        ctx_tiles = dram["ctx_1024"].rearrange("(t p) d -> t p d", p=P)
        out_tiles = out.rearrange("(t p) d -> p t d", p=P)

        layers = {}
        base = [dict(dve=0, act=0, pe=0, pool=0, ctx=0) for _ in range(LANES)]

        def declare(key, rounds, dve=(), act=(), pe=(), pool=(), context=False, lanes=LANES):
            lay = dict(rounds=rounds, lanes=lanes, ctx=base[0]["ctx"])
            for n, names, sems in (("dve", dve, dve_sem), ("act", act, act_sem), ("pe", pe, pe_sem), ("pool", pool, pool_sem)):
                lay[n] = [Steps(sems[l], base[l][n], names) for l in range(lanes)]
                for l in range(lanes):
                    base[l][n] += rounds * len(names)
            for l in range(lanes):
                base[l]["ctx"] += 16 * rounds if context else 0
            layers[key] = lay

        def attention_layer(L):
            declare(f"att{L}", ROUNDS, context=True,
                    dve=["xn", "qx", "v"] + (["am", "masked"] if L == 0 else []) + ["mx", "sub"]
                        + (["fx", "fs"] if L == 0 else []) + ["rc", "o", "fin", "st"],
                    act=["xcT", "kT", "exp", "probT", "oT"],
                    pe=["xcT", "proj", "s0", "s1", "s2", "s", "probT", "pv", "oT", "y"],
                    pool=["zero"] if L == 0 else [])
        QROUNDS = TILES // GROUP // WIDE
        attention_layer(0)
        declare("ffn0", ROUNDS, dve=["xn", "nrm", "nw", "nb", "mx", "eq", "pick", "one", "th", "w", "xw", "sh", "h", "acc", "acc2", "sel", "red", "fin", "st"],
                act=["nT", "tanh", "ssilu", "xwT", "silu", "hT"], pe=["nT", "lg", "sh", "xwT", "gu", "hT", "sdn", "dn"])
        attention_layer(1)
        declare("ffn1a", QROUNDS, lanes=WIDE, dve=["xs", "xn", "xr", "xc", "xT", "hmx", "hmn"], act=["g0", "g1", "g2", "g3"],
                pe=["xT", "m0", "m1", "m2", "m3"])
        declare("ffn1b", QROUNDS, lanes=WIDE, dve=["hc", "hb", "yb", "fin", "st"], act=["hr"], pe=["y"])
        declare("freq", ROUNDS, context=True, dve=["xs", "q", "kb", "p", "pm", "ps", "pz", "vb", "r", "rm", "rs", "rz", "fin", "st"],
                act=["xf", "cf", "qk", "g", "gT"], pe=["dft", "pq", "pk", "pv", "qk", "g", "gT", "y"])
        declare("ffn2", QROUNDS, lanes=WIDE, dve=["xs", "xn", "amax", "ls", "ls2", "inv", "y", "yr", "yc", "yT", "a", "b", "fin", "st"], pe=["yT", "mm"])
        attention_layer(3)
        declare("ffn3", TILES // 2 // WIDE, lanes=WIDE, dve=["xn", "h0", "h1", "fin"], act=["xnT", "s0", "s1"], pe=["xnT", "gu0", "gu1", "y"])
        ORDER = ["att0", "ffn0", "att1", "ffn1b", "freq", "ffn2", "att3", "ffn3"]

        FILLS = 4 * LANES + 4
        LATE_FILLS = FILLS + 4 * (LANES - EARLY)

        dve_chain = sem("dve_chain")
        pool_chain = sem("pool_chain")
        act_chain = sem("act_chain")
        to_pe = sem("column_ready")
        from_pe = sem("column_turned")
        norm_ready = sem("norm_ready")
        hidden_scaled = sem("hidden_scaled")
        eneg_ready = sem("eneg_ready")


        block = ctx.enter_context(nc.Block())

        LATE = [("f_wq", f_wq), ("f_wk", f_wk), ("f_wv", f_wv), ("f_bq", f_bq), ("f_bk", f_bk), ("f_bv", f_bv),
                ("c_unit", f_unit), ("c_dft", dft), ("c_idft", idft), ("c_wave", wave), ("r_raw", r_raw), ("g_raw", g_raw)]

        @block.sync
        def _(sp):
            sp.dma_start(ident[:], dram["c_ident"]).then_inc(loaded["const"], 16)
            sp.dma_start(head_mask[:], dram["c_head_mask"]).then_inc(loaded["const"], 16)
            sp.dma_start(causal[:], dram["c_causal"]).then_inc(loaded["const"], 16)
            sp.dma_start(half_pad[:], dram["c_half_pad"]).then_inc(loaded["const"], 16)
            for c in range(4):
                q = TILES // 4
                sp.dma_start(x[:, c * q:(c + 1) * q, :], x_tiles[:, c * q:(c + 1) * q, :]).then_inc(loaded["x"], 16)
            def weights(L):
                w = att[L]
                for n in ("wq", "wk", "wv", "bq", "bk"):
                    sp.dma_start(w[n], dram[f"a{L}_{n}"]).then_inc(loaded[f"att{L}"], 16)
                sp.dma_start(w["wo"][0:64], dram[f"a{L}_wo"]).then_inc(loaded[f"att{L}"], 16)
                sp.dma_start(w["wo"][64:65, 0, :], dram[f"a{L}_bo"]).then_inc(loaded[f"att{L}"], 16)
                sp.dma_start(w["bv"], dram[f"a{L}_bv"].to_broadcast([P, P])).then_inc(loaded[f"att{L}"], 16)
                if L == 0:
                    sp.dma_start(key_mask, dram["mask_BxS2_bf1"].to_broadcast([P, TOKENS])).then_inc(loaded["const"], 16)
                    for n, where_ in (("gate_up", gate_up), ("down0", down0), ("shared_gu", shared_gu), ("shared_dn", shared_dn), ("router", router)):
                        sp.dma_start(where_, dram[n]).then_inc(loaded["ffn0"], 16)
                    for n, where_ in (("ln_w", ln_w), ("ln_b", ln_b), ("c_rank", rank)):
                        sp.dma_start(where_, dram[n].to_broadcast([P, where_.shape[1]])).then_inc(loaded["ffn0"], 16)
            weights(0)
            weights(1)
            for n, where_ in (("w12", w_raw), ("b1", b1[:])):
                sp.dma_start(where_, dram[n]).then_inc(loaded["ffn1"], 16)
            sp.dma_start(b2[:], dram["b2"].to_broadcast([P, P])).then_inc(loaded["ffn1"], 16)

            def ctx_loads(key):
                lay = layers[key]
                for l in range(LANES):
                    if lay["pe"][l].base:
                        sp.wait_ge(pe_sem[l], lay["pe"][l].base)
                    sp.dma_start(cx[l][:], ctx_tiles[l]).then_inc(ctx_in[l], 16)
                with nc.sync.Fori(0, ROUNDS - 1) as i:
                    for l in range(LANES):
                        sp.wait_ge(pe_sem[l], lay["pe"][l].at(i, lay["pe"][l].names[0]))
                        sp.dma_start(cx[l][:], ctx_tiles[(i + 1) * LANES + l]).then_inc(ctx_in[l], 16)

            ctx_loads("att0")
            if STOP >= 3:
                ctx_loads("att1")
            if STOP >= 5:
                for l in range(WIDE):
                    sp.wait_ge(dve_sem[l], layers["ffn1b"]["dve"][l].end(QROUNDS))
                for n, where_ in LATE:
                    sp.dma_start(where_, dram[n]).then_inc(loaded["late"], 16)
                weights(3)
                ctx_loads("freq")
            if STOP >= 7:
                ctx_loads("att3")
            last = layers[ORDER[STOP - 1]]
            for l in range(last["lanes"]):
                sp.wait_ge(dve_sem[l], last["dve"][l].end(last["rounds"]))
            sp.dma_start(out_tiles, x[:]).then_inc(stored, 16)
            sp.wait_ge(stored, 16)
            for n, count in (("att1", 8), ("ffn0", 8), ("ffn1", 3)):
                sp.wait_ge(loaded[n], 16 * count)

        @block.gpsimd
        def _(pool):
            fill_count = [0]

            def fill(fills):
                for where_, value in fills:
                    if fill_count[0]:
                        pool.wait_ge(filled, fill_count[0])
                    nc.gpsimd.memset(where_, value).then_inc(filled, 1)
                    fill_count[0] += 1

            def lane_fills(lanes):
                for l in lanes:
                    fill([(vbd[l][:], 0.0), (oT[l][64:65], 1.0), (vbd[l][0:64, :, 0, 8:9], 1.0), (vbd[l][64:128, :, 1, 8:9], 1.0)])
            lane_fills(range(LANES))
            fill([(minus_half[:], -0.5), (ones[:], 1.0), (magic[:], MAGIC), (half[:], 0.5)])

            def deviations(n):
                pool.wait_ge(vpe_ready, n + 1)
                nc.gpsimd.tensor_tensor(rstd[:], vpe[:], minus_half[:], ALU.pow).then_inc(rstd_ready, 1)

            pool.wait_ge(filled, fill_count[0])
            deviations(0)
            lay = layers["att0"]
            with nc.gpsimd.Fori(0, ROUNDS) as i:
                for l in range(LANES):
                    pool.wait_ge(act_sem[l], lay["act"][l].at(i, "exp"))
                    nc.gpsimd.nop(nofuse=True)
                    nc.gpsimd.memset(prob[l][0:32, :, 32:64], 0.0)
                    nc.gpsimd.memset(prob[l][64:96, :, 32:64], 0.0).then_inc(pool_sem[l], 1)
            if STOP >= 2:
                deviations(1)
                chain = [0]

                def step(ins):
                    chain[0] += 1
                    ins.then_inc(pool_chain, 1)
                    pool.wait_ge(pool_chain, chain[0])
                pool.wait_ge(rstd_ready, 2)
                step(nc.gpsimd.tensor_tensor(rstd2, rstd[:], rstd[:], ALU.mult))
                step(nc.gpsimd.tensor_scalar(rstd2, rstd2, -EPS, 1.0 + EPS, ALU.mult, ALU.add))
                step(nc.gpsimd.tensor_tensor(rstd2, rstd2, minus_half[:], ALU.pow))
                nc.gpsimd.tensor_tensor(rstd2, rstd2, rstd[:], ALU.mult).then_inc(rstd_ready, 1)
            if STOP >= 3:
                deviations(2)
            if STOP >= 4:
                deviations(3)
            if STOP >= 5:
                deviations(4)
                pool.wait_ge(rstd_ready, 6)
                for l in range(WIDE):
                    pool.wait_ge(dve_sem[l], layers["ffn1b"]["dve"][l].end(QROUNDS))
                step(nc.gpsimd.tensor_tensor(norm, rstd[:], rstd[:], ALU.mult))
                step(nc.gpsimd.tensor_scalar(norm, norm, -EPS * P, 1.0 * P, ALU.mult, ALU.add))
                nc.gpsimd.tensor_tensor(norm, norm, half[:], ALU.pow).then_inc(norm_ready, 1)
            if STOP >= 6:
                deviations(5)
            if STOP >= 7:
                for l in range(WIDE):
                    pool.wait_ge(dve_sem[l], layers["ffn1b"]["dve"][l].end(QROUNDS))
                lane_fills(range(EARLY, LANES))
                pool.wait_ge(filled, fill_count[0])
                deviations(6)
            if STOP >= 8:
                deviations(7)

        @block.scalar
        def _(act):
            def attention(L):
                lay, w = layers[f"att{L}"], att[L]
                act.wait_ge(loaded[f"att{L}"], 16 * 8)
                nc.scalar.activation(scratch[:], magic[:], ACT.Exp, scale=0.0).then_inc(act_chain, 1)
                with nc.scalar.Fori(0, ROUNDS) as i:
                    pe = [lambda n, l=l: act.wait_ge(pe_sem[l], lay["pe"][l].at(i, n)) for l in range(LANES)]
                    for l in range(LANES):
                        pe[l]("xcT")
                        nc.scalar.copy(xcT[l][:], ps_a[l][:, 0:256]).then_inc(act_sem[l], 1)
                    for l in range(LANES):
                        pe[l]("proj")
                        nc.scalar.activation(kT[l][:], ps_a[l][:, 0:128], ACT.Identity, bias=w["bk"]).then_inc(act_sem[l], 1)
                    for l in range(LANES):
                        act.wait_ge(dve_sem[l], lay["dve"][l].at(i, "sub"))
                        nc.scalar.activation(prob[l][:], prob[l][:], ACT.Exp).then_inc(act_sem[l], 1)
                    for l in range(LANES):
                        pe[l]("probT")
                        nc.scalar.copy(probT[l][:], ps_s[l][:]).then_inc(act_sem[l], 1)
                    for l in range(LANES):
                        pe[l]("oT")
                        nc.scalar.copy(oT[l][0:64].rearrange("p j b q -> p b j q"), ps_b[l][0:64, 0:256].rearrange("p (b j q) -> p b j q", b=2, j=2)).then_inc(act_sem[l], 1)
            act.wait_ge(filled, FILLS)
            attention(0)
            if STOP >= 2:
                lay = layers["ffn0"]
                act.wait_ge(act_chain, 1)
                nc.scalar.activation(scratch[:], magic[:], ACT.Silu, scale=0.0).then_inc(act_chain, 1)
                with nc.scalar.Fori(0, ROUNDS) as i:
                    pe = [lambda n, l=l: act.wait_ge(pe_sem[l], lay["pe"][l].at(i, n)) for l in range(LANES)]
                    dve = [lambda n, l=l: act.wait_ge(dve_sem[l], lay["dve"][l].at(i, n)) for l in range(LANES)]
                    for l in range(LANES):
                        pe[l]("nT")
                        nc.scalar.copy(moe[l]["nT"], ps_a[l][:, 0:128]).then_inc(act_sem[l], 1)
                    for l in range(LANES):
                        dve[l]("mx")
                        nc.scalar.activation(moe[l]["th"], moe[l]["mx"], ACT.Tanh, scale=0.5).then_inc(act_sem[l], 1)
                        pe[l]("sh")
                        nc.scalar.activation(moe[l]["silu"][:, 0:FFN0], ps_b[l][:, 0:FFN0], ACT.Silu).then_inc(act_sem[l], 1)
                    for l in range(LANES):
                        pe[l]("xwT")
                        nc.scalar.copy(probT[l][:], ps_s[l][:]).then_inc(act_sem[l], 1)
                    for l in range(LANES):
                        pe[l]("gu")
                        nc.scalar.activation(moe[l]["silu"][:, FFN0:2 * FFN0], ps_a[l][:, 0:FFN0], ACT.Silu).then_inc(act_sem[l], 1)
                    for l in range(LANES):
                        pe[l]("hT")
                        nc.scalar.copy(moe[l]["hT"], ps_b[l][:]).then_inc(act_sem[l], 1)
            if STOP >= 3:
                act.wait_ge(act_chain, 2)
                attention(1)
            if STOP >= 4:
                act.wait_ge(loaded["ffn1"], 16 * 3)
                lay = layers["ffn1a"]
                act.wait_ge(act_chain, 3)
                nc.scalar.activation(scratch[:], magic[:], ACT.Gelu, scale=0.0).then_inc(act_chain, 1)
                with nc.scalar.Fori(0, QROUNDS) as i:
                    for l in range(WIDE):
                        for c, bank in enumerate((ps_s[l][:, 0:512], ps_s[l][:, 512:1024], wide_b[l][:], wide_a[l][:])):
                            act.wait_ge(pe_sem[l], lay["pe"][l].at(i, f"m{c}"))
                            nc.scalar.activation(hidden[:, i * WIDE + l, c * 512:c * 512 + 512], bank, ACT.Gelu,
                                                 bias=b1[:, c:c + 1], scale=qs[:, 8:9]).then_inc(act_sem[l], 1)
                lay = layers["ffn1b"]
                act.wait_ge(hidden_scaled, 1)
                with nc.scalar.Fori(0, QROUNDS) as i:
                    for l in range(WIDE):
                        nc.scalar.activation(hidden[:, i * WIDE + l, :], hidden[:, i * WIDE + l, :], ACT.Identity,
                                             bias=magic[:], scale=qs[:, 1:2]).then_inc(act_sem[l], 1)
            if STOP >= 5:
                act.wait_ge(norm_ready, 1)
                nc.scalar.activation(eneg, norm, ACT.Exp, scale=-1.0).then_inc(eneg_ready, 1)
                act.wait_ge(loaded["late"], 16 * len(LATE))
                lay = layers["freq"]
                with nc.scalar.Fori(0, ROUNDS) as i:
                    pe = [lambda n, l=l: act.wait_ge(pe_sem[l], lay["pe"][l].at(i, n)) for l in range(LANES)]
                    for l in range(LANES):
                        pe[l]("dft")
                        nc.scalar.copy(xcT[l][:, 0, :], ps_a[l][:, 0:128]).then_inc(act_sem[l], 1)
                        nc.scalar.mul(xcT[l][:, 1, :], ps_a[l][:, 128:256], MEMORY_SCALE).then_inc(act_sem[l], 1)
                    for l in range(LANES):
                        pe[l]("qk")
                        nc.scalar.copy(fl[l]["qk"], ps_b[l][:, 0:128]).then_inc(act_sem[l], 1)
                    for l in range(LANES):
                        pe[l]("g")
                        nc.scalar.copy(fl[l]["g"], ps_b[l][:, 0:128]).then_inc(act_sem[l], 1)
                    for l in range(LANES):
                        pe[l]("gT")
                        nc.scalar.copy(fl[l]["gT"], ps_a[l][:, 0:128]).then_inc(act_sem[l], 1)
            if STOP >= 7:
                act.wait_ge(act_chain, 4)
                attention(3)
            if STOP >= 8:
                lay = layers["ffn3"]
                act.wait_ge(act_chain, 5)
                nc.scalar.activation(scratch[:], magic[:], ACT.Silu, scale=0.0).then_inc(act_chain, 1)
                with nc.scalar.Fori(0, TILES // 2 // WIDE) as i:
                    pe = [lambda n, l=l: act.wait_ge(pe_sem[l], lay["pe"][l].at(i, n)) for l in range(WIDE)]
                    for l in range(WIDE):
                        pe[l]("xnT")
                        nc.scalar.copy(ff[l]["xnT"], wide_b[l][:, 0:256]).then_inc(act_sem[l], 1)
                    for l in range(WIDE):
                        pe[l]("gu0")
                        nc.scalar.activation(ff[l]["silu"][:, 0:512].rearrange("p (c t) -> p c t", c=2),
                                             ps_s[l][:].rearrange("p (c k t) -> p c k t", c=2, k=2)[:, :, 0, :], ACT.Silu).then_inc(act_sem[l], 1)
                        pe[l]("gu1")
                        nc.scalar.activation(ff[l]["silu"][:, 512:768], wide_a[l][:, 0:256], ACT.Silu).then_inc(act_sem[l], 1)

        @block.tensor
        def _(te):
            te.wait_ge(loaded["const"], 16 * 5)
            te.wait_ge(filled, FILLS)

            def attention(L):
                lay, w = layers[f"att{L}"], att[L]
                te.wait_ge(loaded[f"att{L}"], 16 * 8)
                if L == 3:
                    te.wait_ge(filled, LATE_FILLS)
                with nc.tensor.Fori(0, ROUNDS) as i:
                    dve = [lambda n, l=l: te.wait_ge(dve_sem[l], lay["dve"][l].at(i, n)) for l in range(LANES)]
                    act = [lambda n, l=l: te.wait_ge(act_sem[l], lay["act"][l].at(i, n)) for l in range(LANES)]
                    for l in range(LANES):
                        dve[l]("xn")
                        nc.tensor.transpose(ps_a[l][:, 0:128], xn[l][:], ident[:])
                        te.wait_ge(ctx_in[l], i * 16 + (lay["ctx"] + 16))
                        nc.tensor.transpose(ps_a[l][:, 128:256], cx[l][:], ident[:]).then_inc(pe_sem[l], 1)
                    for l in range(LANES):
                        act[l]("xcT")
                        nc.tensor.matmul(ps_b[l][:, 0:128], w["wq"], xcT[l][:, 0, :], start=True, stop=True)
                        nc.tensor.matmul(ps_a[l][:, 0:128], w["wk"], xcT[l][:, 1, :], start=True, stop=True)
                        nc.tensor.matmul(ps_b[l][:, 256:384], xcT[l][:, 1, :], w["wv"], start=True, stop=True).then_inc(pe_sem[l], 1)
                    for l in range(LANES):
                        act[l]("kT")
                        dve[l]("v")
                        for s, first in enumerate((0, 4, 2, 6)):
                            if s >= 2:
                                te.wait_ge(pe_sem[l], lay["pe"][l].at(i, f"s{s - 2}"))
                            for c in (first, first + 1):
                                for b in range(2):
                                    jj = 2 * (c - first)
                                    mm = nc.tensor.matmul(
                                        ps_s[l][:, c * 128 + b * 64:c * 128 + b * 64 + 64],
                                        qx[l][32 * s:32 * s + 32, b, jj:jj + 2, :],
                                        kT[l][32 * s:32 * s + 32, b * 64:b * 64 + 64], start=True, stop=True)
                            mm.then_inc(pe_sem[l], 1)
                    for l in range(LANES):
                        if L == 0:
                            te.wait_ge(pool_sem[l], lay["pool"][l].at(i, "zero"))
                        else:
                            act[l]("exp")
                        for c in range(8):
                            mm = nc.tensor.transpose(ps_s[l][:, c * 128:c * 128 + 128],
                                                     prob[l][:, 2 * c:2 * c + 2, :], ident[:])
                        mm.then_inc(pe_sem[l], 1)
                    for l in range(LANES):
                        act[l]("probT")
                        dve[l]("v")
                        for c in range(8):
                            mm = nc.tensor.matmul(ps_a[l][:, c * 36:c * 36 + 36], probT[l][:, c, :],
                                                  vbd[l][:, 2 * c:2 * c + 2, :, :], start=True, stop=True)
                        mm.then_inc(pe_sem[l], 1)
                    for l in range(LANES):
                        dve[l]("o")
                        nc.tensor.nop(nofuse=True)
                        for b in range(2):
                            mm = nc.tensor.transpose(ps_b[l][0:64, b * 128:b * 128 + 128], o[l][:, b, :, :], ident[:])
                        mm.then_inc(pe_sem[l], 1)
                    for l in range(LANES):
                        act[l]("oT")
                        nc.tensor.matmul(ps_a[l][:, 0:128], oT[l][0:65, 0], w["wo"][0:65, 0, :], start=True, stop=False)
                        nc.tensor.matmul(ps_a[l][:, 0:128], oT[l][0:64, 1], w["wo"][0:64, 1, :], start=False, stop=True).then_inc(pe_sem[l], 1)
            attention(0)
            if STOP >= 2:
                lay = layers["ffn0"]
                te.wait_ge(loaded["ffn0"], 16 * 8)
                with nc.tensor.Fori(0, ROUNDS) as i:
                    dve = [lambda n, l=l: te.wait_ge(dve_sem[l], lay["dve"][l].at(i, n)) for l in range(LANES)]
                    act = [lambda n, l=l: te.wait_ge(act_sem[l], lay["act"][l].at(i, n)) for l in range(LANES)]
                    for l in range(LANES):
                        dve[l]("nb")
                        nc.tensor.transpose(ps_a[l][:, 0:128], moe[l]["nrm"], ident[:]).then_inc(pe_sem[l], 1)
                    for l in range(LANES):
                        act[l]("nT")
                        nc.tensor.matmul(ps_a[l][:, 128:128 + EXPERTS], moe[l]["nT"], router, start=True, stop=True).then_inc(pe_sem[l], 1)
                        nc.tensor.matmul(ps_b[l][:], moe[l]["nT"], shared_gu, start=True, stop=True).then_inc(pe_sem[l], 1)
                    for l in range(LANES):
                        dve[l]("sh")
                        for e in range(EXPERTS):
                            mm = nc.tensor.transpose(ps_s[l][:, e * 128:e * 128 + 128], prob[l][:, 2 * e:2 * e + 2, :], ident[:])
                        mm.then_inc(pe_sem[l], 1)
                    for l in range(LANES):
                        act[l]("xwT")
                        for e in range(EXPERTS):
                            mm = nc.tensor.matmul(ps_a[l][:], probT[l][:, e, :], gate_up[:, e, :], start=(e == 0), stop=(e == EXPERTS - 1))
                        mm.then_inc(pe_sem[l], 1)
                    for l in range(LANES):
                        dve[l]("h")
                        for c in range(4):
                            mm = nc.tensor.transpose(ps_b[l][:, c * 128:c * 128 + 128], moe[l]["h"][:, c * 128:c * 128 + 128], ident[:])
                        mm.then_inc(pe_sem[l], 1)
                    for l in range(LANES):
                        act[l]("hT")
                        for c in range(2):
                            mm = nc.tensor.matmul(ps_a[l][:, 0:128], moe[l]["hT"][:, c * 128:c * 128 + 128], shared_dn[:, c, :], start=(c == 0), stop=(c == 1))
                        mm.then_inc(pe_sem[l], 1)
                    for l in range(LANES):
                        dve[l]("acc2")
                        for half_ in range(2):
                            for c in range(2):
                                mm = nc.tensor.matmul(ps_s[l][:, half_ * 512:half_ * 512 + 512], moe[l]["hT"][:, 256 + c * 128:256 + c * 128 + 128],
                                                      down0[:, c, half_ * 512:half_ * 512 + 512], start=(c == 0), stop=(c == 1))
                        mm.then_inc(pe_sem[l], 1)
            if STOP >= 3:
                attention(1)

            def turn(columns, n):
                te.wait_ge(to_pe, n + 1)
                nc.tensor.transpose(ps_a[0][0:columns, 0:128], gcol[:, 0:columns], ident[:]).then_inc(from_pe, 1)
                te.wait_ge(to_pe, n + 2)
                nc.tensor.matmul(ps_b[0][:, 0:columns], ones[0:columns, :], gdiag[0:columns, 0:columns], start=True, stop=True).then_inc(from_pe, 1)

            if STOP >= 4:
                turn(4, 0)
                te.wait_ge(to_pe, 3)
                lay = layers["ffn1a"]
                with nc.tensor.Fori(0, QROUNDS) as i:
                    for l in range(WIDE):
                        te.wait_ge(dve_sem[l], lay["dve"][l].at(i, "xc"))
                        for k in range(GROUP):
                            mm = nc.tensor.transpose(wide_a[l][:, k * 128:k * 128 + 128], prob[l][:, 2 * k:2 * k + 2, :], ident[:])
                        mm.then_inc(pe_sem[l], 1)
                    for l in range(WIDE):
                        te.wait_ge(dve_sem[l], lay["dve"][l].at(i, "xT"))
                        for c, bank in enumerate((ps_s[l][:, 0:512], ps_s[l][:, 512:1024], wide_b[l][:], wide_a[l][:])):
                            nc.tensor.matmul(bank, w_q[:, 0, c * 128:c * 128 + 128], xqT[l], start=True, stop=True).then_inc(pe_sem[l], 1)
                turn(2, 3)
                lay = layers["ffn1b"]
                with nc.tensor.Fori(0, QROUNDS) as i:
                    for l in range(WIDE):
                        te.wait_ge(dve_sem[l], lay["dve"][l].at(i, "hb"))
                        for k in range(GROUP):
                            for c in range(4):
                                mm = nc.tensor.matmul(wide_a[l][:, k * 128:k * 128 + 128], hq[l][:, c * 512 + k * 128:c * 512 + k * 128 + 128],
                                                      w_q[:, 1, c * 128:c * 128 + 128], start=(c == 0), stop=(c == 3))
                        mm.then_inc(pe_sem[l], 1)
            if STOP >= 5:
                te.wait_ge(loaded["late"], 16 * len(LATE))
                lay = layers["freq"]
                with nc.tensor.Fori(0, ROUNDS) as i:
                    dve = [lambda n, l=l: te.wait_ge(dve_sem[l], lay["dve"][l].at(i, n)) for l in range(LANES)]
                    act = [lambda n, l=l: te.wait_ge(act_sem[l], lay["act"][l].at(i, n)) for l in range(LANES)]

                    def units(bank, l):
                        for r_ in range(4):
                            mm = nc.tensor.matmul(bank[:, 0:128], f_unit[:, r_, :], fl[l]["p1"][:, r_ * 128:r_ * 128 + 128], start=(r_ == 0), stop=(r_ == 3))
                        mm.then_inc(pe_sem[l], 1)

                    for l in range(LANES):
                        dve[l]("xs")
                        nc.tensor.matmul(ps_a[l][:, 0:128], xn[l][:], dft, start=True, stop=True)
                        te.wait_ge(ctx_in[l], i * 16 + (lay["ctx"] + 16))
                        nc.tensor.matmul(ps_a[l][:, 128:256], cx[l][:], dft, start=True, stop=True).then_inc(pe_sem[l], 1)
                    for l in range(LANES):
                        act[l]("cf")
                        nc.tensor.matmul(ps_a[l][:, 0:128], f_wq, xcT[l][:, 0, :], start=True, stop=True).then_inc(pe_sem[l], 1)
                        for r_ in range(4):
                            mm = nc.tensor.matmul(ps_b[l][:, r_ * 128:r_ * 128 + 128], f_wk[:, r_, :], xcT[l][:, 1, :], start=True, stop=True)
                        mm.then_inc(pe_sem[l], 1)
                    for l in range(LANES):
                        dve[l]("q")
                        for r_ in range(4):
                            mm = nc.tensor.matmul(ps_a[l][:, r_ * 128:r_ * 128 + 128], f_wv[:, r_, :], xcT[l][:, 1, :], start=True, stop=True)
                        mm.then_inc(pe_sem[l], 1)
                    for l in range(LANES):
                        dve[l]("pz")
                        units(ps_b[l], l)
                    for l in range(LANES):
                        dve[l]("rz")
                        units(ps_b[l], l)
                    for l in range(LANES):
                        act[l]("g")
                        nc.tensor.transpose(ps_a[l][:, 0:128], fl[l]["g"], ident[:]).then_inc(pe_sem[l], 1)
                    for l in range(LANES):
                        act[l]("gT")
                        nc.tensor.matmul(ps_b[l][:, 0:128], idft, fl[l]["gT"], start=True, stop=True).then_inc(pe_sem[l], 1)
            if STOP >= 6:
                te.wait_ge(to_pe, 6)
                nc.tensor.transpose(ps_a[0][:, 0:128], r_t, ident[:])
                nc.tensor.matmul(ps_a[0][:, 128:256], ones[:], r_diag, start=True, stop=True).then_inc(from_pe, 1)
                te.wait_ge(to_pe, 7)
                lay = layers["ffn2"]
                with nc.tensor.Fori(0, QROUNDS) as i:
                    for l in range(WIDE):
                        te.wait_ge(dve_sem[l], lay["dve"][l].at(i, "yc"))
                        for k in range(GROUP):
                            mm = nc.tensor.transpose(wide_a[l][:, k * 128:k * 128 + 128], q8[l]["y"][:, k * 128:k * 128 + 128], ident[:])
                        mm.then_inc(pe_sem[l], 1)
                    for l in range(WIDE):
                        te.wait_ge(dve_sem[l], lay["dve"][l].at(i, "yT"))
                        for k in range(GROUP):
                            mm = nc.tensor.matmul(wide_b[l][:, k * 128:k * 128 + 128], q8[l]["yT"][:, k * 128:k * 128 + 128], r_q, start=True, stop=True)
                        mm.then_inc(pe_sem[l], 1)
            if STOP >= 7:
                attention(3)
            if STOP >= 8:
                te.wait_ge(to_pe, 8)
                gw = g_w[:, 0:2 * FFN3].rearrange("p (k c n) -> p k c n", k=2, c=3)
                dw = g_w[:, 2 * FFN3:3 * FFN3].rearrange("p (c n) -> p c n", c=3)
                lay = layers["ffn3"]
                with nc.tensor.Fori(0, TILES // 2 // WIDE) as i:
                    dve = [lambda n, l=l: te.wait_ge(dve_sem[l], lay["dve"][l].at(i, n)) for l in range(WIDE)]
                    act = [lambda n, l=l: te.wait_ge(act_sem[l], lay["act"][l].at(i, n)) for l in range(WIDE)]
                    for l in range(WIDE):
                        dve[l]("xn")
                        for k in range(2):
                            mm = nc.tensor.transpose(wide_b[l][:, k * 128:k * 128 + 128], ff[l]["xn"][:, k * 128:k * 128 + 128], ident[:])
                        mm.then_inc(pe_sem[l], 1)
                    for l in range(WIDE):
                        act[l]("xnT")
                        for c, bank in enumerate((ps_s[l][:, 0:512], ps_s[l][:, 512:1024], wide_a[l][:])):
                            for k in range(2):
                                mm = nc.tensor.matmul(bank[:, k * 256:k * 256 + 256], gw[:, k, c, :], ff[l]["xnT"], start=True, stop=True)
                            if c:
                                mm.then_inc(pe_sem[l], 1)
                    for l in range(WIDE):
                        dve[l]("h1")
                        for k in range(2):
                            for c in range(3):
                                mm = nc.tensor.matmul(wide_b[l][:, k * 128:k * 128 + 128], ff[l]["hT"][:, c * 256 + k * 128:c * 256 + k * 128 + 128],
                                                      dw[:, c, :], start=(c == 0), stop=(c == 2))
                        mm.then_inc(pe_sem[l], 1)

        @block.vector
        def _(dve):
            count = [0]

            def step(ins):
                count[0] += 1
                ins.then_inc(dve_chain, 1)
                dve.wait_ge(dve_chain, count[0])
            TT, TS, STT = nc.vector.tensor_tensor, nc.vector.tensor_scalar, nc.vector.scalar_tensor_tensor

            def moments():
                me, mo, ve, vo = (stats[:, :, k] for k in (1, 4, 2, 5))
                step(TT(agg[:, 0], me, mo, ALU.add))
                step(TS(mean[:], agg[:, 0], 0.5, None, ALU.mult))
                step(TT(agg[:, 1], me, mo, ALU.subtract))
                step(TT(agg[:, 2], agg[:, 1], agg[:, 1], ALU.mult))
                step(TT(agg[:, 0], ve, vo, ALU.add))
                step(TS(agg[:, 3], agg[:, 0], 1.0 / P, EPS, ALU.mult, ALU.add))
                STT(vpe[:], agg[:, 2], 0.25, agg[:, 3], ALU.mult, ALU.add).then_inc(vpe_ready, 1)

            def finished(key):
                for l in range(layers[key]["lanes"]):
                    dve.wait_ge(dve_sem[l], layers[key]["dve"][l].end(layers[key]["rounds"]))

            dve.wait_ge(loaded["x"], 16 * 4)
            with nc.vector.Fori(0, TILES) as t:
                nc.vector.bn_stats(stats[:, t, :], x[:, t, :]).then_inc(x_stats, 1)
            dve.wait_ge(x_stats, TILES)
            moments()

            def attention(L, n_rstd):
                lay, w = layers[f"att{L}"], att[L]
                dve.wait_ge(loaded["const"], 16 * 5)
                dve.wait_ge(filled, LATE_FILLS if L == 3 else FILLS)
                dve.wait_ge(loaded[f"att{L}"], 16 * 8)
                dve.wait_ge(rstd_ready, n_rstd)
                bv = w["bv"].rearrange("p (h d) -> p h d", d=HD)
                with nc.vector.Fori(0, ROUNDS) as i:
                    pe = [lambda n, l=l: dve.wait_ge(pe_sem[l], lay["pe"][l].at(i, n)) for l in range(LANES)]
                    own = [lambda n, l=l: dve.wait_ge(dve_sem[l], lay["dve"][l].at(i, n)) for l in range(LANES)]
                    for l in range(LANES):
                        t = i * LANES + l
                        nc.vector.tensor_scalar(xn[l][:], x[:, t, :], mean[:, bass.ds(t, 1)], rstd[:, bass.ds(t, 1)], ALU.subtract, ALU.mult).then_inc(dve_sem[l], 1)
                    for l in range(LANES):
                        pe[l]("proj")
                        for b in range(2):
                            q = nc.vector.scalar_tensor_tensor(qx[l][:, b], ps_b[l][:, b * 64:b * 64 + 64].unsqueeze(1).to_broadcast([P, 4, SEQ]), w["bq"],
                                                               head_mask[:].unsqueeze(2).to_broadcast([P, 4, SEQ]), ALU.add, ALU.mult)
                        q.then_inc(dve_sem[l], 1)
                        for b in range(2):
                            r = slice(64 * b, 64 * b + 64)
                            v = nc.vector.tensor_tensor(vbd[l][r, :, b, 0:8], ps_b[l][r, 256:384].rearrange("p (h d) -> p h d", d=HD), bv[r], ALU.add)
                        v.then_inc(dve_sem[l], 1)
                        if L == 0:
                            t = i * LANES + l
                            nc.vector.scalar_tensor_tensor(am[l], key_mask[:, bass.ds(t * P, P)], 1.0, causal[:], ALU.subtract, ALU.min).then_inc(dve_sem[l], 1)
                    for l in range(LANES):
                        pe[l]("s")
                        s = ps_s[l][:].rearrange("p (g k) -> p g k", k=SEQ)
                        if L == 0:
                            own[l]("am")
                            nc.vector.scalar_tensor_tensor(prob[l][:].rearrange("p (c b) k -> p c (b k)", b=2), am[l].unsqueeze(1).to_broadcast([P, 8, P]), MASKED,
                                                           ps_s[l][:].rearrange("p (c k) -> p c k", k=P), ALU.mult, ALU.add).then_inc(dve_sem[l], 1)
                            s = prob[l][:]
                            own[l]("masked")
                        nc.vector.tensor_reduce(mx[l][:], s, AX.X, ALU.max).then_inc(dve_sem[l], 1)
                        own[l]("mx")
                        nc.vector.tensor_tensor(prob[l][:], s, mx[l][:].unsqueeze(2).to_broadcast([P, 16, SEQ]), ALU.subtract).then_inc(dve_sem[l], 1)
                        if L == 0:
                            nc.vector.tensor_scalar(fx[l][:], mx[l][:], -MASKED / 2, half_pad[:], ALU.is_lt, ALU.mult).then_inc(dve_sem[l], 1)
                    for l in range(LANES):
                        pe[l]("pv")
                        pv = ps_a[l][:, 0:288].rearrange("p (c j b e) -> p c j b e", c=8, j=2, b=2)
                        if L == 0:
                            own[l]("fx")
                            nc.vector.tensor_tensor(rc[l][:], pv[:, :, 0, :, 8], fx[l][:].rearrange("p (c b) -> p c b", b=2), ALU.add).then_inc(dve_sem[l], 1)
                            own[l]("fs")
                            nc.vector.reciprocal(rc[l][:], rc[l][:]).then_inc(dve_sem[l], 1)
                        else:
                            nc.vector.reciprocal(rc[l][:], pv[:, :, 0, :, 8]).then_inc(dve_sem[l], 1)
                        own[l]("rc")
                        for j in range(2):
                            r = slice(64 * j, 64 * j + 64)
                            oo = nc.vector.tensor_tensor(o[l][r].rearrange("p b c d -> p c b d"), pv[r, :, j, :, 0:8],
                                                         rc[l][r].unsqueeze(3).to_broadcast([64, 8, 2, 8]), ALU.mult)
                        oo.then_inc(dve_sem[l], 1)
                    for l in range(LANES):
                        t = i * LANES + l
                        pe[l]("y")
                        nc.vector.tensor_tensor(x[:, t, :], x[:, t, :], ps_a[l][:, 0:128], ALU.add).then_inc(dve_sem[l], 1)
                        own[l]("fin")
                        nc.vector.nop(nofuse=True)
                        nc.vector.bn_stats(stats[:, t, :], x[:, t, :]).then_inc(dve_sem[l], 1)
            attention(0, 1)

            if STOP >= 2:
                finished("att0")
                moments()
                dve.wait_ge(loaded["ffn0"], 16 * 8)
                dve.wait_ge(rstd_ready, 3)
                lay = layers["ffn0"]
                with nc.vector.Fori(0, ROUNDS) as i:
                    pe = [lambda n, l=l: dve.wait_ge(pe_sem[l], lay["pe"][l].at(i, n)) for l in range(LANES)]
                    act = [lambda n, l=l: dve.wait_ge(act_sem[l], lay["act"][l].at(i, n)) for l in range(LANES)]
                    own = [lambda n, l=l: dve.wait_ge(dve_sem[l], lay["dve"][l].at(i, n)) for l in range(LANES)]
                    for l in range(LANES):
                        t, m = i * LANES + l, moe[l]
                        TS(xn[l][:], x[:, t, :], mean[:, bass.ds(t, 1)], rstd[:, bass.ds(t, 1)], ALU.subtract, ALU.mult).then_inc(dve_sem[l], 1)
                        TS(m["nrm"], x[:, t, :], mean[:, bass.ds(t, 1)], rstd2[:, bass.ds(t, 1)], ALU.subtract, ALU.mult).then_inc(dve_sem[l], 1)
                    for l in range(LANES):
                        m = moe[l]
                        own[l]("nrm")
                        TT(m["nrm"], m["nrm"], ln_w, ALU.mult).then_inc(dve_sem[l], 1)
                        own[l]("nw")
                        TT(m["nrm"], m["nrm"], ln_b, ALU.add).then_inc(dve_sem[l], 1)
                    for l in range(LANES):
                        m = moe[l]
                        pe[l]("lg")
                        lg = ps_a[l][:, 128:128 + EXPERTS]
                        nc.vector.tensor_reduce(m["mx"], lg, AX.X, ALU.max).then_inc(dve_sem[l], 1)
                        own[l]("mx")
                        STT(m["eq"], lg, m["mx"], rank, ALU.is_equal, ALU.mult).then_inc(dve_sem[l], 1)
                        own[l]("eq")
                        nc.vector.tensor_reduce(m["pick"], m["eq"], AX.X, ALU.max).then_inc(dve_sem[l], 1)
                        own[l]("pick")
                        TS(m["one"], m["eq"], m["pick"], None, ALU.is_equal).then_inc(dve_sem[l], 1)
                        act[l]("tanh")
                        TS(m["th"], m["th"], 0.5, 0.5, ALU.mult, ALU.add).then_inc(dve_sem[l], 1)
                        own[l]("th")
                        TS(m["w"], m["one"], m["th"], None, ALU.mult).then_inc(dve_sem[l], 1)
                        own[l]("w")
                        TT(prob[l][:].rearrange("p (e j) k -> p e (j k)", j=2), m["nrm"].unsqueeze(1).to_broadcast([P, EXPERTS, P]),
                           m["w"].unsqueeze(2).to_broadcast([P, EXPERTS, P]), ALU.mult).then_inc(dve_sem[l], 1)
                    for l in range(LANES):
                        m = moe[l]
                        act[l]("ssilu")
                        TT(m["h"][:, 0:FFN0], m["silu"][:, 0:FFN0], ps_b[l][:, FFN0:2 * FFN0], ALU.mult).then_inc(dve_sem[l], 1)
                    for l in range(LANES):
                        m = moe[l]
                        act[l]("silu")
                        TT(m["h"][:, FFN0:2 * FFN0], m["silu"][:, FFN0:2 * FFN0], ps_a[l][:, FFN0:2 * FFN0], ALU.mult).then_inc(dve_sem[l], 1)
                        t = i * LANES + l
                        TT(m["acc"], x[:, t, :], xn[l][:], ALU.add).then_inc(dve_sem[l], 1)
                    for l in range(LANES):
                        t, m = i * LANES + l, moe[l]
                        m = moe[l]
                        pe[l]("sdn")
                        own[l]("acc")
                        TT(m["acc"], m["acc"], ps_a[l][:, 0:128], ALU.add).then_inc(dve_sem[l], 1)
                    for l in range(LANES):
                        t, m = i * LANES + l, moe[l]
                        pe[l]("dn")
                        TT(prob[l][:].rearrange("p (e j) k -> p e (j k)", j=2), ps_s[l][:].rearrange("p (e d) -> p e d", e=EXPERTS),
                           m["one"].unsqueeze(2).to_broadcast([P, EXPERTS, P]), ALU.mult).then_inc(dve_sem[l], 1)
                        own[l]("sel")
                        nc.vector.tensor_reduce(m["red"], prob[l][:].rearrange("p (e j) k -> p (j k) e", j=2), AX.X, ALU.add).then_inc(dve_sem[l], 1)
                        own[l]("red")
                        TT(x[:, t, :], m["acc"], m["red"], ALU.add).then_inc(dve_sem[l], 1)
                    for l in range(LANES):
                        t = i * LANES + l
                        own[l]("fin")
                        nc.vector.nop(nofuse=True)
                        nc.vector.bn_stats(stats[:, t, :], x[:, t, :]).then_inc(dve_sem[l], 1)
            if STOP >= 3:
                finished("ffn0")
                moments()
                attention(1, 4)

            def everywhere(columns, n):
                dve.wait_ge(from_pe, n + 1)
                step(nc.vector.tensor_reduce(grow[0:columns], ps_a[0][0:columns, 0:128], AX.X, ALU.max))
                TS(gdiag[0:columns, 0:columns], ident[0:columns, 0:columns], grow[0:columns], None, ALU.mult).then_inc(to_pe, 1)
                dve.wait_ge(from_pe, n + 2)
                step(nc.vector.tensor_copy(gall[:, 0:columns], ps_b[0][:, 0:columns]))

            def affine():
                step(TT(qs[:, 0:1], gall[:, 0:1], gall[:, 1:2], ALU.add))
                step(TS(qs[:, 0:1], qs[:, 0:1], 1.0 / 255.0, 1e-8, ALU.mult, ALU.max))
                step(nc.vector.reciprocal(qs[:, 1:2], qs[:, 0:1]))
                step(TS(qs[:, 2:3], gall[:, 1:2], qs[:, 1:2], MAGIC, ALU.mult, ALU.add))
                step(TS(qs[:, 2:3], qs[:, 2:3], MAGIC, 128.0, ALU.subtract, ALU.subtract))
                step(TS(qs[:, 2:3], qs[:, 2:3], -128.0, 127.0, ALU.max, ALU.min))
                step(TS(qs[:, 3:4], qs[:, 2:3], -1.0, MAGIC - 128.0, ALU.mult, ALU.add))
                step(TS(qs[:, 4:5], qs[:, 2:3], -1.0, MAGIC + 127.0, ALU.mult, ALU.add))

            if STOP >= 4:
                finished("att1")
                moments()
                dve.wait_ge(loaded["ffn1"], 16 * 3)
                step(nc.vector.tensor_reduce(tmx[:, 0], x[:], AX.X, ALU.max))
                step(nc.vector.tensor_reduce(tmx[:, 1], x[:], AX.X, ALU.min))
                dve.wait_ge(rstd_ready, 5)
                for k in range(2):
                    step(TT(tmx[:, k], tmx[:, k], mean[:], ALU.subtract))
                    step(TT(tmx[:, k], tmx[:, k], rstd[:], ALU.mult))
                step(nc.vector.tensor_reduce(gcol[:, 0:1], tmx[:, 0], AX.X, ALU.max))
                step(nc.vector.tensor_reduce(gcol[:, 1:2], tmx[:, 1], AX.X, ALU.min))
                step(TS(gcol[:, 1:2], gcol[:, 1:2], -1.0, None, ALU.mult))
                step(nc.vector.tensor_reduce(gcol[:, 2:3], w_raw[:, 0], AX.X, ALU.max, apply_absolute_value=True))
                nc.vector.tensor_reduce(gcol[:, 3:4], w_raw[:, 1], AX.X, ALU.max, apply_absolute_value=True).then_inc(to_pe, 1)
                everywhere(4, 0)
                affine()
                step(TS(qs[:, 5:7], gall[:, 2:4], 1.0 / 127.0, 1e-8, ALU.mult, ALU.max))
                step(nc.vector.reciprocal(gall[:, 2:4], qs[:, 5:7]))
                step(TT(qs[:, 8:9], qs[:, 0:1], qs[:, 5:6], ALU.mult))
                for k in range(2):
                    step(TS(w_rnd, w_raw[:, k], gall[:, 2 + k:3 + k], MAGIC, ALU.mult, ALU.add))
                    step(TS(w_rnd, w_rnd, MAGIC - 127.0, MAGIC + 127.0, ALU.max, ALU.min))
                    wq = TS(w_q[:, k], w_rnd, MAGIC, None, ALU.subtract)
                    if k == 0:
                        step(wq)
                wq.then_inc(to_pe, 1)
                lay = layers["ffn1a"]
                with nc.vector.Fori(0, QROUNDS) as i:
                    own = [lambda n, l=l: dve.wait_ge(dve_sem[l], lay["dve"][l].at(i, n)) for l in range(WIDE)]
                    view = [prob[l][:].rearrange("p (k j) d -> p k (j d)", j=2)[:, 0:GROUP] for l in range(WIDE)]
                    for l in range(WIDE):
                        ts = bass.ds((i * WIDE + l) * GROUP, GROUP)
                        TT(view[l], x[:, ts, :], mean[:, ts].unsqueeze(2).to_broadcast([P, GROUP, P]), ALU.subtract).then_inc(dve_sem[l], 1)
                    for l in range(WIDE):
                        ts = bass.ds((i * WIDE + l) * GROUP, GROUP)
                        own[l]("xs")
                        TT(view[l], view[l], rstd[:, ts].unsqueeze(2).to_broadcast([P, GROUP, P]), ALU.mult).then_inc(dve_sem[l], 1)
                    for l in range(WIDE):
                        own[l]("xn")
                        TS(view[l], view[l], qs[:, 1:2], MAGIC, ALU.mult, ALU.add).then_inc(dve_sem[l], 1)
                    for l in range(WIDE):
                        own[l]("xr")
                        TS(view[l], view[l], qs[:, 3:4], qs[:, 4:5], ALU.max, ALU.min).then_inc(dve_sem[l], 1)
                    for l in range(WIDE):
                        dve.wait_ge(pe_sem[l], lay["pe"][l].at(i, "xT"))
                        TS(xqT[l], wide_a[l][:], MAGIC, None, ALU.subtract).then_inc(dve_sem[l], 1)
                    for l in range(WIDE):
                        g = i * WIDE + l
                        dve.wait_ge(act_sem[l], lay["act"][l].at(i, "g3"))
                        nc.vector.tensor_reduce(hmm[:, 0, bass.ds(g, 1)], hidden[:, g, :], AX.X, ALU.max).then_inc(dve_sem[l], 1)
                        nc.vector.tensor_reduce(hmm[:, 1, bass.ds(g, 1)], hidden[:, g, :], AX.X, ALU.min).then_inc(dve_sem[l], 1)
                finished("ffn1a")
                step(nc.vector.tensor_reduce(gcol[:, 0:1], hmm[:, 0], AX.X, ALU.max))
                step(nc.vector.tensor_reduce(gcol[:, 1:2], hmm[:, 1], AX.X, ALU.min))
                TS(gcol[:, 1:2], gcol[:, 1:2], -1.0, None, ALU.mult).then_inc(to_pe, 1)
                everywhere(2, 2)
                affine()
                TT(qs[:, 9:10], qs[:, 0:1], qs[:, 6:7], ALU.mult).then_inc(hidden_scaled, 1)
                dve.wait_ge(hidden_scaled, 1)
                lay = layers["ffn1b"]
                with nc.vector.Fori(0, QROUNDS) as i:
                    own = [lambda n, l=l: dve.wait_ge(dve_sem[l], lay["dve"][l].at(i, n)) for l in range(WIDE)]
                    for l in range(WIDE):
                        g = i * WIDE + l
                        dve.wait_ge(act_sem[l], lay["act"][l].at(i, "hr"))
                        TS(hidden[:, g, :], hidden[:, g, :], qs[:, 3:4], qs[:, 4:5], ALU.max, ALU.min).then_inc(dve_sem[l], 1)
                    for l in range(WIDE):
                        g = i * WIDE + l
                        own[l]("hc")
                        TS(hq[l], hidden[:, g, :], MAGIC, None, ALU.subtract).then_inc(dve_sem[l], 1)
                    for l in range(WIDE):
                        y = probT[l][:, 0:GROUP]
                        ts = bass.ds((i * WIDE + l) * GROUP, GROUP)
                        dve.wait_ge(pe_sem[l], lay["pe"][l].at(i, "y"))
                        STT(y, wide_a[l][:].rearrange("p (k d) -> p k d", k=GROUP), qs[:, 9:10], b2[:].unsqueeze(1).to_broadcast([P, GROUP, P]), ALU.mult, ALU.add).then_inc(dve_sem[l], 1)
                        own[l]("yb")
                        TT(x[:, ts, :], x[:, ts, :], y, ALU.add).then_inc(dve_sem[l], 1)
                    for l in range(WIDE):
                        own[l]("fin")
                        nc.vector.nop(nofuse=True)
                        for k in range(GROUP):
                            t = (i * WIDE + l) * GROUP + k
                            st = nc.vector.bn_stats(stats[:, t, :], x[:, t, :])
                        st.then_inc(dve_sem[l], 1)

            if STOP >= 5:
                finished("ffn1b")
                moments()
                dve.wait_ge(loaded["late"], 16 * len(LATE))
                step(nc.vector.memset(dc_q, 0.0))
                for b in range(2):
                    step(TS(dc_q[:, b * SEQ:b * SEQ + 1], f_bq, float(SEQ), None, ALU.mult))
                    step(TS(dc_kv[:, 0, :, b], f_bk, float(SEQ), None, ALU.mult))
                    step(TS(dc_kv[:, 1, :, b], f_bv, float(SEQ), None, ALU.mult))
                dve.wait_ge(eneg_ready, 1)
                s_, u_, v_ = chaos[:, 0], chaos[:, 1], chaos[:, 2]
                step(TS(u_, eneg, 1.0, None, ALU.add))
                step(nc.vector.reciprocal(s_, u_))
                for _ in range(LOGISTIC_STEPS):
                    step(TS(u_, s_, -1.0, 1.0, ALU.mult, ALU.add))
                    step(STT(v_, s_, LOGISTIC, u_, ALU.mult, ALU.mult))
                    s_, v_ = v_, s_
                step(TS(u_, s_, 0.5, 0.1, ALU.subtract, ALU.mult))
                step(TS(u_, u_, 1.0, wave, ALU.add, ALU.mult))
                step(TT(fac, u_, rstd[:], ALU.mult))
                lay = layers["freq"]
                re, im, mid = slice(0, FREQ), slice(FREQ, SEQ), slice(1, FREQ - 1)
                with nc.vector.Fori(0, ROUNDS) as i:
                    pe = [lambda n, l=l: dve.wait_ge(pe_sem[l], lay["pe"][l].at(i, n)) for l in range(LANES)]
                    own = [lambda n, l=l: dve.wait_ge(dve_sem[l], lay["dve"][l].at(i, n)) for l in range(LANES)]

                    def products(l, one, four, first, done):
                        a_ = one.rearrange("p (b m) -> p b m", b=2)
                        b_ = four.rearrange("p (r b m) -> p r b m", r=4, b=2)
                        half_spectrum = [P, 4, 2, FREQ - 2]
                        p1 = fl[l]["p1"].rearrange("p (r b m) -> p r b m", r=4, b=2)
                        p2 = fl[l]["p2"].rearrange("p (r b m) -> p r b m", r=4, b=2)
                        p3 = fl[l]["p3"].rearrange("p (r b m) -> p r b m", r=4, b=2)
                        TT(fl[l]["p1"].rearrange("p (r m) -> p r m", r=4), one.unsqueeze(1).to_broadcast([P, 4, P]), four.rearrange("p (r m) -> p r m", r=4), ALU.mult).then_inc(dve_sem[l], 1)
                        TT(p2, a_[:, :, mid].unsqueeze(1).to_broadcast(half_spectrum), b_[:, :, :, im], ALU.mult)
                        TT(p3, a_[:, :, im].unsqueeze(1).to_broadcast(half_spectrum), b_[:, :, :, mid], ALU.mult).then_inc(dve_sem[l], 1)
                        own[l](first)
                        TT(p1[:, :, :, mid], p1[:, :, :, mid], p1[:, :, :, im], ALU.subtract).then_inc(dve_sem[l], 1)
                        own[l](done)
                        TT(p1[:, :, :, im], p2, p3, ALU.add).then_inc(dve_sem[l], 1)
                    for l in range(LANES):
                        t = i * LANES + l
                        TS(xn[l][:], x[:, t, :], mean[:, bass.ds(t, 1)], fac[:, bass.ds(t, 1)], ALU.subtract, ALU.mult).then_inc(dve_sem[l], 1)
                    for l in range(LANES):
                        pe[l]("pq")
                        TT(fl[l]["qh"], ps_a[l][:, 0:128], dc_q, ALU.add).then_inc(dve_sem[l], 1)
                        pe[l]("pk")
                        dc = ps_b[l].rearrange("p (r b m) -> p r b m", r=4, b=2)[:, :, :, 0]
                        TT(dc, dc, dc_kv[:, 0], ALU.add).then_inc(dve_sem[l], 1)
                        own[l]("kb")
                        products(l, fl[l]["qh"], ps_b[l], "p", "ps")
                        pe[l]("pv")
                        dc = ps_a[l].rearrange("p (r b m) -> p r b m", r=4, b=2)[:, :, :, 0]
                        TT(dc, dc, dc_kv[:, 1], ALU.add).then_inc(dve_sem[l], 1)
                    for l in range(LANES):
                        own[l]("vb")
                        dve.wait_ge(act_sem[l], lay["act"][l].at(i, "qk"))
                        products(l, fl[l]["qk"], ps_a[l], "r", "rs")
                    for l in range(LANES):
                        t = i * LANES + l
                        pe[l]("y")
                        TT(x[:, t, :], x[:, t, :], ps_b[l][:, 0:128], ALU.add).then_inc(dve_sem[l], 1)
                    for l in range(LANES):
                        t = i * LANES + l
                        own[l]("fin")
                        nc.vector.nop(nofuse=True)
                        nc.vector.bn_stats(stats[:, t, :], x[:, t, :]).then_inc(dve_sem[l], 1)

            if STOP >= 6:
                finished("freq")
                moments()
                step(nc.vector.tensor_reduce(r_scale[:, 0:1], r_raw, AX.X, ALU.max, apply_absolute_value=True))
                step(TS(r_scale[:, 0:1], r_scale[:, 0:1], 1e-12, 1.0 / 127.0, ALU.max, ALU.mult))
                step(nc.vector.reciprocal(r_scale[:, 1:2], r_scale[:, 0:1]))
                step(TS(r_t, r_raw, r_scale[:, 1:2], MAGIC, ALU.mult, ALU.add))
                step(TS(r_t, r_t, MAGIC - 127.0, MAGIC + 127.0, ALU.max, ALU.min))
                TS(r_diag, ident[:], r_scale[:, 0:1], None, ALU.mult).then_inc(to_pe, 1)
                dve.wait_ge(from_pe, 5)
                step(TS(r_q, ps_a[0][:, 0:128], MAGIC, None, ALU.subtract))
                nc.vector.tensor_copy(r_bc, ps_a[0][:, 128:256]).then_inc(to_pe, 1)
                dve.wait_ge(to_pe, 7)
                dve.wait_ge(rstd_ready, 7)
                lay = layers["ffn2"]
                with nc.vector.Fori(0, QROUNDS) as i:
                    own = [lambda n, l=l: dve.wait_ge(dve_sem[l], lay["dve"][l].at(i, n)) for l in range(WIDE)]
                    view = [q8[l]["y"].rearrange("p (k d) -> p k d", k=GROUP) for l in range(WIDE)]
                    wide = [P, GROUP, P]
                    for l in range(WIDE):
                        ts = bass.ds((i * WIDE + l) * GROUP, GROUP)
                        TT(view[l], x[:, ts, :], mean[:, ts].unsqueeze(2).to_broadcast(wide), ALU.subtract).then_inc(dve_sem[l], 1)
                    for l in range(WIDE):
                        ts = bass.ds((i * WIDE + l) * GROUP, GROUP)
                        own[l]("xs")
                        TT(view[l], view[l], rstd[:, ts].unsqueeze(2).to_broadcast(wide), ALU.mult).then_inc(dve_sem[l], 1)
                    for l in range(WIDE):
                        own[l]("xn")
                        nc.vector.tensor_reduce(q8[l]["amax"], view[l], AX.X, ALU.max, apply_absolute_value=True).then_inc(dve_sem[l], 1)
                    for l in range(WIDE):
                        own[l]("amax")
                        TS(q8[l]["ls"], q8[l]["amax"], 1e-12, 1.0 / 127.0, ALU.max, ALU.mult).then_inc(dve_sem[l], 1)
                        own[l]("ls")
                        nc.vector.tensor_copy(q8[l]["amax"], q8[l]["ls"]).then_inc(dve_sem[l], 1)
                        nc.vector.reciprocal(q8[l]["inv"], q8[l]["ls"]).then_inc(dve_sem[l], 1)
                    for l in range(WIDE):
                        own[l]("inv")
                        TT(view[l], view[l], q8[l]["inv"].unsqueeze(2).to_broadcast(wide), ALU.mult).then_inc(dve_sem[l], 1)
                    for l in range(WIDE):
                        own[l]("y")
                        TS(view[l], view[l], MAGIC, None, ALU.add).then_inc(dve_sem[l], 1)
                    for l in range(WIDE):
                        own[l]("yr")
                        TS(view[l], view[l], MAGIC - 127.0, MAGIC + 127.0, ALU.max, ALU.min).then_inc(dve_sem[l], 1)
                    for l in range(WIDE):
                        dve.wait_ge(pe_sem[l], lay["pe"][l].at(i, "yT"))
                        TS(q8[l]["yT"], wide_a[l][:], MAGIC, None, ALU.subtract).then_inc(dve_sem[l], 1)
                    for l in range(WIDE):
                        ts = bass.ds((i * WIDE + l) * GROUP, GROUP)
                        dve.wait_ge(pe_sem[l], lay["pe"][l].at(i, "mm"))
                        TT(view[l], wide_b[l][:].rearrange("p (k d) -> p k d", k=GROUP), r_bc.unsqueeze(1).to_broadcast(wide), ALU.mult).then_inc(dve_sem[l], 1)
                        own[l]("a")
                        TT(view[l], view[l], q8[l]["ls"].unsqueeze(2).to_broadcast(wide), ALU.mult).then_inc(dve_sem[l], 1)
                        own[l]("b")
                        TT(x[:, ts, :], x[:, ts, :], view[l], ALU.add).then_inc(dve_sem[l], 1)
                    for l in range(WIDE):
                        own[l]("fin")
                        nc.vector.nop(nofuse=True)
                        for k in range(GROUP):
                            t = (i * WIDE + l) * GROUP + k
                            st = nc.vector.bn_stats(stats[:, t, :], x[:, t, :])
                        st.then_inc(dve_sem[l], 1)
            if STOP >= 7:
                finished("ffn2")
                moments()
                attention(3, 8)

            if STOP >= 8:
                finished("att3")
                moments()
                TS(g_w, g_raw, 1.0 / 127.0, None, ALU.mult).then_inc(to_pe, 1)
                dve.wait_ge(rstd_ready, 9)
                lay = layers["ffn3"]
                with nc.vector.Fori(0, TILES // 2 // WIDE) as i:
                    for l in range(WIDE):
                        for k in range(2):
                            t = (i * WIDE + l) * 2 + k
                            n = TS(ff[l]["xn"][:, k * 128:k * 128 + 128], x[:, t, :], mean[:, bass.ds(t, 1)], rstd[:, bass.ds(t, 1)], ALU.subtract, ALU.mult)
                        n.then_inc(dve_sem[l], 1)
                    for l in range(WIDE):
                        dve.wait_ge(act_sem[l], lay["act"][l].at(i, "s0"))
                        TT(ff[l]["hT"][:, 0:512].rearrange("p (c t) -> p c t", c=2), ff[l]["silu"][:, 0:512].rearrange("p (c t) -> p c t", c=2),
                           ps_s[l][:].rearrange("p (c k t) -> p c k t", c=2, k=2)[:, :, 1, :], ALU.mult).then_inc(dve_sem[l], 1)
                        dve.wait_ge(act_sem[l], lay["act"][l].at(i, "s1"))
                        TT(ff[l]["hT"][:, 512:768], ff[l]["silu"][:, 512:768], wide_a[l][:, 256:512], ALU.mult).then_inc(dve_sem[l], 1)
                    for l in range(WIDE):
                        ts = bass.ds((i * WIDE + l) * 2, 2)
                        dve.wait_ge(pe_sem[l], lay["pe"][l].at(i, "y"))
                        TT(x[:, ts, :], x[:, ts, :], wide_b[l][:, 0:256].rearrange("p (k d) -> p k d", k=2), ALU.add).then_inc(dve_sem[l], 1)


def memory_scale():
    sigmoid = lambda v: np.float32(1) / (np.float32(1) + np.exp(-np.float32(v)))
    part_ = lambda v: np.float32(0.9 * 0.5) + np.float32(0.1) * sigmoid(v)
    return float(np.float32(0.4) * part_(0.7) + np.float32(0.3) * part_(0.8) + np.float32(0.3) * part_(0.6))


MEMORY_SCALE = memory_scale()


def spectral_constants():
    f8 = np.float64
    n, k = np.arange(SEQ), np.arange(FREQ)
    angle = 2 * np.pi * np.outer(n, k) / SEQ
    forward = np.concatenate([np.cos(angle), -np.sin(angle[:, 1:FREQ - 1])], axis=1)
    filt = np.exp(1j * 1.5 * np.arctan(np.log(np.arange(SEQ, dtype=f8) + 1e-10))) ** 3
    turned = np.exp(2j * np.pi * np.outer(k, n) / SEQ)
    both = filt[:FREQ].copy()
    both[1:FREQ - 1] += np.conj(filt[SEQ - k[1:FREQ - 1]])
    g = both[:, None] * turned / SEQ
    inverse = np.concatenate([g.real, -g.imag[1:FREQ - 1]], axis=0)
    twice = lambda m: np.kron(np.eye(2), m).astype(np.float32)
    sign = [[1, 1, 1, 1], [1, -1, 1, -1], [1, -1, -1, 1], [1, 1, -1, -1]]
    units = np.zeros((4, P, P), np.float32)
    for r in range(4):
        for i in range(4):
            j = (i + r) % 4
            for c in range(32):
                units[r, i * 32 + c, (i ^ j) * 32 + c] = sign[i][j]
    lam = np.arange(SEQ, dtype=np.float32) / SEQ
    alpha = np.clip(1.0 * (1.0 + 0.5 * (1.5 - 2.0) / 2.0), 0.1, 3.0)
    wave = np.sin(alpha * lam) * np.cos(-2.0 * lam + (2 * 1 + 1 - 2 * 1.5) * lam ** 2)
    return dict(c_dft=twice(forward), c_idft=twice(inverse), c_unit=np.ascontiguousarray(units.transpose(1, 0, 2)),
                c_wave=np.tile(1.0 + 0.1 * wave, 2).astype(np.float32).reshape(P, 1))



STRIPS = [0, 2, 1, 3]


def kernel(**inputs):
    import numpy as _np
    import concourse.bacc as _bacc
    from concourse import mybir as _mybir
    from concourse.bass_utils import run_bass_kernel_spmd as _run

    a = {k: _np.asarray(v) for k, v in inputs.items()}
    strip = lambda w: w.reshape(w.shape[0], 4, 32)[:, STRIPS].reshape(w.shape[0], 128)
    d = {"x": a["x"].reshape(-1, 128), "ctx_1024": a["ctx_1024"].reshape(-1, 128),
         "mask_BxS2_bf1": a["mask_BxS2_bf1"].view(_np.uint8).reshape(1, -1)}

    def attention(L, wq, wk, wv, wo, bq, bk, bv, bo):
        d.update({f"a{L}_wq": strip(wq), f"a{L}_wk": strip(wk), f"a{L}_wv": wv,
                  f"a{L}_wo": wo.reshape(8, 2, 8, 128).transpose(0, 2, 1, 3).reshape(64, 2, 128),
                  f"a{L}_bq": strip(bq[None]).reshape(128, 1), f"a{L}_bk": strip(bk[None]).reshape(128, 1),
                  f"a{L}_bv": bv.reshape(1, 128), f"a{L}_bo": bo.reshape(1, 128)})
    attention(0, a["L0_xattn_W_q"].T, a["L0_xattn_W_k"].T, a["L0_xattn_W_v"].T, a["L0_xattn_W_o"].T,
              a["L0_xattn_b_q"], a["L0_xattn_b_k"], a["L0_xattn_b_v"], a["L0_xattn_b_o"])
    for L in (1, 3):
        g = lambda n: a[f"L{L}_xattn_{n}"]
        attention(L, g("Wq"), g("Wkv")[:, :128], g("Wkv")[:, 128:], g("Wo"), g("bq"), g("bkv")[:128], g("bkv")[128:], g("bo"))

    f = lambda n: a[f"L0_ffn_{n}"]
    d["gate_up"] = _np.concatenate([f("gate_w"), f("up_w")], axis=2).transpose(1, 0, 2)
    d["down0"] = f("down_w").reshape(8, 2, 128, 128).transpose(2, 1, 0, 3).reshape(128, 2, 1024)
    d["shared_gu"] = _np.concatenate([f("sh_gate"), f("sh_up")], axis=1)
    d["shared_dn"] = f("sh_down").reshape(2, 128, 128).transpose(1, 0, 2)
    d["router"], d["ln_w"], d["ln_b"] = f("router_w"), f("ln_w").reshape(1, -1), f("ln_b").reshape(1, -1)
    d["w12"] = _np.stack([a["L1_ffn_W1"].T, a["L1_ffn_W2"].T.reshape(4, 128, 128).transpose(1, 0, 2).reshape(128, 512)], axis=1)
    d["b1"], d["b2"] = a["L1_ffn_b1"].reshape(4, 128).T, a["L1_ffn_b2"].reshape(1, -1)
    around = lambda w: _np.stack([_np.roll(w, -32 * r_, axis=-1) for r_ in range(4)], axis=1)
    h = lambda n: a[f"L2_xattn_{n}"]
    d["f_wq"], d["f_wk"], d["f_wv"] = h("Wq").T, around(h("Wk").T), around(h("Wv").T)
    d["f_bq"], d["f_bk"], d["f_bv"] = h("bq").reshape(128, 1), around(h("bk")[None])[0].T, around(h("bv")[None])[0].T
    d["r_raw"] = a["L2_ffn_rhs"].T
    m = lambda n: a[f"L3_ffn_{n}"]
    d["g_raw"] = _np.concatenate([m("w_gate").T, m("w_up").T, m("w_down").T.reshape(3, 128, 128).transpose(1, 0, 2).reshape(128, 384)], axis=1)

    r = _np.arange(128)
    d["c_ident"] = _np.eye(128, dtype=_np.float32)
    d["c_head_mask"] = ((r[:, None] % 32 // 8 == _np.arange(4)) * _np.float32(8 ** -0.5)).astype(_np.float32)
    d["c_causal"] = -(r[:, None] % 64 < r[None] % 64).astype(_np.float32)
    d["c_rank"] = (EXPERTS - _np.arange(EXPERTS, dtype=_np.float32)).reshape(1, -1)
    d.update(spectral_constants())
    d["c_half_pad"] = _np.where(r % 64 < 32, 32.0, 0.0).astype(_np.float32).reshape(128, 1)

    nc = _bacc.Bacc("TRN2", target_bir_lowering=False, num_devices=1)
    arrays, dram = {}, {}
    for n, v in d.items():
        v = _np.ascontiguousarray(v)
        arrays[f"in_{n}"] = v
        dram[n] = nc.dram_tensor(f"in_{n}", v.shape, _mybir.dt.from_np(v.dtype), kind="ExternalInput").ap()
    out = nc.dram_tensor("out", (8192, 128), F32, kind="ExternalOutput").ap()
    build_program(nc, dram, out)
    res = _run(nc, [arrays], core_ids=[0])
    return res.results[0]["out"].reshape(128, 64, 128)
```

```python
import math
from contextlib import ExitStack
import numpy as np
import concourse.bass as bass
from concourse import mybir

F32 = mybir.dt.float32
BF16 = mybir.dt.bfloat16
U8 = mybir.dt.uint8
I32 = mybir.dt.int32
ALU = mybir.AluOpType
ACT = mybir.ActivationFunctionType
AX = mybir.AxisListType

P = 128
TOKENS = 128 * 64
TILES = TOKENS // P
SEQ = 64
LANES = 4
ROUNDS = TILES // LANES
HEADS, HD = 16, 8
EPS = 1e-5
MASKED = 1e30
MAGIC = 1.5 * 2 ** 23
EXPERTS, FFN0, FFN1, FFN3 = 8, 256, 512, 384
SLOT_ROUNDS = -(-(TILES + EXPERTS - 1) // LANES)
SLOTS = SLOT_ROUNDS * LANES
GROUP = 4
WIDE = 2
FREQ = SEQ // 2 + 1
LOGISTIC, LOGISTIC_STEPS = 3.9, 10


class Steps:

    def __init__(self, sem, base, names, ahead, rounds):
        self.sem, self.base, self.names, self.ahead, self.rounds = sem, base, names, ahead, rounds

    def at(self, i, name):
        if name in self.ahead:
            if isinstance(i, int) and i == 0:
                return self.base + self.ahead.index(name) + 1
            round_before = len(self.names)
            return i * len(self.names) + (self.base + len(self.ahead) + self.names.index(name) + 1 - round_before)
        left_out = 0
        if isinstance(i, int) and i == self.rounds - 1:
            left_out = sum(n in self.ahead for n in self.names[:self.names.index(name)])
        return i * len(self.names) + (self.base + len(self.ahead) + self.names.index(name) + 1 - left_out)

    def end(self):
        return self.base + self.rounds * len(self.names)


def build_program(nc, dram, out, rows_in, rows_out):
    with ExitStack() as ctx:
        sb = lambda name, shape, dt=F32: ctx.enter_context(nc.sbuf_tensor(name, shape, dt))
        pb = lambda name, shape: ctx.enter_context(nc.psum_tensor(name, shape, F32))
        sem = lambda name: ctx.enter_context(nc.semaphore(name))

        x = sb("x", [P, TILES, P])
        stats = sb("stats", [P, TILES, 6])
        mean = sb("mean", [P, TILES])
        agg = sb("agg", [P, 4, TILES])
        rstd = sb("rstd", [P, TILES])
        vpe = sb("vpe", [P, TILES])
        root = sb("root", [P, TILES])
        ident = sb("ident", [P, P])

        head_mask = sb("head_mask", [P, HEADS // 2])
        causal = sb("causal", [P, SEQ])
        half_pad = sb("half_pad", [P, 1])

        area = sb("area", [P, TOKENS * FFN1 // P])
        where = [0]

        def part(width):
            where[0] += width
            return area[:, where[0] - width:where[0]]
        def attention_weights():
            return dict(wq=part(2 * P).rearrange("p (j n) -> p j n", j=2), wk=part(2 * P).rearrange("p (j n) -> p j n", j=2),
                        wv=part(P), wo=part(P), bq=part(2), bk=part(2), bv=part(P), bo=part(P))
        att = {0: attention_weights(), 1: attention_weights()}
        gate_up = part(EXPERTS * 2 * FFN0).rearrange("p (e n) -> p e n", e=EXPERTS)
        down0 = part(2 * EXPERTS * P).rearrange("p (c n) -> p c n", c=2)
        shared_gu = part(2 * FFN0)
        shared_dn = part(2 * P).rearrange("p (c n) -> p c n", c=2)
        router = part(EXPERTS)
        ln_w = part(1)
        ln_b = part(1)
        rank = part(EXPERTS)
        rstd2 = part(TILES)
        key_mask = part(TILES * SEQ // 4).bitcast(U8).rearrange("p (t k) -> p t k", k=SEQ)
        am = [part(SEQ // 2).bitcast(BF16) for _ in range(LANES)]
        minus_masked = part(P // 2).bitcast(BF16)
        w_raw = part(2 * FFN1).rearrange("p (k n) -> p k n", k=2)
        w_rnd = part(FFN1)
        xw = part(TILES * P).rearrange("p (t d) -> p t d", d=P)
        per_expert = lambda: part(TILES * EXPERTS).rearrange("p (t e) -> p t e", e=EXPERTS)
        logits, one, before, scan = per_expert(), per_expert(), per_expert(), [per_expert(), per_expert()]
        earlier = part(P)
        best, pick, score, slot = part(TILES), part(TILES), part(TILES), part(TILES)
        slot_i = part(TILES).bitcast(I32)
        first = part(EXPERTS + 1)
        used = part(EXPERTS)
        slot_tile = part(SLOTS)
        owner = part(SLOTS)
        owner_i = part(SLOTS).bitcast(I32)
        rstd_one = part(TILES)
        mean_rstd = part(TILES)
        column = [part(1).bitcast(I32) for _ in range(LANES)]
        zeros = part(P + 1)
        reach = [where[0]]
        hidden = area[:].rearrange("p (g n) -> p g n", n=GROUP * FFN1)
        where[0] = 0
        att[3] = attention_weights()
        f_wq = part(P)
        f_wk = part(4 * P).rearrange("p (r n) -> p r n", r=4)
        f_wv = part(4 * P).rearrange("p (r n) -> p r n", r=4)
        f_bq = part(1)
        f_bk = part(4)
        f_bv = part(4)
        f_unit = part(4 * P).rearrange("p (s n) -> p s n", s=4)
        dft = part(P)
        idft = part(P)
        wave = part(1)
        dc_q = part(P)
        dc_kv = part(16).rearrange("p (v r b) -> p v r b", v=2, r=4)
        chaos = part(3 * TILES).rearrange("p (k t) -> p k t", k=3)
        norm = part(TILES)
        eneg = part(TILES)
        fac = part(TILES)
        fl = []
        for l in range(LANES):
            fl.append(dict(qh=part(P), p1=part(4 * P), p2=part(4 * 2 * (FREQ - 2)), p3=part(4 * 2 * (FREQ - 2)), qk=part(P), g=part(P), gT=part(P)))
        r_raw = part(P)
        r_t = part(P)
        r_scale = part(2)
        r_diag = part(P)
        r_bc = part(P)
        r_q = part(P // 2).bitcast(BF16)
        q8 = []
        for l in range(WIDE):
            q8.append(dict(amax=part(GROUP), ls=part(GROUP), inv=part(GROUP), y=part(GROUP * P), yT=part(GROUP * P // 2).bitcast(BF16)))
        g_raw = part(3 * FFN3).bitcast(mybir.dt.int32)
        g_w = part(3 * FFN3)
        ff = []
        for l in range(WIDE):
            ff.append(dict(xn=part(2 * P), xnT=part(2 * P), silu=part(2 * FFN3), hT=part(2 * FFN3)))

        reach.append(where[0])

        w_q = sb("w_q", [P, 2, FFN1], BF16)
        b1 = sb("b1", [P, 4])
        b2 = sb("b2", [P, P])
        ones = sb("ones", [P, P])
        magic = sb("magic", [P, 1])
        scratch = sb("scratch", [P, 1])
        tmx = sb("tmx", [P, 2, TILES])
        gcol = sb("gcol", [P, 4])
        grow = sb("grow", [4, 1])
        gdiag = sb("gdiag", [4, 4])
        gall = sb("gall", [P, 4])
        qs = sb("qs", [P, 16])
        hmm = sb("hmm", [P, 2, TILES // GROUP])

        EARLY = 2
        end = [TOKENS * FFN1 // P]

        def lane(name, shape):
            width = math.prod(shape[1:])
            first = [sb(f"{name}{l}", shape)[:] for l in range(EARLY)]
            rest = []
            for l in range(EARLY, LANES):
                end[0] -= width
                flat = area[0:shape[0], end[0]:end[0] + width]
                if len(shape) > 2:
                    names = "abc"[:len(shape) - 1]
                    flat = flat.rearrange(f"p ({' '.join(names)}) -> p {' '.join(names)}", **dict(zip(names, shape[1:])))
                rest.append(flat)
            return first + rest
        xn = lane("xn", [P, P])
        cx = lane("cx", [P, P])
        xc = lane("xc", [P, 3, P])
        qb = lane("qb", [P, 2, P])
        kc = lane("kc", [P, 2, SEQ])
        vflat = lane("vflat", [P, 7 * 34 + P])
        vbd = [v[:, 0:8 * 34].rearrange("p (c e) -> p c e", c=8) for v in vflat]
        mx = lane("mx", [P, 16])
        prob = lane("prob", [P, 16, SEQ])
        probT = lane("probT", [P, 8, P])
        rc = lane("rc", [P, 8, 2])
        fx = lane("fx", [P, 16])
        o = lane("o", [P, 8, 2, 8])
        oT = lane("oT", [P, P])
        assert max(reach) <= end[0]
        moe, exp = [], []
        for l in range(LANES):
            cuts = lambda flat: dict(t=flat[:, 0:128], tT=flat[:, 128:256], silu=flat[:, 256:512], h=flat[:, 512:768], hT=flat[:, 768:1024])
            moe.append(cuts(prob[l][:].rearrange("p g k -> p (g k)")))
            exp.append(cuts(probT[l][:].rearrange("p c k -> p (c k)")))
            moe[l]["row"] = xc[l][:].rearrange("p b k -> p (b k)")[:, 0:P + 1]
            exp[l]["score"] = rc[l][:, 0, 0:1]
            exp[l]["row"] = xc[l][:].rearrange("p b k -> p (b k)")[:, P + 1:2 * (P + 1)]
        kx = [probT[l] for l in range(LANES)]
        xqT = [xc[l][:, 1:3, :].rearrange("p b k -> p (b k)").bitcast(BF16) for l in range(WIDE)]
        hq = [prob[l][:].rearrange("p g k -> p (g k)").bitcast(BF16) for l in range(WIDE)]

        ps_s = [pb(f"ps{l}", [P, 1024]) for l in range(LANES)]
        ps_a = [p_[:, 0:512] for p_ in ps_s]
        ps_b = [p_[:, 512:1024] for p_ in ps_s]
        wide_a = [ps_s[WIDE + l][:, 0:512] for l in range(WIDE)]
        wide_b = [ps_s[WIDE + l][:, 512:1024] for l in range(WIDE)]

        loaded = {n: sem(f"loaded_{n}") for n in ("x0", "x1", "x2", "x3", "const", "att0", "att1", "att3", "ffn0", "ffn1", "late")}
        ctx_in = [sem(f"ctx_in{l}") for l in range(LANES)]
        dve_sem = [sem(f"dve_done{l}") for l in range(LANES)]
        act_sem = [sem(f"act_done{l}") for l in range(LANES)]
        pe_sem = [sem(f"pe_done{l}") for l in range(LANES)]
        pool_sem = [sem(f"pool_done{l}") for l in range(LANES)]
        filled = sem("filled")
        scattered = [sem(f"scattered{l}") for l in range(LANES)]
        slots_in = [sem(f"slots_in{l}") for l in range(LANES)]
        slots_out = [sem(f"slots_out{l}") for l in range(LANES)]
        gathered = [sem(f"gathered{l}") for l in range(LANES)]
        best_ready = sem("best_ready")
        tanh_ready = sem("tanh_ready")
        score_ready = sem("score_ready")
        one_ready = sem("one_ready")
        counted = sem("counted")
        slots_ready = sem("slots_ready")
        x_stats = sem("x_stats")
        root_wanted = sem("root_wanted")
        root_given = sem("root_given")
        stored = sem("stored")

        x_tiles = dram["x"].rearrange("(t p) d -> p t d", p=P)
        ctx_tiles = dram["ctx_1024"].rearrange("(t p) d -> t p d", p=P)
        out_tiles = out.rearrange("(t p) d -> p t d", p=P)

        layers = {}
        base = [dict(dve=0, act=0, pe=0, pool=0, ctx=0) for _ in range(LANES)]

        def declare(key, rounds, dve=(), act=(), pe=(), pool=(), context=False, lanes=LANES, ahead={}):
            lay = dict(rounds=rounds, lanes=lanes, ctx=base[0]["ctx"])
            for n, names, sems in (("dve", dve, dve_sem), ("act", act, act_sem), ("pe", pe, pe_sem), ("pool", pool, pool_sem)):
                lay[n] = [Steps(sems[l], base[l][n], names, ahead.get(n, []), rounds) for l in range(lanes)]
                for l in range(lanes):
                    base[l][n] += rounds * len(names)
            for l in range(lanes):
                base[l]["ctx"] += 16 * rounds if context else 0
            layers[key] = lay

        def attention_layer(L):
            masked = L == 0
            declare(f"att{L}", ROUNDS, context=True,
                    dve=["mx", "sub"] + ["fx"] * masked + ["xn"] + ["fs"] * masked + ["rc", "o", "fin", "st"] + ["am"] * masked + ["v"],
                    act=["exp", "probT", "oT", "xc", "k", "q"],
                    pe=["s", "probT", "pv", "T", "oT", "y", "qk", "v"],
                    pool=["bo", "kx"],
                    ahead=dict(dve=["xn"] + ["am"] * masked + ["v"], act=["xc", "k", "q"], pe=["T", "qk", "v"], pool=["kx"]))
        QROUNDS = TILES // GROUP // WIDE
        FFN3_ROUNDS = TILES // 2 // WIDE
        attention_layer(0)
        declare("ffn0r", ROUNDS, dve=["t", "xw"], act=["nT", "lg"], pe=["nT", "lg"])
        declare("ffn0a", ROUNDS, dve=["sh", "acc", "acc2"], act=["ssilu", "hT", "sc", "nT"], pe=["sh", "hT", "sdn", "nT"], pool=["col"],
                ahead=dict(act=["sc", "nT"], pe=["nT"], pool=["col"]))
        declare("ffn0b", SLOT_ROUNDS, dve=["h", "score"], act=["silu", "hT", "o", "xT"], pe=["gu", "hT", "T", "dn"], ahead=dict(dve=["score"], act=["xT"], pe=["T"]))
        declare("ffn0c", ROUNDS, dve=["fin", "st"], pool=["col"], ahead=dict(pool=["col"]))
        attention_layer(1)
        declare("ffn1a", QROUNDS, lanes=WIDE, dve=["xs", "xn", "xr", "xc", "hmx", "hmn", "xT"], act=["g0", "g1", "g2", "g3"],
                pe=["m0", "m1", "m2", "m3", "xT"], ahead=dict(dve=["xs", "xn", "xr", "xc", "xT"], pe=["xT"]))
        declare("ffn1b", QROUNDS, lanes=WIDE, dve=["hc", "hb", "yb", "fin", "st"], act=["hr"], pe=["y"])
        declare("freq", ROUNDS, context=True, dve=["q", "kb", "p", "pm", "ps", "vb", "r", "rm", "rs", "xs", "fin", "st"],
                act=["qk", "g", "xf", "cf", "gT"], pe=["pq", "pk", "pv", "qk", "g", "dft", "gT", "y"], pool=["pz", "rz"],
                ahead=dict(dve=["xs"], act=["xf", "cf"], pe=["dft"]))
        declare("ffn2", QROUNDS, lanes=WIDE, dve=["xs", "xn", "amax", "ls", "inv", "y", "yr", "yc", "yT", "a", "b", "fin", "st"], pe=["yT", "mm"])
        attention_layer(3)
        declare("ffn3", FFN3_ROUNDS, lanes=WIDE, dve=["h0", "xn", "h1", "fin"], act=["s0", "s1", "xnT"], pe=["gu0", "gu1", "xnT", "y"],
                ahead=dict(dve=["xn"], act=["xnT"], pe=["xnT"]))

        FILLS = 4 * LANES + 3
        LATE_FILLS = FILLS + 4 * (LANES - EARLY)

        dve_chain = sem("dve_chain")
        act_chain = sem("act_chain")
        to_pe = sem("column_ready")
        from_pe = sem("column_turned")
        norm_ready = sem("norm_ready")
        hidden_scaled = sem("hidden_scaled")
        eneg_ready = sem("eneg_ready")

        block = ctx.enter_context(nc.Block())

        LATE = [("f_wq", f_wq), ("f_wk", f_wk), ("f_wv", f_wv), ("f_bq", f_bq), ("f_bk", f_bk), ("f_bv", f_bv),
                ("c_unit", f_unit), ("c_dft", dft), ("c_idft", idft), ("c_wave", wave), ("r_raw", r_raw), ("g_raw", g_raw)]

        @block.sync
        def _(sp):
            for c in range(4):
                q = TILES // 4
                sp.dma_start(x[:, c * q:(c + 1) * q, :], x_tiles[:, c * q:(c + 1) * q, :]).then_inc(loaded[f"x{c}"], 16)
            sp.dma_start(ident[:], dram["c_ident"]).then_inc(loaded["const"], 16)
            sp.dma_start(head_mask[:], dram["c_head_mask"]).then_inc(loaded["const"], 16)
            sp.dma_start(causal[:], dram["c_causal"]).then_inc(loaded["const"], 16)
            sp.dma_start(half_pad[:], dram["c_half_pad"]).then_inc(loaded["const"], 16)
            def weights(L):
                w = att[L]
                for n in ("wq", "wk", "wv", "wo", "bq", "bk"):
                    sp.dma_start(w[n], dram[f"a{L}_{n}"]).then_inc(loaded[f"att{L}"], 16)
                for n in ("bv", "bo"):
                    sp.dma_start(w[n], dram[f"a{L}_{n}"].to_broadcast([P, P])).then_inc(loaded[f"att{L}"], 16)
                if L == 0:
                    keys = dram["mask_BxS2_bf1"].rearrange("o (t b k) -> o b t k", b=2, k=SEQ)
                    for b in range(2):
                        sp.dma_start(key_mask[64 * b:64 * b + 64], keys[:, b].to_broadcast([SEQ, TILES, SEQ])).then_inc(loaded["const"], 16)
                    for n, where_ in (("gate_up", gate_up), ("down0", down0), ("shared_gu", shared_gu), ("shared_dn", shared_dn), ("router", router),
                                      ("ln_w", ln_w), ("ln_b", ln_b), ("c_earlier", earlier)):
                        sp.dma_start(where_, dram[n]).then_inc(loaded["ffn0"], 16)
                    for n, where_ in (("c_rank", rank), ("c_slot_tile", slot_tile)):
                        sp.dma_start(where_, dram[n].to_broadcast([P, where_.shape[1]])).then_inc(loaded["ffn0"], 16)
            weights(0)
            weights(1)
            for n, where_ in (("w12", w_raw), ("b1", b1[:])):
                sp.dma_start(where_, dram[n]).then_inc(loaded["ffn1"], 16)
            sp.dma_start(b2[:], dram["b2"].to_broadcast([P, P])).then_inc(loaded["ffn1"], 16)

            def ctx_loads(key):
                lay = layers[key]
                for l in range(LANES):
                    if lay["pe"][l].base:
                        sp.wait_ge(pe_sem[l], lay["pe"][l].base)
                    sp.dma_start(cx[l][:], ctx_tiles[l]).then_inc(ctx_in[l], 16)

                def load(i, l, read):
                    sp.wait_ge(pe_sem[l], lay["pe"][l].at(i, read))
                    sp.dma_start(cx[l][:], ctx_tiles[(i + 1) * LANES + l]).then_inc(ctx_in[l], 16)
                read = "dft" if key == "freq" else "T"
                for l in range(LANES):
                    load(0, l, read)
                with nc.sync.Fori(0, ROUNDS - 2) as i:
                    for l in range(LANES):
                        load(i + 1, l, read)

            sp.wait_ge(filled, FILLS)
            to_slots = rows_in.rearrange("(l k p) d -> l p k d", l=LANES, p=P)
            for l in range(LANES):
                sp.dma_start(to_slots[l], zeros.unsqueeze(1).to_broadcast([P, SLOT_ROUNDS, P + 1])).then_inc(slots_out[l], 16)

            ctx_loads("att0")
            lay = layers["ffn0b"]
            in_tiles, out_tiles_ = rows_in.rearrange("(k p) d -> k p d", p=P), rows_out.rearrange("(k p) d -> k p d", p=P)
            for l in range(LANES):
                sp.wait_ge(scattered[l], 16 * ROUNDS)

            def load_slots(i):
                for l in range(LANES):
                    if not (isinstance(i, int) and i == 0):
                        sp.wait_ge(pe_sem[l], lay["pe"][l].at(i - 1, "T"))
                        sp.wait_ge(dve_sem[l], lay["dve"][l].at(i - 1, "score"))
                    sp.dma_start(exp[l]["row"], in_tiles[i * LANES + l]).then_inc(slots_in[l], 16)

            def store_slots(i):
                for l in range(LANES):
                    sp.wait_ge(act_sem[l], lay["act"][l].at(i, "o"))
                    sp.dma_start(out_tiles_[i * LANES + l], moe[l]["t"]).then_inc(slots_out[l], 16)
            load_slots(0)
            load_slots(1)
            with nc.sync.Fori(0, SLOT_ROUNDS - 2) as i:
                store_slots(i)
                load_slots(i + 2)
            store_slots(SLOT_ROUNDS - 2)
            store_slots(SLOT_ROUNDS - 1)
            ctx_loads("att1")
            for l in range(WIDE):
                sp.wait_ge(dve_sem[l], layers["ffn1b"]["dve"][l].end())
            for n, where_ in LATE:
                sp.dma_start(where_, dram[n]).then_inc(loaded["late"], 16)
            weights(3)
            ctx_loads("freq")
            ctx_loads("att3")
            last = layers["ffn3"]
            for c in range(4):
                q = TILES // 4
                for l in range(last["lanes"]):
                    sp.wait_ge(dve_sem[l], last["dve"][l].at((c + 1) * last["rounds"] // 4 - 1, last["dve"][l].names[-1]))
                sp.dma_start(out_tiles[:, c * q:(c + 1) * q, :], x[:, c * q:(c + 1) * q, :]).then_inc(stored, 16)
            sp.wait_ge(stored, 16 * 4)
            for n, count in (("att1", 8), ("ffn0", 10), ("ffn1", 3)):
                sp.wait_ge(loaded[n], 16 * count)

        @block.gpsimd
        def _(pool):
            fill_count = [0]

            def fill(fills):
                for where_, value in fills:
                    if fill_count[0]:
                        pool.wait_ge(filled, fill_count[0])
                    nc.gpsimd.memset(where_, value).then_inc(filled, 1)
                    fill_count[0] += 1

            def lane_fills(lanes):
                for l in lanes:
                    fill([(vflat[l][:], 0.0), (qb[l][:], 0.0), (vbd[l][0:64, :, 32:33], 1.0), (vbd[l][64:128, :, 33:34], 1.0)])
            lane_fills(range(LANES))
            fill([(ones[:], 1.0), (magic[:], MAGIC), (zeros, 0.0)])

            pool.wait_ge(filled, fill_count[0])

            def attention(L):
                lay, w = layers[f"att{L}"], att[L]
                pool.wait_ge(loaded["const"], 16 * 6)
                pool.wait_ge(loaded[f"att{L}"], 16 * 8)

                def spread(i):
                    for l in range(LANES):
                        pool.wait_ge(act_sem[l], lay["act"][l].at(i, "k"))
                        nc.gpsimd.tensor_tensor(kx[l][:].rearrange("p (g c) (j k) -> p g (c j) k", g=2, j=2),
                                                kc[l][:].unsqueeze(2).to_broadcast([P, 2, 8, SEQ]),
                                                head_mask[:].unsqueeze(1).unsqueeze(3).to_broadcast([P, 2, 8, SEQ]), ALU.mult).then_inc(pool_sem[l], 1)

                def body(i, more):
                    for l in range(LANES):
                        t = i * LANES + l
                        pool.wait_ge(dve_sem[l], lay["dve"][l].at(i, "mx"))
                        nc.gpsimd.tensor_tensor(x[:, t, :], x[:, t, :], w["bo"], ALU.add).then_inc(pool_sem[l], 1)
                    if more:
                        spread(i + 1)
                spread(0)
                with nc.gpsimd.Fori(0, ROUNDS - 1) as i:
                    body(i, True)
                body(ROUNDS - 1, False)
            attention(0)
            pool.wait_ge(slots_ready, 1)
            for l in range(LANES):
                pool.wait_ge(slots_out[l], 16)

            def column_of(lay, i, l):
                nc.gpsimd.tensor_copy(column[l], slot_i[:, bass.ds(i * LANES + l, 1)]).then_inc(pool_sem[l], 1)
                pool.wait_ge(pool_sem[l], lay["pool"][l].at(i, "col"))

            def scatter(i, l):
                column_of(layers["ffn0a"], i, l)
                pool.wait_ge(act_sem[l], layers["ffn0a"]["act"][l].at(i, "sc"))
                nc.gpsimd.nop(nofuse=True)
                nc.gpsimd.indirect_dma_start(rows_in, bass.IndirectOffsetOnAxis(ap=column[l], axis=0), moe[l]["row"], None).then_inc(scattered[l], 16)
            for l in range(LANES):
                scatter(0, l)
            with nc.gpsimd.Fori(0, ROUNDS - 1) as i:
                for l in range(LANES):
                    pool.wait_ge(scattered[l], i * 16 + 16)
                    scatter(i + 1, l)
            for l in range(LANES):
                pool.wait_ge(scattered[l], 16 * ROUNDS)
                pool.wait_ge(slots_out[l], 16 * (SLOT_ROUNDS + 1))

            def gather(i, l):
                column_of(layers["ffn0c"], i, l)
                nc.gpsimd.nop(nofuse=True)
                nc.gpsimd.indirect_dma_start(exp[l]["t"], None, rows_out, bass.IndirectOffsetOnAxis(ap=column[l], axis=0)).then_inc(gathered[l], 16)
            for l in range(LANES):
                gather(0, l)
            with nc.gpsimd.Fori(0, ROUNDS - 1) as i:
                for l in range(LANES):
                    pool.wait_ge(dve_sem[l], layers["ffn0c"]["dve"][l].at(i, "fin"))
                    gather(i + 1, l)
            attention(1)
            lay = layers["freq"]
            with nc.gpsimd.Fori(0, ROUNDS) as i:
                for after, name in (("ps", "pz"), ("rs", "rz")):
                    for l in range(LANES):
                        pool.wait_ge(dve_sem[l], lay["dve"][l].at(i, after))
                        nc.gpsimd.tensor_tensor(fl[l]["p1"].rearrange("p (r m) -> p r m", m=SEQ)[:, :, FREQ:SEQ],
                                                fl[l]["p2"].rearrange("p (r m) -> p r m", m=FREQ - 2), fl[l]["p3"].rearrange("p (r m) -> p r m", m=FREQ - 2), ALU.add).then_inc(pool_sem[l], 1)
            for l in range(WIDE):
                pool.wait_ge(dve_sem[l], layers["ffn1b"]["dve"][l].end())
            lane_fills(range(EARLY, LANES))
            pool.wait_ge(filled, fill_count[0])
            attention(3)

        @block.scalar
        def _(act):
            roots = [0]

            def square_root():
                roots[0] += 1
                act.wait_ge(root_wanted, roots[0])
                nc.scalar.activation(root[:], vpe[:], ACT.Sqrt).then_inc(root_given, 1)

            def attention(L):
                lay, w = layers[f"att{L}"], att[L]
                square_root()
                act.wait_ge(loaded[f"att{L}"], 16 * 8)
                nc.scalar.activation(scratch[:], magic[:], ACT.Exp, scale=0.0).then_inc(act_chain, 1)

                def inputs(i):
                    pe = [lambda n, l=l: act.wait_ge(pe_sem[l], lay["pe"][l].at(i, n)) for l in range(LANES)]
                    for l in range(LANES):
                        pe[l]("T")
                        nc.scalar.copy(xc[l][:, 0, :], ps_b[l][:, 0:128])
                        nc.scalar.copy(xc[l][:, 1:3, :].rearrange("p b (two k) -> p b two k", two=2),
                                       ps_b[l][:, 128:256].rearrange("p (b k) -> p b k", b=2).unsqueeze(2).to_broadcast([P, 2, 2, SEQ])).then_inc(act_sem[l], 1)
                    for l in range(LANES):
                        pe[l]("qk")
                        for first, bias, into in ((256, w["bk"], lambda r, g: kc[l][r, g, :]), (0, w["bq"], lambda r, g: qb[l][r, g, r])):
                            for g in range(2):
                                for b in range(2):
                                    r = slice(64 * b, 64 * b + 64)
                                    e = nc.scalar.activation(into(r, g), ps_b[l][r, first + g * 128 + 64 * b:first + g * 128 + 64 * b + 64], ACT.Identity, bias=bias[r, g:g + 1])
                            e.then_inc(act_sem[l], 1)

                def body(i, more):
                    pe = [lambda n, l=l: act.wait_ge(pe_sem[l], lay["pe"][l].at(i, n)) for l in range(LANES)]
                    for l in range(LANES):
                        act.wait_ge(dve_sem[l], lay["dve"][l].at(i, "sub"))
                        nc.scalar.activation(prob[l][:], prob[l][:], ACT.Exp).then_inc(act_sem[l], 1)
                    for l in range(LANES):
                        pe[l]("probT")
                        nc.scalar.copy(probT[l][:], ps_s[l][:]).then_inc(act_sem[l], 1)
                    for l in range(LANES):
                        pe[l]("oT")
                        nc.scalar.copy(oT[l][:], ps_a[l][:, 384:512]).then_inc(act_sem[l], 1)
                    if more:
                        inputs(i + 1)
                inputs(0)
                with nc.scalar.Fori(0, ROUNDS - 1) as i:
                    body(i, True)
                body(ROUNDS - 1, False)
            act.wait_ge(filled, FILLS)
            attention(0)
            square_root()
            square_root()
            lay = layers["ffn0r"]
            act.wait_ge(loaded["ffn0"], 16 * 10)
            act.wait_ge(act_chain, 1)
            nc.scalar.activation(scratch[:], magic[:], ACT.Tanh, scale=0.0).then_inc(act_chain, 1)

            def weighted(l, bank):
                nc.scalar.activation(moe[l]["tT"], bank, ACT.Identity, bias=ln_b, scale=ln_w).then_inc(act_sem[l], 1)
            with nc.scalar.Fori(0, ROUNDS) as i:
                for l in range(LANES):
                    act.wait_ge(pe_sem[l], lay["pe"][l].at(i, "nT"))
                    weighted(l, ps_a[l][:, 0:128])
                for l in range(LANES):
                    act.wait_ge(pe_sem[l], lay["pe"][l].at(i, "lg"))
                    nc.scalar.copy(logits[:, i * LANES + l, :], ps_b[l][:, 0:EXPERTS]).then_inc(act_sem[l], 1)
            act.wait_ge(best_ready, 1)
            nc.scalar.activation(score, best, ACT.Tanh, scale=0.5).then_inc(tanh_ready, 1)
            act.wait_ge(act_chain, 2)
            nc.scalar.activation(scratch[:], magic[:], ACT.Silu, scale=0.0).then_inc(act_chain, 1)
            act.wait_ge(score_ready, 1)
            lay = layers["ffn0a"]

            def inputs(i):
                for l in range(LANES):
                    t = i * LANES + l
                    if not (isinstance(i, int) and i == 0):
                        act.wait_ge(scattered[l], i * 16)
                    nc.scalar.copy(moe[l]["row"][:, 0:P], xw[:, t, :])
                    nc.scalar.copy(moe[l]["row"][:, P:P + 1], score[:, bass.ds(t, 1)]).then_inc(act_sem[l], 1)
                for l in range(LANES):
                    act.wait_ge(pe_sem[l], lay["pe"][l].at(i, "nT"))
                    weighted(l, ps_a[l][:, 0:128])

            def body(i, more):
                pe = [lambda n, l=l: act.wait_ge(pe_sem[l], lay["pe"][l].at(i, n)) for l in range(LANES)]
                for l in range(LANES):
                    pe[l]("sh")
                    nc.scalar.activation(moe[l]["silu"], ps_b[l][:, 0:FFN0], ACT.Silu).then_inc(act_sem[l], 1)
                for l in range(LANES):
                    pe[l]("hT")
                    nc.scalar.copy(moe[l]["hT"], ps_a[l][:, 256:512]).then_inc(act_sem[l], 1)
                if more:
                    inputs(i + 1)
            inputs(0)
            with nc.scalar.Fori(0, ROUNDS - 1) as i:
                body(i, True)
            body(ROUNDS - 1, False)
            lay = layers["ffn0b"]

            def spread(i, l):
                act.wait_ge(pe_sem[l], lay["pe"][l].at(i, "T"))
                nc.scalar.activation(exp[l]["tT"], ps_b[l][:, 0:128], ACT.Identity, bias=ln_b, scale=ln_w).then_inc(act_sem[l], 1)

            def body(i, more):
                pe = [lambda n, l=l: act.wait_ge(pe_sem[l], lay["pe"][l].at(i, n)) for l in range(LANES)]
                for l in range(LANES):
                    pe[l]("gu")
                    act.wait_ge(dve_sem[l], lay["dve"][l].at(i, "score"))
                    nc.scalar.activation(exp[l]["silu"], ps_b[l][:, 0:FFN0], ACT.Silu, scale=exp[l]["score"]).then_inc(act_sem[l], 1)
                for l in range(LANES):
                    pe[l]("hT")
                    nc.scalar.copy(exp[l]["hT"], ps_a[l][:, 128:384]).then_inc(act_sem[l], 1)
                for l in range(LANES):
                    pe[l]("dn")
                    act.wait_ge(slots_out[l], i * 16 + 16)
                    nc.scalar.copy(moe[l]["t"], ps_a[l][:, 384:512]).then_inc(act_sem[l], 1)
                    if more:
                        spread(i + 1, l)
            for l in range(LANES):
                spread(0, l)
            with nc.scalar.Fori(0, SLOT_ROUNDS - 1) as i:
                body(i, True)
            body(SLOT_ROUNDS - 1, False)
            act.wait_ge(act_chain, 3)
            attention(1)
            square_root()
            act.wait_ge(loaded["ffn1"], 16 * 3)
            lay = layers["ffn1a"]
            act.wait_ge(act_chain, 4)
            nc.scalar.activation(scratch[:], magic[:], ACT.Gelu, scale=0.0).then_inc(act_chain, 1)
            with nc.scalar.Fori(0, QROUNDS) as i:
                for l in range(WIDE):
                    for c, bank in enumerate((ps_s[l][:, 0:512], ps_s[l][:, 512:1024], wide_b[l][:], wide_a[l][:])):
                        act.wait_ge(pe_sem[l], lay["pe"][l].at(i, f"m{c}"))
                        nc.scalar.activation(hidden[:, i * WIDE + l, c * 512:c * 512 + 512], bank, ACT.Gelu,
                                             bias=b1[:, c:c + 1], scale=qs[:, 8:9]).then_inc(act_sem[l], 1)
            lay = layers["ffn1b"]
            act.wait_ge(hidden_scaled, 1)
            with nc.scalar.Fori(0, QROUNDS) as i:
                for l in range(WIDE):
                    nc.scalar.activation(hidden[:, i * WIDE + l, :], hidden[:, i * WIDE + l, :], ACT.Identity,
                                         bias=magic[:], scale=qs[:, 1:2]).then_inc(act_sem[l], 1)
            square_root()
            square_root()
            act.wait_ge(norm_ready, 1)
            nc.scalar.activation(eneg, norm, ACT.Exp, scale=-1.0).then_inc(eneg_ready, 1)
            act.wait_ge(loaded["late"], 16 * len(LATE))
            lay = layers["freq"]

            def inputs(i, l):
                act.wait_ge(pe_sem[l], lay["pe"][l].at(i, "dft"))
                nc.scalar.copy(xc[l][:, 0, :], ps_a[l][:, 256:384]).then_inc(act_sem[l], 1)
                nc.scalar.mul(xc[l][:, 1, :], ps_a[l][:, 384:512], MEMORY_SCALE).then_inc(act_sem[l], 1)

            def body(i, more):
                pe = [lambda n, l=l: act.wait_ge(pe_sem[l], lay["pe"][l].at(i, n)) for l in range(LANES)]
                for l in range(LANES):
                    pe[l]("qk")
                    nc.scalar.copy(fl[l]["qk"], ps_b[l][:, 0:128]).then_inc(act_sem[l], 1)
                for l in range(LANES):
                    pe[l]("g")
                    nc.scalar.copy(fl[l]["g"], ps_b[l][:, 0:128]).then_inc(act_sem[l], 1)
                if more:
                    for l in range(LANES):
                        inputs(i + 1, l)
                for l in range(LANES):
                    pe[l]("gT")
                    nc.scalar.copy(fl[l]["gT"], ps_a[l][:, 0:128]).then_inc(act_sem[l], 1)
            for l in range(LANES):
                inputs(0, l)
            with nc.scalar.Fori(0, ROUNDS - 1) as i:
                body(i, True)
            body(ROUNDS - 1, False)
            square_root()
            act.wait_ge(act_chain, 5)
            attention(3)
            square_root()
            lay = layers["ffn3"]
            act.wait_ge(act_chain, 6)
            nc.scalar.activation(scratch[:], magic[:], ACT.Silu, scale=0.0).then_inc(act_chain, 1)

            def inputs(i):
                for l in range(WIDE):
                    act.wait_ge(pe_sem[l], lay["pe"][l].at(i, "xnT"))
                    nc.scalar.copy(ff[l]["xnT"], wide_b[l][:, 256:512]).then_inc(act_sem[l], 1)

            def body(i, more):
                pe = [lambda n, l=l: act.wait_ge(pe_sem[l], lay["pe"][l].at(i, n)) for l in range(WIDE)]
                for l in range(WIDE):
                    pe[l]("gu0")
                    nc.scalar.activation(ff[l]["silu"][:, 0:512].rearrange("p (c t) -> p c t", c=2),
                                         ps_s[l][:].rearrange("p (c k t) -> p c k t", c=2, k=2)[:, :, 0, :], ACT.Silu).then_inc(act_sem[l], 1)
                    pe[l]("gu1")
                    nc.scalar.activation(ff[l]["silu"][:, 512:768], wide_a[l][:, 0:256], ACT.Silu).then_inc(act_sem[l], 1)
                if more:
                    inputs(i + 1)
            inputs(0)
            with nc.scalar.Fori(0, FFN3_ROUNDS - 1) as i:
                body(i, True)
            body(FFN3_ROUNDS - 1, False)

        @block.tensor
        def _(te):
            te.wait_ge(loaded["const"], 16 * 6)
            te.wait_ge(filled, FILLS)

            def attention(L):
                lay, w = layers[f"att{L}"], att[L]
                te.wait_ge(loaded[f"att{L}"], 16 * 8)
                if L == 3:
                    te.wait_ge(filled, LATE_FILLS)

                def inputs(i):
                    for l in range(LANES):
                        te.wait_ge(dve_sem[l], lay["dve"][l].at(i, "xn"))
                        nc.tensor.transpose(ps_b[l][:, 0:128], xn[l][:], ident[:])
                        te.wait_ge(ctx_in[l], i * 16 + (lay["ctx"] + 16))
                        nc.tensor.transpose(ps_b[l][:, 128:256], cx[l][:], ident[:]).then_inc(pe_sem[l], 1)

                def projections(i, before):
                    for l in range(LANES):
                        te.wait_ge(act_sem[l], lay["act"][l].at(i, "xc"))
                        for g in range(2):
                            nc.tensor.matmul(ps_b[l][:, g * 128:g * 128 + 128], w["wq"][:, g, :], xc[l][:, 0, :], start=True, stop=True)
                            mm = nc.tensor.matmul(ps_b[l][:, 256 + g * 128:256 + g * 128 + 128], w["wk"][:, g, :],
                                                  xc[l][:, 1:3, 0:SEQ], start=True, stop=True)
                        mm.then_inc(pe_sem[l], 1)
                    for l in range(LANES):
                        if before is not None:
                            te.wait_ge(dve_sem[l], lay["dve"][l].at(before, "fin"))
                        for b in range(2):
                            mm = nc.tensor.matmul(ps_a[l][:, 128 + b * 128:256 + b * 128], xc[l][:, 1 + b, :], w["wv"], start=True, stop=True)
                        mm.then_inc(pe_sem[l], 1)

                def body(i, more):
                    dve = [lambda n, l=l: te.wait_ge(dve_sem[l], lay["dve"][l].at(i, n)) for l in range(LANES)]
                    act = [lambda n, l=l: te.wait_ge(act_sem[l], lay["act"][l].at(i, n)) for l in range(LANES)]
                    for l in range(LANES):
                        act[l]("q")
                        te.wait_ge(pool_sem[l], lay["pool"][l].at(i, "kx"))
                        dve[l]("v")
                        for g in range(2):
                            bank = ps_s[l][:, g * 512:g * 512 + 512]
                            if L == 0:
                                nc.tensor.matmul(bank, minus_masked, am[l].unsqueeze(1).to_broadcast([P, 8, SEQ]), start=True, stop=False)
                            mm = nc.tensor.matmul(bank, qb[l][:, g, :], kx[l][:, 4 * g:4 * g + 4, :], start=(L != 0), stop=True)
                        mm.then_inc(pe_sem[l], 1)
                    for l in range(LANES):
                        act[l]("exp")
                        for c in range(8):
                            mm = nc.tensor.transpose(ps_s[l][:, c * 128:c * 128 + 128], prob[l][:, 2 * c:2 * c + 2, :], ident[:])
                        mm.then_inc(pe_sem[l], 1)
                    for l in range(LANES):
                        act[l]("probT")
                        for c in range(8):
                            mm = nc.tensor.matmul(ps_a[l][:, c * 34:c * 34 + P], probT[l][:, c, :], vflat[l][:, c * 34:c * 34 + P], start=True, stop=True)
                        mm.then_inc(pe_sem[l], 1)
                    if more:
                        inputs(i + 1)
                    for l in range(LANES):
                        dve[l]("o")
                        nc.tensor.transpose(ps_a[l][:, 384:512], o[l][:].rearrange("p c j d -> p (c j d)"), ident[:]).then_inc(pe_sem[l], 1)
                    for l in range(LANES):
                        act[l]("oT")
                        nc.tensor.matmul(ps_a[l][:, 0:128], oT[l][:], w["wo"], start=True, stop=True).then_inc(pe_sem[l], 1)
                    if more:
                        projections(i + 1, i)
                inputs(0)
                projections(0, None)
                with nc.tensor.Fori(0, ROUNDS - 1) as i:
                    body(i, True)
                body(ROUNDS - 1, False)
            attention(0)
            lay = layers["ffn0r"]
            te.wait_ge(loaded["ffn0"], 16 * 10)
            with nc.tensor.Fori(0, ROUNDS) as i:
                for l in range(LANES):
                    te.wait_ge(dve_sem[l], lay["dve"][l].at(i, "t"))
                    nc.tensor.transpose(ps_a[l][:, 0:128], moe[l]["t"], ident[:]).then_inc(pe_sem[l], 1)
                for l in range(LANES):
                    te.wait_ge(act_sem[l], lay["act"][l].at(i, "nT"))
                    nc.tensor.matmul(ps_b[l][:, 0:EXPERTS], moe[l]["tT"], router, start=True, stop=True).then_inc(pe_sem[l], 1)
                for l in range(LANES):
                    te.wait_ge(act_sem[l], lay["act"][l].at(i, "lg"))
            te.wait_ge(one_ready, 1)
            nc.tensor.matmul(ps_a[0][:], earlier, one.rearrange("p t e -> p (t e)"), start=True, stop=True)
            nc.tensor.matmul(ps_b[0][:], ones[:], one.rearrange("p t e -> p (t e)"), start=True, stop=True).then_inc(counted, 1)
            te.wait_ge(slots_ready, 1)
            lay = layers["ffn0a"]

            def inputs(i, before):
                for l in range(LANES):
                    te.wait_ge(act_sem[l], lay["act"][l].at(i, "sc"))
                    if before is not None:
                        te.wait_ge(dve_sem[l], lay["dve"][l].at(before, "acc2"))
                    nc.tensor.transpose(ps_a[l][:, 0:128], moe[l]["row"][:, 0:P], ident[:]).then_inc(pe_sem[l], 1)

            def body(i, more):
                dve = [lambda n, l=l: te.wait_ge(dve_sem[l], lay["dve"][l].at(i, n)) for l in range(LANES)]
                act = [lambda n, l=l: te.wait_ge(act_sem[l], lay["act"][l].at(i, n)) for l in range(LANES)]
                for l in range(LANES):
                    act[l]("nT")
                    nc.tensor.matmul(ps_b[l][:], moe[l]["tT"], shared_gu, start=True, stop=True).then_inc(pe_sem[l], 1)
                for l in range(LANES):
                    dve[l]("sh")
                    for c in range(2):
                        mm = nc.tensor.transpose(ps_a[l][:, 256 + c * 128:384 + c * 128], moe[l]["h"][:, c * 128:c * 128 + 128], ident[:])
                    mm.then_inc(pe_sem[l], 1)
                for l in range(LANES):
                    act[l]("hT")
                    for c in range(2):
                        mm = nc.tensor.matmul(ps_b[l][:, 0:128], moe[l]["hT"][:, c * 128:c * 128 + 128], shared_dn[:, c, :], start=(c == 0), stop=(c == 1))
                    mm.then_inc(pe_sem[l], 1)
                if more:
                    inputs(i + 1, i)
            inputs(0, None)
            with nc.tensor.Fori(0, ROUNDS - 1) as i:
                body(i, True)
            body(ROUNDS - 1, False)
            lay = layers["ffn0b"]
            owner_regs = [te.alloc_register(f"owner{l}") for l in range(LANES)]

            def inputs(i):
                for l in range(LANES):
                    te.wait_ge(slots_in[l], i * 16 + 16)
                    nc.tensor.transpose(ps_b[l][:, 0:128], exp[l]["row"][:, 0:P], ident[:]).then_inc(pe_sem[l], 1)

            def body(i, more):
                te.load(owner_regs, owner_i[0:1, bass.ds(i * LANES, LANES)])
                mine = [te.snap(r, min_val=0, max_val=EXPERTS - 1) for r in owner_regs]
                for l in range(LANES):
                    te.wait_ge(act_sem[l], lay["act"][l].at(i, "xT"))
                    nc.tensor.matmul(ps_b[l][:], exp[l]["tT"], gate_up[:, mine[l], :], start=True, stop=True).then_inc(pe_sem[l], 1)
                for l in range(LANES):
                    te.wait_ge(dve_sem[l], lay["dve"][l].at(i, "h"))
                    for c in range(2):
                        mm = nc.tensor.transpose(ps_a[l][:, 128 + c * 128:256 + c * 128], exp[l]["h"][:, c * 128:c * 128 + 128], ident[:])
                    mm.then_inc(pe_sem[l], 1)
                if more:
                    inputs(i + 1)
                for l in range(LANES):
                    te.wait_ge(act_sem[l], lay["act"][l].at(i, "hT"))
                    for c in range(2):
                        mm = nc.tensor.matmul(ps_a[l][:, 384:512], exp[l]["hT"][:, c * 128:c * 128 + 128], down0[:, c, bass.ds(mine[l] * P, P)], start=(c == 0), stop=(c == 1))
                    mm.then_inc(pe_sem[l], 1)
            for l in range(LANES):
                te.wait_ge(dve_sem[l], layers["ffn0a"]["dve"][l].end())
            inputs(0)
            with nc.tensor.Fori(0, SLOT_ROUNDS - 1) as i:
                body(i, True)
            body(SLOT_ROUNDS - 1, False)
            attention(1)

            def turn(columns, n):
                te.wait_ge(to_pe, n + 1)
                nc.tensor.transpose(ps_a[0][0:columns, 0:128], gcol[:, 0:columns], ident[:]).then_inc(from_pe, 1)
                te.wait_ge(to_pe, n + 2)
                nc.tensor.matmul(ps_b[0][:, 0:columns], ones[0:columns, :], gdiag[0:columns, 0:columns], start=True, stop=True).then_inc(from_pe, 1)

            turn(4, 0)
            te.wait_ge(to_pe, 3)
            lay = layers["ffn1a"]

            def inputs(i, before):
                for l in range(WIDE):
                    te.wait_ge(dve_sem[l], lay["dve"][l].at(i, "xc"))
                    if before is not None:
                        te.wait_ge(act_sem[l], lay["act"][l].at(before, "g3"))
                    for k in range(GROUP):
                        mm = nc.tensor.transpose(wide_a[l][:, k * 128:k * 128 + 128], prob[l][:, 2 * k:2 * k + 2, :], ident[:])
                    mm.then_inc(pe_sem[l], 1)

            def body(i, more):
                for l in range(WIDE):
                    te.wait_ge(dve_sem[l], lay["dve"][l].at(i, "xT"))
                    for c, bank in enumerate((ps_s[l][:, 0:512], ps_s[l][:, 512:1024], wide_b[l][:], wide_a[l][:])):
                        nc.tensor.matmul(bank, w_q[:, 0, c * 128:c * 128 + 128], xqT[l], start=True, stop=True).then_inc(pe_sem[l], 1)
                if more:
                    inputs(i + 1, i)
            inputs(0, None)
            with nc.tensor.Fori(0, QROUNDS - 1) as i:
                body(i, True)
            body(QROUNDS - 1, False)
            turn(2, 3)
            lay = layers["ffn1b"]
            with nc.tensor.Fori(0, QROUNDS) as i:
                for l in range(WIDE):
                    te.wait_ge(dve_sem[l], lay["dve"][l].at(i, "hb"))
                    for k in range(GROUP):
                        for c in range(4):
                            mm = nc.tensor.matmul(wide_a[l][:, k * 128:k * 128 + 128], hq[l][:, c * 512 + k * 128:c * 512 + k * 128 + 128],
                                                  w_q[:, 1, c * 128:c * 128 + 128], start=(c == 0), stop=(c == 3))
                    mm.then_inc(pe_sem[l], 1)
            te.wait_ge(loaded["late"], 16 * len(LATE))
            lay = layers["freq"]

            def units(bank, l):
                for r_ in range(4):
                    mm = nc.tensor.matmul(bank[:, 0:128], f_unit[:, r_, :], fl[l]["p1"][:, r_ * 128:r_ * 128 + 128], start=(r_ == 0), stop=(r_ == 3))
                mm.then_inc(pe_sem[l], 1)

            def inputs(i):
                for l in range(LANES):
                    te.wait_ge(dve_sem[l], lay["dve"][l].at(i, "xs"))
                    nc.tensor.matmul(ps_a[l][:, 256:384], xn[l][:], dft, start=True, stop=True)
                    te.wait_ge(ctx_in[l], i * 16 + (lay["ctx"] + 16))
                    nc.tensor.matmul(ps_a[l][:, 384:512], cx[l][:], dft, start=True, stop=True).then_inc(pe_sem[l], 1)

            def body(i, more):
                dve = [lambda n, l=l: te.wait_ge(dve_sem[l], lay["dve"][l].at(i, n)) for l in range(LANES)]
                act = [lambda n, l=l: te.wait_ge(act_sem[l], lay["act"][l].at(i, n)) for l in range(LANES)]
                for l in range(LANES):
                    nc.tensor.matmul(ps_a[l][:, 0:128], f_wq, xc[l][:, 0, :], start=True, stop=True).then_inc(pe_sem[l], 1)
                    for r_ in range(4):
                        mm = nc.tensor.matmul(ps_b[l][:, r_ * 128:r_ * 128 + 128], f_wk[:, r_, :], xc[l][:, 1, :], start=True, stop=True)
                    mm.then_inc(pe_sem[l], 1)
                for l in range(LANES):
                    dve[l]("q")
                    for r_ in range(4):
                        mm = nc.tensor.matmul(ps_a[l][:, r_ * 128:r_ * 128 + 128], f_wv[:, r_, :], xc[l][:, 1, :], start=True, stop=True)
                    mm.then_inc(pe_sem[l], 1)
                for l in range(LANES):
                    te.wait_ge(pool_sem[l], lay["pool"][l].at(i, "pz"))
                    units(ps_b[l], l)
                for l in range(LANES):
                    te.wait_ge(pool_sem[l], lay["pool"][l].at(i, "rz"))
                    units(ps_b[l], l)
                if more:
                    inputs(i + 1)
                for l in range(LANES):
                    act[l]("g")
                    if more:
                        te.wait_ge(act_sem[l], lay["act"][l].at(i + 1, "cf"))
                    nc.tensor.transpose(ps_a[l][:, 0:128], fl[l]["g"], ident[:]).then_inc(pe_sem[l], 1)
                for l in range(LANES):
                    act[l]("gT")
                    nc.tensor.matmul(ps_b[l][:, 0:128], idft, fl[l]["gT"], start=True, stop=True).then_inc(pe_sem[l], 1)
                for l in range(LANES):
                    dve[l]("fin")
            inputs(0)
            for l in range(LANES):
                te.wait_ge(act_sem[l], lay["act"][l].at(0, "cf"))
            with nc.tensor.Fori(0, ROUNDS - 1) as i:
                body(i, True)
            body(ROUNDS - 1, False)
            te.wait_ge(to_pe, 6)
            nc.tensor.transpose(ps_a[0][:, 0:128], r_t, ident[:])
            nc.tensor.matmul(ps_a[0][:, 128:256], ones[:], r_diag, start=True, stop=True).then_inc(from_pe, 1)
            te.wait_ge(to_pe, 7)
            lay = layers["ffn2"]
            with nc.tensor.Fori(0, QROUNDS) as i:
                for l in range(WIDE):
                    te.wait_ge(dve_sem[l], lay["dve"][l].at(i, "yc"))
                    for k in range(GROUP):
                        mm = nc.tensor.transpose(wide_a[l][:, k * 128:k * 128 + 128], q8[l]["y"][:, k * 128:k * 128 + 128], ident[:])
                    mm.then_inc(pe_sem[l], 1)
                for l in range(WIDE):
                    te.wait_ge(dve_sem[l], lay["dve"][l].at(i, "yT"))
                    for k in range(GROUP):
                        mm = nc.tensor.matmul(wide_b[l][:, k * 128:k * 128 + 128], q8[l]["yT"][:, k * 128:k * 128 + 128], r_q, start=True, stop=True)
                    mm.then_inc(pe_sem[l], 1)
            attention(3)
            te.wait_ge(to_pe, 8)
            gw = g_w[:, 0:2 * FFN3].rearrange("p (k c n) -> p k c n", k=2, c=3)
            dw = g_w[:, 2 * FFN3:3 * FFN3].rearrange("p (c n) -> p c n", c=3)
            lay = layers["ffn3"]

            def inputs(i):
                for l in range(WIDE):
                    te.wait_ge(dve_sem[l], lay["dve"][l].at(i, "xn"))
                    for k in range(2):
                        mm = nc.tensor.transpose(wide_b[l][:, 256 + k * 128:384 + k * 128], ff[l]["xn"][:, k * 128:k * 128 + 128], ident[:])
                    mm.then_inc(pe_sem[l], 1)

            def body(i, more):
                for l in range(WIDE):
                    te.wait_ge(act_sem[l], lay["act"][l].at(i, "xnT"))
                    for c, bank in enumerate((ps_s[l][:, 0:512], ps_s[l][:, 512:1024], wide_a[l][:])):
                        for k in range(2):
                            mm = nc.tensor.matmul(bank[:, k * 256:k * 256 + 256], gw[:, k, c, :], ff[l]["xnT"], start=True, stop=True)
                        if c:
                            mm.then_inc(pe_sem[l], 1)
                if more:
                    inputs(i + 1)
                for l in range(WIDE):
                    te.wait_ge(dve_sem[l], lay["dve"][l].at(i, "h1"))
                    if more:
                        te.wait_ge(act_sem[l], lay["act"][l].at(i + 1, "xnT"))
                    for k in range(2):
                        for c in range(3):
                            mm = nc.tensor.matmul(wide_b[l][:, k * 128:k * 128 + 128], ff[l]["hT"][:, c * 256 + k * 128:c * 256 + k * 128 + 128],
                                                  dw[:, c, :], start=(c == 0), stop=(c == 2))
                    mm.then_inc(pe_sem[l], 1)
            inputs(0)
            with nc.tensor.Fori(0, FFN3_ROUNDS - 1) as i:
                body(i, True)
            body(FFN3_ROUNDS - 1, False)

        @block.vector
        def _(dve):
            count = [0]

            def step(ins):
                count[0] += 1
                ins.then_inc(dve_chain, 1)
                dve.wait_ge(dve_chain, count[0])
            TT, TS, STT = nc.vector.tensor_tensor, nc.vector.tensor_scalar, nc.vector.scalar_tensor_tensor

            roots = [0]

            def inverse_root(out_, last):
                roots[0] += 1
                last.then_inc(root_wanted, 1)
                dve.wait_ge(root_given, roots[0])
                step(nc.vector.reciprocal(root[:], root[:]))
                step(TT(agg[:, 0], root[:], root[:], ALU.mult))
                step(TT(agg[:, 1], agg[:, 0], vpe[:], ALU.mult))
                step(TS(agg[:, 2], agg[:, 1], -0.5, 1.5, ALU.mult, ALU.add))
                step(TT(out_, root[:], agg[:, 2], ALU.mult))

            def moments():
                me, mo, ve, vo = (stats[:, :, k] for k in (1, 4, 2, 5))
                step(TT(agg[:, 0], me, mo, ALU.add))
                step(TS(mean[:], agg[:, 0], 0.5, None, ALU.mult))
                step(TT(agg[:, 1], me, mo, ALU.subtract))
                step(TT(agg[:, 2], agg[:, 1], agg[:, 1], ALU.mult))
                step(TT(agg[:, 0], ve, vo, ALU.add))
                step(TS(agg[:, 3], agg[:, 0], 1.0 / P, EPS, ALU.mult, ALU.add))
                inverse_root(rstd[:], STT(vpe[:], agg[:, 2], 0.25, agg[:, 3], ALU.mult, ALU.add))

            def finished(key):
                for l in range(layers[key]["lanes"]):
                    dve.wait_ge(dve_sem[l], layers[key]["dve"][l].end())

            for c in range(4):
                dve.wait_ge(loaded[f"x{c}"], 16)
                with nc.vector.Fori(c * ROUNDS // 4, (c + 1) * ROUNDS // 4) as i:
                    for l in range(LANES):
                        t = i * LANES + l
                        nc.vector.bn_stats(stats[:, t, :], x[:, t, :]).then_inc(x_stats, 1)
            dve.wait_ge(x_stats, TILES)
            moments()

            def attention(L):
                lay, w = layers[f"att{L}"], att[L]
                dve.wait_ge(loaded["const"], 16 * 6)
                dve.wait_ge(filled, LATE_FILLS if L == 3 else FILLS)
                dve.wait_ge(loaded[f"att{L}"], 16 * 8)
                if L == 0:
                    TS(minus_masked, ident[:], MASKED, None, ALU.mult)
                bv = w["bv"].rearrange("p (c j d) -> p c j d", j=2, d=HD)

                def normed(i):
                    for l in range(LANES):
                        t = i * LANES + l
                        nc.vector.tensor_scalar(xn[l][:], x[:, t, :], mean[:, bass.ds(t, 1)], rstd[:, bass.ds(t, 1)], ALU.subtract, ALU.mult).then_inc(dve_sem[l], 1)

                def values(i):
                    for l in range(LANES):
                        if L == 0:
                            t = i * LANES + l
                            nc.vector.scalar_tensor_tensor(am[l], key_mask[:, t, :], 1.0, causal[:], ALU.subtract, ALU.min).then_inc(dve_sem[l], 1)
                    for l in range(LANES):
                        dve.wait_ge(pe_sem[l], lay["pe"][l].at(i, "v"))
                        for j in range(2):
                            r = slice(64 * j, 64 * j + 64)
                            v = nc.vector.tensor_tensor(vbd[l][r, :, 0:32].rearrange("p c (b j d) -> p b c j d", b=2, j=2)[:, :, :, j, :],
                                                        ps_a[l][r, 128:384].rearrange("p (b c j d) -> p b c j d", b=2, j=2, d=HD)[:, :, :, j, :],
                                                        bv[r, :, j, :].unsqueeze(1).to_broadcast([64, 2, 8, HD]), ALU.add)
                        v.then_inc(dve_sem[l], 1)

                def body(i, more):
                    pe = [lambda n, l=l: dve.wait_ge(pe_sem[l], lay["pe"][l].at(i, n)) for l in range(LANES)]
                    own = [lambda n, l=l: dve.wait_ge(dve_sem[l], lay["dve"][l].at(i, n)) for l in range(LANES)]
                    for l in range(LANES):
                        pe[l]("s")
                        s = ps_s[l][:].rearrange("p (g k) -> p g k", k=SEQ)
                        nc.vector.tensor_reduce(mx[l][:], s, AX.X, ALU.max).then_inc(dve_sem[l], 1)
                        own[l]("mx")
                        nc.vector.tensor_tensor(prob[l][:], s, mx[l][:].unsqueeze(2).to_broadcast([P, 16, SEQ]), ALU.subtract).then_inc(dve_sem[l], 1)
                        if L == 0:
                            nc.vector.tensor_scalar(fx[l][:], mx[l][:], -MASKED / 2, half_pad[:], ALU.is_lt, ALU.mult).then_inc(dve_sem[l], 1)
                    if more:
                        normed(i + 1)
                    for l in range(LANES):
                        pe[l]("pv")
                        pv = ps_a[l][:, 0:272].rearrange("p (c e) -> p c e", c=8)
                        sums = pv[:, :, 32:34]
                        if L == 0:
                            own[l]("fx")
                            nc.vector.tensor_tensor(rc[l][:], sums, fx[l][:].rearrange("p (c b) -> p c b", b=2), ALU.add).then_inc(dve_sem[l], 1)
                            own[l]("fs")
                            nc.vector.reciprocal(rc[l][:], rc[l][:]).then_inc(dve_sem[l], 1)
                        else:
                            nc.vector.reciprocal(rc[l][:], sums).then_inc(dve_sem[l], 1)
                        own[l]("rc")
                        for b in range(2):
                            r = slice(64 * b, 64 * b + 64)
                            oo = nc.vector.tensor_tensor(o[l][r], pv[r, :, 16 * b:16 * b + 16].rearrange("p c (j d) -> p c j d", j=2),
                                                         rc[l][r].unsqueeze(3).to_broadcast([64, 8, 2, 8]), ALU.mult)
                        oo.then_inc(dve_sem[l], 1)
                    for l in range(LANES):
                        t = i * LANES + l
                        pe[l]("y")
                        dve.wait_ge(pool_sem[l], lay["pool"][l].at(i, "bo"))
                        nc.vector.tensor_tensor(x[:, t, :], x[:, t, :], ps_a[l][:, 0:128], ALU.add).then_inc(dve_sem[l], 1)
                    for l in range(LANES):
                        t = i * LANES + l
                        own[l]("fin")
                        nc.vector.nop(nofuse=True)
                        nc.vector.bn_stats(stats[:, t, :], x[:, t, :]).then_inc(dve_sem[l], 1)
                    if more:
                        values(i + 1)
                normed(0)
                values(0)
                with nc.vector.Fori(0, ROUNDS - 1) as i:
                    body(i, True)
                body(ROUNDS - 1, False)
            attention(0)

            finished("att0")
            moments()
            dve.wait_ge(loaded["ffn0"], 16 * 10)
            step(TT(rstd2, rstd[:], rstd[:], ALU.mult))
            inverse_root(rstd2, TS(vpe[:], rstd2, -EPS, 1.0 + EPS, ALU.mult, ALU.add))
            step(TT(rstd2, rstd2, rstd[:], ALU.mult))
            step(TS(rstd_one, rstd[:], 1.0, None, ALU.add))
            step(TT(mean_rstd, mean[:], rstd[:], ALU.mult))
            lay = layers["ffn0r"]
            with nc.vector.Fori(0, ROUNDS) as i:
                for into in ([m["t"] for m in moe], [xw[:, i * LANES + l, :] for l in range(LANES)]):
                    for l in range(LANES):
                        t = i * LANES + l
                        TS(into[l], x[:, t, :], mean[:, bass.ds(t, 1)], rstd2[:, bass.ds(t, 1)], ALU.subtract, ALU.mult).then_inc(dve_sem[l], 1)
                for l in range(LANES):
                    dve.wait_ge(pe_sem[l], lay["pe"][l].at(i, "nT"))
            finished("ffn0r")
            for l in range(LANES):
                dve.wait_ge(act_sem[l], layers["ffn0r"]["act"][l].end())

            every = [P, TILES, EXPERTS]
            step(nc.vector.tensor_reduce(best, logits, AX.X, ALU.max))
            TT(scan[0], logits, best.unsqueeze(2).to_broadcast(every), ALU.is_equal).then_inc(best_ready, 1)
            dve.wait_ge(best_ready, 1)
            step(TT(scan[1], scan[0], rank.unsqueeze(1).to_broadcast(every), ALU.mult))
            step(nc.vector.tensor_reduce(pick, scan[1], AX.X, ALU.max))
            TT(one, scan[1], pick.unsqueeze(2).to_broadcast(every), ALU.is_equal).then_inc(one_ready, 1)
            dve.wait_ge(tanh_ready, 1)
            TS(score, score, 0.5, 0.5, ALU.mult, ALU.add).then_inc(score_ready, 1)
            dve.wait_ge(counted, 1)
            flat = lambda v: v.rearrange("p t e -> p (t e)")
            step(nc.vector.tensor_copy(flat(scan[0]), ps_b[0][:]))
            step(TT(flat(before), ps_a[0][:], flat(scan[0]), ALU.subtract))
            src, dst, reach_ = scan[0], scan[1], 1
            while reach_ < TILES:
                TT(dst[:, reach_:], src[:, reach_:], src[:, 0:TILES - reach_], ALU.add)
                step(nc.vector.tensor_copy(dst[:, 0:reach_], src[:, 0:reach_]))
                src, dst, reach_ = dst, src, 2 * reach_
            step(TT(before, before, src, ALU.add))
            step(TS(used, src[:, TILES - 1, :], P / 2 - 0.5, 1.0 / P, ALU.add, ALU.mult))
            step(TS(used, used, MAGIC, None, ALU.add))
            step(TS(used, used, MAGIC, None, ALU.subtract))
            step(nc.vector.memset(first[:, 0:1], 0.0))
            for e in range(EXPERTS):
                step(TT(first[:, e + 1:e + 2], first[:, e:e + 1], used[:, e:e + 1], ALU.add))
            step(STT(before, first[:, 0:EXPERTS].unsqueeze(1).to_broadcast(every), float(P), before, ALU.mult, ALU.add))
            step(TT(before, before, one, ALU.mult))
            step(nc.vector.tensor_reduce(slot, before, AX.X, ALU.add))
            step(TS(slot_i, slot, 0.0, None, ALU.add))
            step(nc.vector.memset(owner, 0.0))
            for e in range(1, EXPERTS):
                step(STT(owner, slot_tile, first[:, e:e + 1], owner, ALU.is_ge, ALU.add))
            TS(owner_i, owner, 0.0, None, ALU.add).then_inc(slots_ready, 1)

            lay = layers["ffn0a"]
            with nc.vector.Fori(0, ROUNDS) as i:
                own = [lambda n, l=l: dve.wait_ge(dve_sem[l], lay["dve"][l].at(i, n)) for l in range(LANES)]
                for l in range(LANES):
                    dve.wait_ge(act_sem[l], lay["act"][l].at(i, "ssilu"))
                    TT(moe[l]["h"], moe[l]["silu"], ps_b[l][:, FFN0:2 * FFN0], ALU.mult).then_inc(dve_sem[l], 1)
                for l in range(LANES):
                    t = i * LANES + l
                    TS(x[:, t, :], x[:, t, :], rstd_one[:, bass.ds(t, 1)], mean_rstd[:, bass.ds(t, 1)], ALU.mult, ALU.subtract).then_inc(dve_sem[l], 1)
                for l in range(LANES):
                    t = i * LANES + l
                    dve.wait_ge(pe_sem[l], lay["pe"][l].at(i, "sdn"))
                    own[l]("acc")
                    TT(x[:, t, :], x[:, t, :], ps_b[l][:, 0:128], ALU.add).then_inc(dve_sem[l], 1)
            finished("ffn0a")
            lay = layers["ffn0b"]

            def scores(i, l):
                dve.wait_ge(slots_in[l], i * 16 + 16)
                nc.vector.tensor_copy(exp[l]["score"], exp[l]["row"][:, P:P + 1]).then_inc(dve_sem[l], 1)

            def body(i, more):
                for l in range(LANES):
                    dve.wait_ge(act_sem[l], lay["act"][l].at(i, "silu"))
                    STT(exp[l]["h"], ps_b[l][:, FFN0:2 * FFN0], exp[l]["score"], exp[l]["silu"], ALU.mult, ALU.mult).then_inc(dve_sem[l], 1)
                if more:
                    for l in range(LANES):
                        dve.wait_ge(dve_sem[l], lay["dve"][l].at(i, "h"))
                        scores(i + 1, l)
            for l in range(LANES):
                scores(0, l)
            with nc.vector.Fori(0, SLOT_ROUNDS - 1) as i:
                body(i, True)
            body(SLOT_ROUNDS - 1, False)
            lay = layers["ffn0c"]
            with nc.vector.Fori(0, ROUNDS) as i:
                for l in range(LANES):
                    t = i * LANES + l
                    dve.wait_ge(gathered[l], i * 16 + 16)
                    TT(x[:, t, :], x[:, t, :], exp[l]["t"], ALU.add).then_inc(dve_sem[l], 1)
                for l in range(LANES):
                    t = i * LANES + l
                    dve.wait_ge(dve_sem[l], lay["dve"][l].at(i, "fin"))
                    nc.vector.nop(nofuse=True)
                    nc.vector.bn_stats(stats[:, t, :], x[:, t, :]).then_inc(dve_sem[l], 1)
            finished("ffn0c")
            moments()
            attention(1)

            def everywhere(columns, n):
                dve.wait_ge(from_pe, n + 1)
                step(nc.vector.tensor_reduce(grow[0:columns], ps_a[0][0:columns, 0:128], AX.X, ALU.max))
                TS(gdiag[0:columns, 0:columns], ident[0:columns, 0:columns], grow[0:columns], None, ALU.mult).then_inc(to_pe, 1)
                dve.wait_ge(from_pe, n + 2)
                step(nc.vector.tensor_copy(gall[:, 0:columns], ps_b[0][:, 0:columns]))

            def affine():
                step(TT(qs[:, 0:1], gall[:, 0:1], gall[:, 1:2], ALU.add))
                step(TS(qs[:, 0:1], qs[:, 0:1], 1.0 / 255.0, 1e-8, ALU.mult, ALU.max))
                step(nc.vector.reciprocal(qs[:, 1:2], qs[:, 0:1]))
                step(TS(qs[:, 2:3], gall[:, 1:2], qs[:, 1:2], MAGIC, ALU.mult, ALU.add))
                step(TS(qs[:, 2:3], qs[:, 2:3], MAGIC, 128.0, ALU.subtract, ALU.subtract))
                step(TS(qs[:, 2:3], qs[:, 2:3], -128.0, 127.0, ALU.max, ALU.min))
                step(TS(qs[:, 3:4], qs[:, 2:3], -1.0, MAGIC - 128.0, ALU.mult, ALU.add))
                step(TS(qs[:, 4:5], qs[:, 2:3], -1.0, MAGIC + 127.0, ALU.mult, ALU.add))

            finished("att1")
            moments()
            dve.wait_ge(loaded["ffn1"], 16 * 3)
            step(nc.vector.tensor_reduce(tmx[:, 0], x[:], AX.X, ALU.max))
            step(nc.vector.tensor_reduce(tmx[:, 1], x[:], AX.X, ALU.min))
            for k in range(2):
                step(TT(tmx[:, k], tmx[:, k], mean[:], ALU.subtract))
                step(TT(tmx[:, k], tmx[:, k], rstd[:], ALU.mult))
            step(nc.vector.tensor_reduce(gcol[:, 0:1], tmx[:, 0], AX.X, ALU.max))
            step(nc.vector.tensor_reduce(gcol[:, 1:2], tmx[:, 1], AX.X, ALU.min))
            step(TS(gcol[:, 1:2], gcol[:, 1:2], -1.0, None, ALU.mult))
            step(nc.vector.tensor_reduce(gcol[:, 2:3], w_raw[:, 0], AX.X, ALU.max, apply_absolute_value=True))
            nc.vector.tensor_reduce(gcol[:, 3:4], w_raw[:, 1], AX.X, ALU.max, apply_absolute_value=True).then_inc(to_pe, 1)
            everywhere(4, 0)
            affine()
            step(TS(qs[:, 5:7], gall[:, 2:4], 1.0 / 127.0, 1e-8, ALU.mult, ALU.max))
            step(nc.vector.reciprocal(gall[:, 2:4], qs[:, 5:7]))
            step(TT(qs[:, 8:9], qs[:, 0:1], qs[:, 5:6], ALU.mult))
            for k in range(2):
                step(TS(w_rnd, w_raw[:, k], gall[:, 2 + k:3 + k], MAGIC, ALU.mult, ALU.add))
                step(TS(w_rnd, w_rnd, MAGIC - 127.0, MAGIC + 127.0, ALU.max, ALU.min))
                wq = TS(w_q[:, k], w_rnd, MAGIC, None, ALU.subtract)
                if k == 0:
                    step(wq)
            wq.then_inc(to_pe, 1)
            lay = layers["ffn1a"]
            view = [prob[l][:].rearrange("p (k j) d -> p k (j d)", j=2)[:, 0:GROUP] for l in range(WIDE)]

            def rounded(i):
                own = [lambda n, l=l: dve.wait_ge(dve_sem[l], lay["dve"][l].at(i, n)) for l in range(WIDE)]
                for l in range(WIDE):
                    ts = bass.ds((i * WIDE + l) * GROUP, GROUP)
                    TT(view[l], x[:, ts, :], mean[:, ts].unsqueeze(2).to_broadcast([P, GROUP, P]), ALU.subtract).then_inc(dve_sem[l], 1)
                for l in range(WIDE):
                    ts = bass.ds((i * WIDE + l) * GROUP, GROUP)
                    own[l]("xs")
                    TT(view[l], view[l], rstd[:, ts].unsqueeze(2).to_broadcast([P, GROUP, P]), ALU.mult).then_inc(dve_sem[l], 1)
                for l in range(WIDE):
                    own[l]("xn")
                    TS(view[l], view[l], qs[:, 1:2], MAGIC, ALU.mult, ALU.add).then_inc(dve_sem[l], 1)
                for l in range(WIDE):
                    own[l]("xr")
                    TS(view[l], view[l], qs[:, 3:4], qs[:, 4:5], ALU.max, ALU.min).then_inc(dve_sem[l], 1)

            def turned(i):
                for l in range(WIDE):
                    dve.wait_ge(pe_sem[l], lay["pe"][l].at(i, "xT"))
                    TS(xqT[l], wide_a[l][:], MAGIC, None, ALU.subtract).then_inc(dve_sem[l], 1)

            def body(i, more):
                if more:
                    rounded(i + 1)
                for l in range(WIDE):
                    g = i * WIDE + l
                    dve.wait_ge(act_sem[l], lay["act"][l].at(i, "g3"))
                    nc.vector.tensor_reduce(hmm[:, 0, bass.ds(g, 1)], hidden[:, g, :], AX.X, ALU.max).then_inc(dve_sem[l], 1)
                    nc.vector.tensor_reduce(hmm[:, 1, bass.ds(g, 1)], hidden[:, g, :], AX.X, ALU.min).then_inc(dve_sem[l], 1)
                if more:
                    turned(i + 1)
            rounded(0)
            turned(0)
            with nc.vector.Fori(0, QROUNDS - 1) as i:
                body(i, True)
            body(QROUNDS - 1, False)
            finished("ffn1a")
            step(nc.vector.tensor_reduce(gcol[:, 0:1], hmm[:, 0], AX.X, ALU.max))
            step(nc.vector.tensor_reduce(gcol[:, 1:2], hmm[:, 1], AX.X, ALU.min))
            TS(gcol[:, 1:2], gcol[:, 1:2], -1.0, None, ALU.mult).then_inc(to_pe, 1)
            everywhere(2, 2)
            affine()
            TT(qs[:, 9:10], qs[:, 0:1], qs[:, 6:7], ALU.mult).then_inc(hidden_scaled, 1)
            dve.wait_ge(hidden_scaled, 1)
            lay = layers["ffn1b"]
            with nc.vector.Fori(0, QROUNDS) as i:
                own = [lambda n, l=l: dve.wait_ge(dve_sem[l], lay["dve"][l].at(i, n)) for l in range(WIDE)]
                for l in range(WIDE):
                    g = i * WIDE + l
                    dve.wait_ge(act_sem[l], lay["act"][l].at(i, "hr"))
                    TS(hidden[:, g, :], hidden[:, g, :], qs[:, 3:4], qs[:, 4:5], ALU.max, ALU.min).then_inc(dve_sem[l], 1)
                for l in range(WIDE):
                    g = i * WIDE + l
                    own[l]("hc")
                    TS(hq[l], hidden[:, g, :], MAGIC, None, ALU.subtract).then_inc(dve_sem[l], 1)
                for l in range(WIDE):
                    y = probT[l][:, 0:GROUP]
                    ts = bass.ds((i * WIDE + l) * GROUP, GROUP)
                    dve.wait_ge(pe_sem[l], lay["pe"][l].at(i, "y"))
                    STT(y, wide_a[l][:].rearrange("p (k d) -> p k d", k=GROUP), qs[:, 9:10], b2[:].unsqueeze(1).to_broadcast([P, GROUP, P]), ALU.mult, ALU.add).then_inc(dve_sem[l], 1)
                    own[l]("yb")
                    TT(x[:, ts, :], x[:, ts, :], y, ALU.add).then_inc(dve_sem[l], 1)
                for l in range(WIDE):
                    own[l]("fin")
                    nc.vector.nop(nofuse=True)
                    for k in range(GROUP):
                        t = (i * WIDE + l) * GROUP + k
                        st = nc.vector.bn_stats(stats[:, t, :], x[:, t, :])
                    st.then_inc(dve_sem[l], 1)

            finished("ffn1b")
            moments()
            dve.wait_ge(loaded["late"], 16 * len(LATE))
            step(nc.vector.memset(dc_q, 0.0))
            for b in range(2):
                step(TS(dc_q[:, b * SEQ:b * SEQ + 1], f_bq, float(SEQ), None, ALU.mult))
                step(TS(dc_kv[:, 0, :, b], f_bk, float(SEQ), None, ALU.mult))
                step(TS(dc_kv[:, 1, :, b], f_bv, float(SEQ), None, ALU.mult))
            step(TT(norm, rstd[:], rstd[:], ALU.mult))
            inverse_root(norm, TS(vpe[:], norm, -EPS * P, 1.0 * P, ALU.mult, ALU.add))
            TT(norm, norm, vpe[:], ALU.mult).then_inc(norm_ready, 1)
            dve.wait_ge(eneg_ready, 1)
            s_, u_, v_ = chaos[:, 0], chaos[:, 1], chaos[:, 2]
            step(TS(u_, eneg, 1.0, None, ALU.add))
            step(nc.vector.reciprocal(s_, u_))
            for _ in range(LOGISTIC_STEPS):
                step(TS(u_, s_, -1.0, 1.0, ALU.mult, ALU.add))
                step(STT(v_, s_, LOGISTIC, u_, ALU.mult, ALU.mult))
                s_, v_ = v_, s_
            step(TS(u_, s_, 0.5, 0.1, ALU.subtract, ALU.mult))
            step(TS(u_, u_, 1.0, wave, ALU.add, ALU.mult))
            step(TT(fac, u_, rstd[:], ALU.mult))
            lay = layers["freq"]
            im, mid = slice(FREQ, SEQ), slice(1, FREQ - 1)

            def products(own, l, one, four, first):
                a_ = one.rearrange("p (b m) -> p b m", b=2)
                b_ = four.rearrange("p (r b m) -> p r b m", r=4, b=2)
                half_spectrum = [P, 4, 2, FREQ - 2]
                p1 = fl[l]["p1"].rearrange("p (r b m) -> p r b m", r=4, b=2)
                p2 = fl[l]["p2"].rearrange("p (r b m) -> p r b m", r=4, b=2)
                p3 = fl[l]["p3"].rearrange("p (r b m) -> p r b m", r=4, b=2)
                TT(fl[l]["p1"].rearrange("p (r m) -> p r m", r=4), one.unsqueeze(1).to_broadcast([P, 4, P]), four.rearrange("p (r m) -> p r m", r=4), ALU.mult).then_inc(dve_sem[l], 1)
                TT(p2, a_[:, :, mid].unsqueeze(1).to_broadcast(half_spectrum), b_[:, :, :, im], ALU.mult)
                TT(p3, a_[:, :, im].unsqueeze(1).to_broadcast(half_spectrum), b_[:, :, :, mid], ALU.mult).then_inc(dve_sem[l], 1)
                own[l](first)
                TT(p1[:, :, :, mid], p1[:, :, :, mid], p1[:, :, :, im], ALU.subtract).then_inc(dve_sem[l], 1)

            def inputs(i):
                for l in range(LANES):
                    t = i * LANES + l
                    TS(xn[l][:], x[:, t, :], mean[:, bass.ds(t, 1)], fac[:, bass.ds(t, 1)], ALU.subtract, ALU.mult).then_inc(dve_sem[l], 1)

            def body(i, more):
                pe = [lambda n, l=l: dve.wait_ge(pe_sem[l], lay["pe"][l].at(i, n)) for l in range(LANES)]
                own = [lambda n, l=l: dve.wait_ge(dve_sem[l], lay["dve"][l].at(i, n)) for l in range(LANES)]
                for l in range(LANES):
                    pe[l]("pq")
                    TT(fl[l]["qh"], ps_a[l][:, 0:128], dc_q, ALU.add).then_inc(dve_sem[l], 1)
                for l in range(LANES):
                    pe[l]("pk")
                    dc = ps_b[l].rearrange("p (r b m) -> p r b m", r=4, b=2)[:, :, :, 0]
                    TT(dc, dc, dc_kv[:, 0], ALU.add).then_inc(dve_sem[l], 1)
                    own[l]("kb")
                    products(own, l, fl[l]["qh"], ps_b[l], "p")
                for l in range(LANES):
                    pe[l]("pv")
                    dc = ps_a[l].rearrange("p (r b m) -> p r b m", r=4, b=2)[:, :, :, 0]
                    TT(dc, dc, dc_kv[:, 1], ALU.add).then_inc(dve_sem[l], 1)
                for l in range(LANES):
                    own[l]("vb")
                    dve.wait_ge(act_sem[l], lay["act"][l].at(i, "qk"))
                    dve.wait_ge(pool_sem[l], lay["pool"][l].at(i, "pz"))
                    products(own, l, fl[l]["qk"], ps_a[l], "r")
                if more:
                    inputs(i + 1)
                for l in range(LANES):
                    t = i * LANES + l
                    pe[l]("y")
                    TT(x[:, t, :], x[:, t, :], ps_b[l][:, 0:128], ALU.add).then_inc(dve_sem[l], 1)
                for l in range(LANES):
                    t = i * LANES + l
                    own[l]("fin")
                    nc.vector.nop(nofuse=True)
                    nc.vector.bn_stats(stats[:, t, :], x[:, t, :]).then_inc(dve_sem[l], 1)
            inputs(0)
            with nc.vector.Fori(0, ROUNDS - 1) as i:
                body(i, True)
            body(ROUNDS - 1, False)

            finished("freq")
            moments()
            step(nc.vector.tensor_reduce(r_scale[:, 0:1], r_raw, AX.X, ALU.max, apply_absolute_value=True))
            step(TS(r_scale[:, 0:1], r_scale[:, 0:1], 1e-12, 1.0 / 127.0, ALU.max, ALU.mult))
            step(nc.vector.reciprocal(r_scale[:, 1:2], r_scale[:, 0:1]))
            step(TS(r_t, r_raw, r_scale[:, 1:2], MAGIC, ALU.mult, ALU.add))
            step(TS(r_t, r_t, MAGIC - 127.0, MAGIC + 127.0, ALU.max, ALU.min))
            TS(r_diag, ident[:], r_scale[:, 0:1], None, ALU.mult).then_inc(to_pe, 1)
            dve.wait_ge(from_pe, 5)
            step(TS(r_q, ps_a[0][:, 0:128], MAGIC, None, ALU.subtract))
            nc.vector.tensor_copy(r_bc, ps_a[0][:, 128:256]).then_inc(to_pe, 1)
            dve.wait_ge(to_pe, 7)
            lay = layers["ffn2"]
            with nc.vector.Fori(0, QROUNDS) as i:
                own = [lambda n, l=l: dve.wait_ge(dve_sem[l], lay["dve"][l].at(i, n)) for l in range(WIDE)]
                view = [q8[l]["y"].rearrange("p (k d) -> p k d", k=GROUP) for l in range(WIDE)]
                wide = [P, GROUP, P]
                for l in range(WIDE):
                    ts = bass.ds((i * WIDE + l) * GROUP, GROUP)
                    TT(view[l], x[:, ts, :], mean[:, ts].unsqueeze(2).to_broadcast(wide), ALU.subtract).then_inc(dve_sem[l], 1)
                for l in range(WIDE):
                    ts = bass.ds((i * WIDE + l) * GROUP, GROUP)
                    own[l]("xs")
                    TT(view[l], view[l], rstd[:, ts].unsqueeze(2).to_broadcast(wide), ALU.mult).then_inc(dve_sem[l], 1)
                for l in range(WIDE):
                    own[l]("xn")
                    nc.vector.tensor_reduce(q8[l]["amax"], view[l], AX.X, ALU.max, apply_absolute_value=True).then_inc(dve_sem[l], 1)
                for l in range(WIDE):
                    own[l]("amax")
                    TS(q8[l]["ls"], q8[l]["amax"], 1e-12, 1.0 / 127.0, ALU.max, ALU.mult).then_inc(dve_sem[l], 1)
                    own[l]("ls")
                    nc.vector.reciprocal(q8[l]["inv"], q8[l]["ls"]).then_inc(dve_sem[l], 1)
                for l in range(WIDE):
                    own[l]("inv")
                    TT(view[l], view[l], q8[l]["inv"].unsqueeze(2).to_broadcast(wide), ALU.mult).then_inc(dve_sem[l], 1)
                for l in range(WIDE):
                    own[l]("y")
                    TS(view[l], view[l], MAGIC, None, ALU.add).then_inc(dve_sem[l], 1)
                for l in range(WIDE):
                    own[l]("yr")
                    TS(view[l], view[l], MAGIC - 127.0, MAGIC + 127.0, ALU.max, ALU.min).then_inc(dve_sem[l], 1)
                for l in range(WIDE):
                    dve.wait_ge(pe_sem[l], lay["pe"][l].at(i, "yT"))
                    TS(q8[l]["yT"], wide_a[l][:], MAGIC, None, ALU.subtract).then_inc(dve_sem[l], 1)
                for l in range(WIDE):
                    ts = bass.ds((i * WIDE + l) * GROUP, GROUP)
                    dve.wait_ge(pe_sem[l], lay["pe"][l].at(i, "mm"))
                    TT(view[l], wide_b[l][:].rearrange("p (k d) -> p k d", k=GROUP), r_bc.unsqueeze(1).to_broadcast(wide), ALU.mult).then_inc(dve_sem[l], 1)
                    own[l]("a")
                    TT(view[l], view[l], q8[l]["ls"].unsqueeze(2).to_broadcast(wide), ALU.mult).then_inc(dve_sem[l], 1)
                    own[l]("b")
                    TT(x[:, ts, :], x[:, ts, :], view[l], ALU.add).then_inc(dve_sem[l], 1)
                for l in range(WIDE):
                    own[l]("fin")
                    nc.vector.nop(nofuse=True)
                    for k in range(GROUP):
                        t = (i * WIDE + l) * GROUP + k
                        st = nc.vector.bn_stats(stats[:, t, :], x[:, t, :])
                    st.then_inc(dve_sem[l], 1)
            finished("ffn2")
            moments()
            attention(3)

            finished("att3")
            moments()
            TS(g_w, g_raw, 1.0 / 127.0, None, ALU.mult).then_inc(to_pe, 1)
            lay = layers["ffn3"]

            def normed(i, l):
                for k in range(2):
                    t = (i * WIDE + l) * 2 + k
                    n = TS(ff[l]["xn"][:, k * 128:k * 128 + 128], x[:, t, :], mean[:, bass.ds(t, 1)], rstd[:, bass.ds(t, 1)], ALU.subtract, ALU.mult)
                n.then_inc(dve_sem[l], 1)

            def body(i, more):
                for l in range(WIDE):
                    dve.wait_ge(act_sem[l], lay["act"][l].at(i, "s0"))
                    TT(ff[l]["hT"][:, 0:512].rearrange("p (c t) -> p c t", c=2), ff[l]["silu"][:, 0:512].rearrange("p (c t) -> p c t", c=2),
                       ps_s[l][:].rearrange("p (c k t) -> p c k t", c=2, k=2)[:, :, 1, :], ALU.mult).then_inc(dve_sem[l], 1)
                    if more:
                        normed(i + 1, l)
                    dve.wait_ge(act_sem[l], lay["act"][l].at(i, "s1"))
                    TT(ff[l]["hT"][:, 512:768], ff[l]["silu"][:, 512:768], wide_a[l][:, 256:512], ALU.mult).then_inc(dve_sem[l], 1)
                for l in range(WIDE):
                    ts = bass.ds((i * WIDE + l) * 2, 2)
                    dve.wait_ge(pe_sem[l], lay["pe"][l].at(i, "y"))
                    TT(x[:, ts, :], x[:, ts, :], wide_b[l][:, 0:256].rearrange("p (k d) -> p k d", k=2), ALU.add).then_inc(dve_sem[l], 1)
            for l in range(WIDE):
                normed(0, l)
            with nc.vector.Fori(0, FFN3_ROUNDS - 1) as i:
                body(i, True)
            body(FFN3_ROUNDS - 1, False)


def memory_scale():
    sigmoid = lambda v: np.float32(1) / (np.float32(1) + np.exp(-np.float32(v)))
    part_ = lambda v: np.float32(0.9 * 0.5) + np.float32(0.1) * sigmoid(v)
    return float(np.float32(0.4) * part_(0.7) + np.float32(0.3) * part_(0.8) + np.float32(0.3) * part_(0.6))


MEMORY_SCALE = memory_scale()


def spectral_constants():
    f8 = np.float64
    n, k = np.arange(SEQ), np.arange(FREQ)
    angle = 2 * np.pi * np.outer(n, k) / SEQ
    forward = np.concatenate([np.cos(angle), -np.sin(angle[:, 1:FREQ - 1])], axis=1)
    filt = np.exp(1j * 1.5 * np.arctan(np.log(np.arange(SEQ, dtype=f8) + 1e-10))) ** 3
    turned = np.exp(2j * np.pi * np.outer(k, n) / SEQ)
    both = filt[:FREQ].copy()
    both[1:FREQ - 1] += np.conj(filt[SEQ - k[1:FREQ - 1]])
    g = both[:, None] * turned / SEQ
    inverse = np.concatenate([g.real, -g.imag[1:FREQ - 1]], axis=0)
    twice = lambda m: np.kron(np.eye(2), m).astype(np.float32)
    sign = [[1, 1, 1, 1], [1, -1, 1, -1], [1, -1, -1, 1], [1, 1, -1, -1]]
    units = np.zeros((4, P, P), np.float32)
    for r in range(4):
        for i in range(4):
            j = (i + r) % 4
            for c in range(32):
                units[r, i * 32 + c, (i ^ j) * 32 + c] = sign[i][j]
    lam = np.arange(SEQ, dtype=np.float32) / SEQ
    alpha = np.clip(1.0 * (1.0 + 0.5 * (1.5 - 2.0) / 2.0), 0.1, 3.0)
    wave = np.sin(alpha * lam) * np.cos(-2.0 * lam + (2 * 1 + 1 - 2 * 1.5) * lam ** 2)
    return dict(c_dft=twice(forward), c_idft=twice(inverse), c_unit=np.ascontiguousarray(units.transpose(1, 0, 2)),
                c_wave=np.tile(1.0 + 0.1 * wave, 2).astype(np.float32).reshape(P, 1))



def kernel(**inputs):
    import numpy as _np
    import concourse.bacc as _bacc
    from concourse import mybir as _mybir
    from concourse.bass_utils import run_bass_kernel_spmd as _run

    a = {k: _np.asarray(v) for k, v in inputs.items()}
    twice = lambda w: _np.stack([w.reshape(-1, 2, 64)] * 2, axis=2).reshape(-1, 2, 128)
    d = {"x": a["x"].reshape(-1, 128), "ctx_1024": a["ctx_1024"].reshape(-1, 128),
         "mask_BxS2_bf1": a["mask_BxS2_bf1"].view(_np.uint8).reshape(1, -1)}

    def attention(L, wq, wk, wv, wo, bq, bk, bv, bo):
        d.update({f"a{L}_wq": twice(wq), f"a{L}_wk": twice(wk), f"a{L}_wv": wv, f"a{L}_wo": wo,
                  f"a{L}_bq": twice(bq)[0].T, f"a{L}_bk": twice(bk)[0].T,
                  f"a{L}_bv": bv.reshape(1, 128), f"a{L}_bo": bo.reshape(1, 128)})
    attention(0, a["L0_xattn_W_q"].T, a["L0_xattn_W_k"].T, a["L0_xattn_W_v"].T, a["L0_xattn_W_o"].T,
              a["L0_xattn_b_q"], a["L0_xattn_b_k"], a["L0_xattn_b_v"], a["L0_xattn_b_o"])
    for L in (1, 3):
        g = lambda n: a[f"L{L}_xattn_{n}"]
        attention(L, g("Wq"), g("Wkv")[:, :128], g("Wkv")[:, 128:], g("Wo"), g("bq"), g("bkv")[:128], g("bkv")[128:], g("bo"))

    f = lambda n: a[f"L0_ffn_{n}"]
    d["gate_up"] = _np.concatenate([f("gate_w"), f("up_w")], axis=2).transpose(1, 0, 2)
    d["down0"] = f("down_w").reshape(8, 2, 128, 128).transpose(2, 1, 0, 3).reshape(128, 2, 1024)
    d["shared_gu"] = _np.concatenate([f("sh_gate"), f("sh_up")], axis=1)
    d["shared_dn"] = f("sh_down").reshape(2, 128, 128).transpose(1, 0, 2)
    d["router"], d["ln_w"], d["ln_b"] = f("router_w"), f("ln_w").reshape(-1, 1), f("ln_b").reshape(-1, 1)
    d["w12"] = _np.stack([a["L1_ffn_W1"].T, a["L1_ffn_W2"].T.reshape(4, 128, 128).transpose(1, 0, 2).reshape(128, 512)], axis=1)
    d["b1"], d["b2"] = a["L1_ffn_b1"].reshape(4, 128).T, a["L1_ffn_b2"].reshape(1, -1)
    around = lambda w: _np.stack([_np.roll(w, -32 * r_, axis=-1) for r_ in range(4)], axis=1)
    h = lambda n: a[f"L2_xattn_{n}"]
    d["f_wq"], d["f_wk"], d["f_wv"] = h("Wq").T, around(h("Wk").T), around(h("Wv").T)
    d["f_bq"], d["f_bk"], d["f_bv"] = h("bq").reshape(128, 1), around(h("bk")[None])[0].T, around(h("bv")[None])[0].T
    d["r_raw"] = a["L2_ffn_rhs"].T
    m = lambda n: a[f"L3_ffn_{n}"]
    d["g_raw"] = _np.concatenate([m("w_gate").T, m("w_up").T, m("w_down").T.reshape(3, 128, 128).transpose(1, 0, 2).reshape(128, 384)], axis=1)

    r = _np.arange(128)
    d["c_ident"] = _np.eye(128, dtype=_np.float32)
    d["c_head_mask"] = ((r[:, None] % 64 // 8 == _np.arange(8)) * _np.float32(8 ** -0.5)).astype(_np.float32)
    q_, k_ = r[:, None] % 64, _np.arange(64)[None]
    d["c_causal"] = -(q_ < k_).astype(_np.float32) - ((q_ < 32) & (k_ >= 32)).astype(_np.float32)
    d["c_rank"] = (EXPERTS - _np.arange(EXPERTS, dtype=_np.float32)).reshape(1, -1)
    d["c_slot_tile"] = _np.arange(SLOTS, dtype=_np.float32).reshape(1, -1)
    d["c_earlier"] = (r[:, None] < r[None]).astype(_np.float32)
    d.update(spectral_constants())
    d["c_half_pad"] = _np.where(r % 64 < 32, 32.0, 0.0).astype(_np.float32).reshape(128, 1)

    nc = _bacc.Bacc("TRN2", target_bir_lowering=False, num_devices=1)
    arrays, dram = {}, {}
    for n, v in d.items():
        v = _np.ascontiguousarray(v)
        arrays[f"in_{n}"] = v
        dram[n] = nc.dram_tensor(f"in_{n}", v.shape, _mybir.dt.from_np(v.dtype), kind="ExternalInput").ap()
    out = nc.dram_tensor("out", (8192, 128), F32, kind="ExternalOutput").ap()
    rows_in = nc.dram_tensor("rows_in", (SLOTS * P, P + 1), F32, kind="Internal").ap()
    rows_out = nc.dram_tensor("rows_out", (SLOTS * P, P), F32, kind="Internal").ap()
    build_program(nc, dram, out, rows_in, rows_out)
    res = _run(nc, [arrays], core_ids=[0])
    return res.results[0]["out"].reshape(128, 64, 128)
```
